# Optimizing a Trainium2 kernel written in Bass

```python
import numpy as np
import jax
import jax.numpy as jnp

def _softmax(x, axis=-1):
    return jax.nn.softmax(x, axis=axis)

def _gelu(x):
    return jax.nn.gelu(x, approximate=True)

def _silu(x):
    return jax.nn.silu(x)

def _sigmoid(x):
    return jax.nn.sigmoid(x)

def _layernorm(x, axis=-1, eps=1e-05):
    m = jnp.mean(x, axis=axis, keepdims=True)
    v = jnp.var(x, axis=axis, keepdims=True)
    return (x - m) / jnp.sqrt(v + eps)

def _scatter_add(tgt, idx, src, axis=0):
    return tgt.at[idx].add(src)

def _segment_sum(src, seg, n):
    return jax.ops.segment_sum(src, seg, n)
kernel_name = 'mk_prb_d1_jaxref_r4_efdf30'

def setup_inputs(seed: int=0):
    np.random.seed(seed)
    _w = jnp.asarray

    def _L0_attn_setup():
        import jax, jax.numpy as jnp
        import numpy as np
        H = 16
        DK = 128
        DV = 128
        HID = 512
        KS = 4

        def _causal_dwconv(x, w, b):
            xc = jnp.transpose(x, (0, 2, 1))
            out = jax.lax.conv_general_dilated(xc, w[:, None, :], window_strides=(1,), padding=[(KS - 1, 0)], feature_group_count=xc.shape[1], dimension_numbers=('NCH', 'OIH', 'NCH'))
            out = out + b[None, :, None]
            return jnp.transpose(out, (0, 2, 1))

        def _forward(x, Wq, Wk, Wv, Wa, ba, Wb, bb, Wg, Wo, qcw, qcb, kcw, kcb, vcw, vcb, ln_w, ln_b):
            B, T, _ = x.shape
            q = jax.nn.silu(_causal_dwconv(x @ Wq, qcw, qcb))
            k = jax.nn.silu(_causal_dwconv(x @ Wk, kcw, kcb))
            v = jax.nn.silu(_causal_dwconv(x @ Wv, vcw, vcb))
            q = q.reshape(B, T, H, DK)
            k = k.reshape(B, T, H, DK) * DK ** (-0.5)
            v = v.reshape(B, T, H, DV)
            alpha = jax.nn.sigmoid(x @ Wa + ba)
            beta = jax.nn.sigmoid(x @ Wb + bb)
            qT = jnp.transpose(q, (1, 0, 2, 3))
            kT = jnp.transpose(k, (1, 0, 2, 3))
            vT = jnp.transpose(v, (1, 0, 2, 3))
            aT = jnp.transpose(alpha, (1, 0, 2))
            bT = jnp.transpose(beta, (1, 0, 2))

            def step(S, inps):
                qt, kt, vt, at, bt = inps
                Sk = jnp.einsum('bhvk,bhk->bhv', S, kt)
                err = Sk - vt
                S = at[..., None, None] * S - bt[..., None, None] * (err[..., None] * kt[:, :, None, :])
                ot = jnp.einsum('bhvk,bhk->bhv', S, qt)
                return (S, ot)
            S0 = jnp.zeros((B, H, DV, DK), x.dtype)
            _, oT = jax.lax.scan(step, S0, (qT, kT, vT, aT, bT))
            o = jnp.transpose(oT, (1, 0, 2, 3))
            mu = jnp.mean(o, axis=-1, keepdims=True)
            var = jnp.mean(jnp.square(o - mu), axis=-1, keepdims=True)
            o = (o - mu) * jax.lax.rsqrt(var + 1e-05) * ln_w + ln_b
            g = jax.nn.sigmoid(x @ Wg).reshape(B, T, H, DV)
            o = (o * g).reshape(B, T, H * DV)
            return o @ Wo
        key = jax.random.key(seed)
        ks = jax.random.split(key, 16)
        s = 0.02
        inp = {'x': jax.random.normal(ks[0], (4, 512, HID), jnp.float32), 'Wq': jax.random.normal(ks[1], (HID, H * DK), jnp.float32) * s, 'Wk': jax.random.normal(ks[2], (HID, H * DK), jnp.float32) * s, 'Wv': jax.random.normal(ks[3], (HID, H * DV), jnp.float32) * s, 'Wa': jax.random.normal(ks[4], (HID, H), jnp.float32) * s, 'ba': jnp.zeros((H,), jnp.float32), 'Wb': jax.random.normal(ks[5], (HID, H), jnp.float32) * s, 'bb': jnp.zeros((H,), jnp.float32), 'Wg': jax.random.normal(ks[6], (HID, H * DV), jnp.float32) * s, 'Wo': jax.random.normal(ks[7], (H * DV, HID), jnp.float32) * s, 'qcw': jax.random.normal(ks[8], (H * DK, KS), jnp.float32) * 0.3, 'qcb': jnp.zeros((H * DK,), jnp.float32), 'kcw': jax.random.normal(ks[9], (H * DK, KS), jnp.float32) * 0.3, 'kcb': jnp.zeros((H * DK,), jnp.float32), 'vcw': jax.random.normal(ks[10], (H * DV, KS), jnp.float32) * 0.3, 'vcb': jnp.zeros((H * DV,), jnp.float32), 'ln_w': jnp.ones((DV,), jnp.float32), 'ln_b': jnp.zeros((DV,), jnp.float32)}
        return inp
    _L0_attn_in = _L0_attn_setup()

    def _L0_ffn_setup():
        import jax, jax.numpy as jnp
        import numpy as np
        E, H, I, TOPK = (16, 512, 352, 4)
        B, S = (2, 256)
        key = jax.random.key(seed)
        ks = jax.random.split(key, 6)
        hidden_states = jax.random.normal(ks[0], (B, S, H), dtype=jnp.float32)
        topk_idx = jax.random.randint(ks[1], (B, S, TOPK), 0, E)
        topk_weight = jax.random.uniform(ks[2], (B, S, TOPK), dtype=jnp.float32) / TOPK
        gate_weight = jax.random.normal(ks[3], (E, I, H), dtype=jnp.float32) * (1.0 / np.sqrt(H))
        up_weight = jax.random.normal(ks[4], (E, I, H), dtype=jnp.float32) * (1.0 / np.sqrt(H))
        down_weight = jax.random.normal(ks[5], (E, H, I), dtype=jnp.float32) * (1.0 / np.sqrt(I))
        return {'hidden_states': hidden_states, 'topk_idx': topk_idx, 'topk_weight': topk_weight, 'gate_weight': gate_weight, 'up_weight': up_weight, 'down_weight': down_weight}
    _L0_ffn_in = _L0_ffn_setup()
    _d = {'L0_attn_x': _L0_attn_in['x'], 'L0_attn_Wq': _L0_attn_in['Wq'], 'L0_attn_Wk': _L0_attn_in['Wk'], 'L0_attn_Wv': _L0_attn_in['Wv'], 'L0_attn_Wa': _L0_attn_in['Wa'], 'L0_attn_ba': _L0_attn_in['ba'], 'L0_attn_Wb': _L0_attn_in['Wb'], 'L0_attn_bb': _L0_attn_in['bb'], 'L0_attn_Wg': _L0_attn_in['Wg'], 'L0_attn_Wo': _L0_attn_in['Wo'], 'L0_attn_qcw': _L0_attn_in['qcw'], 'L0_attn_qcb': _L0_attn_in['qcb'], 'L0_attn_kcw': _L0_attn_in['kcw'], 'L0_attn_kcb': _L0_attn_in['kcb'], 'L0_attn_vcw': _L0_attn_in['vcw'], 'L0_attn_vcb': _L0_attn_in['vcb'], 'L0_attn_ln_w': _L0_attn_in['ln_w'], 'L0_attn_ln_b': _L0_attn_in['ln_b'], 'L0_ffn_topk_idx': _L0_ffn_in['topk_idx'], 'L0_ffn_topk_weight': _L0_ffn_in['topk_weight'], 'L0_ffn_gate_weight': _L0_ffn_in['gate_weight'], 'L0_ffn_up_weight': _L0_ffn_in['up_weight'], 'L0_ffn_down_weight': _L0_ffn_in['down_weight']}
    _x0 = _d['L0_attn_x']
    _d['L0_attn_x'] = jax.random.normal(jax.random.fold_in(jax.random.key(seed), 1), (2, 2048, 512), dtype=_x0.dtype)
    del _x0
    return _d

def reference(L0_attn_x, L0_attn_Wq, L0_attn_Wk, L0_attn_Wv, L0_attn_Wa, L0_attn_ba, L0_attn_Wb, L0_attn_bb, L0_attn_Wg, L0_attn_Wo, L0_attn_qcw, L0_attn_qcb, L0_attn_kcw, L0_attn_kcb, L0_attn_vcw, L0_attn_vcb, L0_attn_ln_w, L0_attn_ln_b, L0_ffn_topk_idx, L0_ffn_topk_weight, L0_ffn_gate_weight, L0_ffn_up_weight, L0_ffn_down_weight):

    def _L0_attn_ref(x, Wq, Wk, Wv, Wa, ba, Wb, bb, Wg, Wo, qcw, qcb, kcw, kcb, vcw, vcb, ln_w, ln_b):
        import jax, jax.numpy as jnp
        import numpy as np
        H = 16
        DK = 128
        DV = 128
        HID = 512
        KS = 4

        def _causal_dwconv(x, w, b):
            xc = jnp.transpose(x, (0, 2, 1))
            out = jax.lax.conv_general_dilated(xc, w[:, None, :], window_strides=(1,), padding=[(KS - 1, 0)], feature_group_count=xc.shape[1], dimension_numbers=('NCH', 'OIH', 'NCH'))
            out = out + b[None, :, None]
            return jnp.transpose(out, (0, 2, 1))

        def _forward(x, Wq, Wk, Wv, Wa, ba, Wb, bb, Wg, Wo, qcw, qcb, kcw, kcb, vcw, vcb, ln_w, ln_b):
            B, T, _ = x.shape
            q = jax.nn.silu(_causal_dwconv(x @ Wq, qcw, qcb))
            k = jax.nn.silu(_causal_dwconv(x @ Wk, kcw, kcb))
            v = jax.nn.silu(_causal_dwconv(x @ Wv, vcw, vcb))
            q = q.reshape(B, T, H, DK)
            k = k.reshape(B, T, H, DK) * DK ** (-0.5)
            v = v.reshape(B, T, H, DV)
            alpha = jax.nn.sigmoid(x @ Wa + ba)
            beta = jax.nn.sigmoid(x @ Wb + bb)
            qT = jnp.transpose(q, (1, 0, 2, 3))
            kT = jnp.transpose(k, (1, 0, 2, 3))
            vT = jnp.transpose(v, (1, 0, 2, 3))
            aT = jnp.transpose(alpha, (1, 0, 2))
            bT = jnp.transpose(beta, (1, 0, 2))

            def step(S, inps):
                qt, kt, vt, at, bt = inps
                Sk = jnp.einsum('bhvk,bhk->bhv', S, kt)
                err = Sk - vt
                S = at[..., None, None] * S - bt[..., None, None] * (err[..., None] * kt[:, :, None, :])
                ot = jnp.einsum('bhvk,bhk->bhv', S, qt)
                return (S, ot)
            S0 = jnp.zeros((B, H, DV, DK), x.dtype)
            _, oT = jax.lax.scan(step, S0, (qT, kT, vT, aT, bT))
            o = jnp.transpose(oT, (1, 0, 2, 3))
            mu = jnp.mean(o, axis=-1, keepdims=True)
            var = jnp.mean(jnp.square(o - mu), axis=-1, keepdims=True)
            o = (o - mu) * jax.lax.rsqrt(var + 1e-05) * ln_w + ln_b
            g = jax.nn.sigmoid(x @ Wg).reshape(B, T, H, DV)
            o = (o * g).reshape(B, T, H * DV)
            return o @ Wo
        return _forward(x, Wq, Wk, Wv, Wa, ba, Wb, bb, Wg, Wo, qcw, qcb, kcw, kcb, vcw, vcb, ln_w, ln_b)

    def _L0_ffn_ref(hidden_states, topk_idx, topk_weight, gate_weight, up_weight, down_weight):
        import jax, jax.numpy as jnp
        import numpy as np
        E, H, I, TOPK = (16, 512, 352, 4)
        B, S = (2, 256)
        b, s, h = hidden_states.shape
        n_tokens = b * s
        topk = topk_idx.shape[-1]
        x = hidden_states.reshape(n_tokens, h)
        flat_expert = topk_idx.reshape(-1)
        flat_weight = topk_weight.reshape(-1).astype(hidden_states.dtype)
        perm = jnp.argsort(flat_expert)
        tok = jnp.repeat(jnp.arange(n_tokens), topk)[perm]
        xs = x[tok]
        group_sizes = jnp.bincount(flat_expert, length=E).astype(jnp.int32)
        gate = jax.lax.ragged_dot(xs, jnp.swapaxes(gate_weight, 1, 2), group_sizes)
        up = jax.lax.ragged_dot(xs, jnp.swapaxes(up_weight, 1, 2), group_sizes)
        h_act = jax.nn.silu(gate) * up
        down = jax.lax.ragged_dot(h_act, jnp.swapaxes(down_weight, 1, 2), group_sizes)
        w_sorted = flat_weight[perm]
        out = jnp.zeros((n_tokens, h), hidden_states.dtype).at[tok].add(down * w_sorted[:, None])
        return out.reshape(b, s, h)
    x = L0_attn_x
    xn = _layernorm(x, axis=-1)
    x = x + _L0_attn_ref(xn, L0_attn_Wq, L0_attn_Wk, L0_attn_Wv, L0_attn_Wa, L0_attn_ba, L0_attn_Wb, L0_attn_bb, L0_attn_Wg, L0_attn_Wo, L0_attn_qcw, L0_attn_qcb, L0_attn_kcw, L0_attn_kcb, L0_attn_vcw, L0_attn_vcb, L0_attn_ln_w, L0_attn_ln_b) + _L0_ffn_ref(xn, L0_ffn_topk_idx, L0_ffn_topk_weight, L0_ffn_gate_weight, L0_ffn_up_weight, L0_ffn_down_weight)
    return x

_drawn_inputs = setup_inputs


def setup_inputs(seed=0):
    import zlib

    import numpy as np

    out = dict(_drawn_inputs(seed))
    spreads = {'L0_attn_ba': (0.0, 0.8),
     'L0_attn_bb': (0.0, 0.765),
     'L0_attn_qcb': (0.0, 0.1),
     'L0_attn_kcb': (0.0, 0.1),
     'L0_attn_vcb': (0.0, 0.1),
     'L0_attn_ln_w': (1.0, 0.2),
     'L0_attn_ln_b': (0.0, 0.1)}
    factors = {}
    for name, (base, spread) in spreads.items():
        noise = np.random.default_rng([zlib.crc32(name.encode()), seed]).standard_normal(out[name].shape)
        drawn = base * np.exp(spread * noise) if base else spread * noise
        out[name] = jnp.asarray(drawn.astype(out[name].dtype))
    for name, factor in factors.items():
        out[name] = (out[name] * factor).astype(out[name].dtype)
    return out
```

```python
from contextlib import ExitStack

import concourse.bass as bass
import concourse.mybir as mybir

F32 = mybir.dt.float32
F32R = mybir.dt.float32r
I32 = mybir.dt.int32
ALU = mybir.AluOpType
ACT = mybir.ActivationFunctionType

P = 128
B, T, HID = 2, 2048, 512
H, D = 16, 128
KS = 4
NT = B * T
KC = HID // P
C = 128
G = 4
GT = G * C
GROUPS = T // GT
NH = B * H
E, I, TOPK = 16, 352, 4
IC = [(0, 128), (128, 128), (256, 96)]
S_K = float(D) ** -0.5
EPS = 1e-5

LEVELS = [2, 4, 8, 16, 32]
STEPS = 2 + 3 * len(LEVELS) + 2
ACT_PER = 1 + 2 * len(LEVELS) + 1
TT_PER = 1 + len(LEVELS) + 1
MK_PER = len(LEVELS) + 1
CHAIN = {1: 0, 2: 1, 4: 2, 5: 3, 7: 4, 8: 5, 10: 6, 11: 7, 13: 8, 14: 9, 16: 10, 17: 11}
PIECES = [len(range(-(-48 * i // (2 * STEPS)), -(-48 * (i + 1) // (2 * STEPS)))) for i in range(2 * STEPS)]
MASK_AT = {0: 0, 1: 1, 3: 2, 6: 3, 9: 4, 12: 5}
COPY_AT = {1: (0, 0)}
TT_AT = {}
for _l in range(MK_PER):
    COPY_AT[2 + 3 * _l] = (1, _l)
    TT_AT[3 + 3 * _l] = _l
    if _l < len(LEVELS):
        COPY_AT[4 + 3 * _l] = (0, _l + 1)
Y_AT = [0, 1, 2, 1]
BUILT = 13 + 5 * (2 + len(LEVELS))
CONV_AT = {6: (0, 0), 7: (0, 1), 8: (0, 2), 11: (1, 0), 12: (1, 1), 13: (1, 2), 16: (2, 0), 17: (2, 1), 18: (2, 2)}


def wait(eng, sem, value):
    if isinstance(value, int) and value <= 0:
        return
    eng.wait_ge(sem, value)


def fixed(eng, value, most):
    return value if isinstance(value, int) else eng.snap(eng.to_reg(value), max_val=most)


def loop(eng, n, turn):
    turn(0)
    with eng.Fori(1, n) as i:
        turn(i)


def program(nc, x, Wq, Wk, Wv, Wab, bab, Wg, Wo, taps, ln_w, ln_b, topk_idx, topk_weight, gate_up, down, out):
    with ExitStack() as ctx:
        def sb(name, shape, dt=F32):
            return ctx.enter_context(nc.sbuf_tensor(name, shape, dt))

        xT_hi_d = nc.dram_tensor("xT_hi_d", (P, KC, NT), F32, kind="Internal").ap()
        xT_lo_d = nc.dram_tensor("xT_lo_d", (P, KC, NT), F32, kind="Internal").ap()
        alpha_d = nc.dram_tensor("alpha_d", (B, H, T), F32, kind="Internal").ap()
        beta_d = nc.dram_tensor("beta_d", (B, H, T), F32, kind="Internal").ap()
        oT_d = nc.dram_tensor("oT_d", (NH, P, T), F32, kind="Internal").ap()
        x_rows = x.rearrange("b t n -> (b t) n")
        out_rows = out.rearrange("b t n -> (b t) n")

        ident = sb("ident", [P, 2, P])
        pow_half = sb("pow_half", [P, G])
        moe = sb("moe", [P, GT // P, HID])
        bank = [ctx.enter_context(nc.psum_tensor(f"bank{i}", [P, 512], F32)) for i in range(8)]

        prepare(nc, bank, ident, pow_half, x_rows, Wab, bab, xT_hi_d, xT_lo_d, alpha_d, beta_d)
        experts(nc, bank, moe, xT_hi_d, xT_lo_d, topk_idx, topk_weight, gate_up, down)
        heads(nc, bank, ident, pow_half, xT_hi_d, xT_lo_d, alpha_d, beta_d, oT_d, (Wk, Wq, Wv, Wg), taps, ln_w, ln_b)
        project(nc, bank, moe, x_rows, oT_d, Wo, out_rows)


def prepare(nc, bank, ident, pow_half, x_rows, Wab, bab, xT_hi_d, xT_lo_d, alpha_d, beta_d):
    NG = NT // GT
    TILES = GT // P
    with ExitStack() as ctx:
        def sb(name, shape, dt=F32):
            return ctx.enter_context(nc.sbuf_tensor(name, shape, dt))

        def sem(name):
            return ctx.enter_context(nc.semaphore(name))

        x_in = sb("x_in", [P, TILES, HID])
        stats = sb("stats", [P, TILES, 6])
        mv = sb("mv", [P, TILES, 2])
        veps = sb("veps", [P, TILES])
        rstd = sb("rstd", [P, TILES])
        xn = sb("xn", [P, 2, HID])
        xT = sb("xT", [P, KC, GT])
        xT_hi = sb("xT_hi", [P, KC, GT], F32R)
        xT_lo = sb("xT_lo", [P, KC, GT], F32R)
        wab = sb("wab", [P, KC, 2 * H])
        bab_s = sb("bab_s", [2 * H, 1])
        ab = sb("ab", [2 * H, GT])
        x_loaded = [sem(f"x_loaded{i}") for i in range(TILES)]
        const_built = sem("const_built")
        small_loaded = sem("small_loaded")
        stats_done = sem("stats_done")
        mv_done = sem("mv_done")
        veps_done = sem("veps_done")
        rstd_done = sem("rstd_done")
        xn_done = sem("xn_done")
        turned = sem("turned")
        hi_done = sem("hi_done")
        lo_done = sem("lo_done")
        z_done = sem("z_done")
        ab_done = sem("ab_done")
        xT_stored = sem("xT_stored")
        ab_stored = sem("ab_stored")
        block = ctx.enter_context(nc.Block())

        @block.sync
        def _(sp):
            sp.dma_start(wab[:], Wab.rearrange("(k p) n -> p k n", p=P)).then_inc(small_loaded, 16)
            sp.dma_start(bab_s[:], bab).then_inc(small_loaded, 16)

            def turn(b, q):
                g = b * GROUPS + q
                for i in range(TILES):
                    wait(sp, xn_done, g * TILES)
                    sp.dma_start(x_in[:, i], x_rows[bass.ds(g * GT + i * P, P), :]).then_inc(x_loaded[i], 16)
                wait(sp, hi_done, g * TILES + TILES)
                sp.dma_start(xT_hi_d[:, :, bass.ds(b * T + q * GT, GT)], xT_hi[:].bitcast(F32)).then_inc(xT_stored, 16)
                wait(sp, lo_done, g * TILES + TILES)
                sp.dma_start(xT_lo_d[:, :, bass.ds(b * T + q * GT, GT)], xT_lo[:].bitcast(F32)).then_inc(xT_stored, 16)
                wait(sp, ab_done, g + 1)
                for part, dst in ((0, alpha_d), (1, beta_d)):
                    sp.dma_start(dst[bass.ds(b, 1), :, bass.ds(q * GT, GT)].rearrange("o h t -> (o h) t"),
                                 ab[part * H:(part + 1) * H, :]).then_inc(ab_stored, 16)

            turn(0, 0)
            with sp.Fori(1, GROUPS) as q:
                turn(sp.snap(sp.to_reg(0), max_val=B - 1), q)
            with sp.Fori(0, GROUPS) as q:
                turn(sp.snap(sp.to_reg(1), max_val=B - 1), q)
            wait(sp, xT_stored, NG * 32)
            wait(sp, ab_stored, NG * 32)

        @block.gpsimd
        def _(pool):
            pool.memset(ident[:], 0.0).then_inc(const_built, 1)
            pool.memset(pow_half[:], -0.5).then_inc(const_built, 1)
            wait(pool, const_built, 2)
            for c in range(2):
                pool.affine_select(out=ident[:, c], in_=ident[:, c], compare_op=ALU.not_equal, fill=1.0, base=0,
                                   pattern=[[-1, P]], channel_multiplier=1).then_inc(const_built, 1)

            def turn(g):
                wait(pool, veps_done, 2 * g + 2)
                pool.tensor_tensor(rstd[:], veps[:], pow_half[:], ALU.pow).then_inc(rstd_done, 1)
                wait(pool, xT_stored, g * 32)
                for i in range(TILES):
                    cols = slice(i * P, (i + 1) * P)
                    wait(pool, hi_done, g * TILES + i + 1)
                    pool.tensor_tensor(xT_lo[:, :, cols], xT[:, :, cols], xT_hi[:, :, cols].bitcast(F32),
                                       ALU.subtract).then_inc(lo_done, 1)

            loop(pool, NG, turn)

        @block.vector
        def _(dve):
            def turn(g):
                last_tile = TILES - 1
                for i in range(TILES):
                    if i:
                        wait(dve, stats_done, g * TILES + i)
                    wait(dve, x_loaded[i], g * 16 + 16)
                    dve.bn_stats(stats[:, i], x_in[:, i]).then_inc(stats_done, 1)
                    if i:
                        dve.bn_aggr(mv[:, i - 1], stats[:, i - 1]).then_inc(mv_done, 1)
                wait(dve, stats_done, g * TILES + TILES)
                wait(dve, mv_done, g * TILES + last_tile)
                dve.tensor_scalar(veps[:, 0:last_tile], mv[:, 0:last_tile, 1], EPS, None, ALU.add)\
                   .then_inc(veps_done, 1)
                dve.bn_aggr(mv[:, last_tile], stats[:, last_tile]).then_inc(mv_done, 1)
                wait(dve, mv_done, g * TILES + TILES)
                dve.tensor_scalar(veps[:, last_tile:], mv[:, last_tile:, 1], EPS, None, ALU.add)\
                   .then_inc(veps_done, 1)
                wait(dve, rstd_done, g + 1)
                for i in range(TILES):
                    wait(dve, turned, g * TILES + max(i - 1, 0))
                    dve.tensor_scalar(xn[:, i % 2], x_in[:, i], mv[:, i, 0:1], rstd[:, i:i + 1],
                                      ALU.subtract, ALU.mult).then_inc(xn_done, 1)

            loop(dve, NG, turn)

        @block.tensor
        def _(pe):
            wait(pe, const_built, 4)
            wait(pe, small_loaded, 32)

            def turn(g):
                for i in range(TILES):
                    wait(pe, xn_done, g * TILES + i + 1)
                    wait(pe, hi_done, g * TILES + max(i - 1, 0))
                    for k in range(KC):
                        last = pe.transpose(bank[i % 2][:, k * P:(k + 1) * P], xn[:, i % 2, k * P:(k + 1) * P],
                                            ident[:, 0])
                    last.then_inc(turned, 1)
                wait(pe, hi_done, g * TILES + TILES)
                wait(pe, ab_done, g)
                for k in range(KC):
                    last = pe.matmul(bank[2][0:2 * H, :], wab[:, k], xT[:, k], start=(k == 0), stop=(k == KC - 1))
                last.then_inc(z_done, 1)

            loop(pe, NG, turn)

        @block.scalar
        def _(act):
            wait(act, small_loaded, 32)

            def turn(g):
                wait(act, xT_stored, g * 32)
                wait(act, lo_done, g * TILES)
                wait(act, z_done, g)
                for i in range(TILES):
                    cols = slice(i * P, (i + 1) * P)
                    tile = bank[i % 2][:, :].rearrange("p (k n) -> p k n", k=KC)
                    wait(act, turned, g * TILES + i + 1)
                    act.activation(xT[:, :, cols], tile, ACT.Copy)
                    act.activation(xT_hi[:, :, cols], tile, ACT.Copy).then_inc(hi_done, 1)
                wait(act, z_done, g + 1)
                wait(act, ab_stored, g * 32)
                act.activation(ab[:], bank[2][0:2 * H, :], ACT.Sigmoid, bias=bab_s[:, 0:1]).then_inc(ab_done, 1)

            loop(act, NG, turn)


def experts(nc, bank, moe, xT_hi_d, xT_lo_d, topk_idx, topk_weight, gate_up, down):
    NM = len(IC)
    TT = GT // P
    with ExitStack() as ctx:
        def sb(name, shape, dt=F32):
            return ctx.enter_context(nc.sbuf_tensor(name, shape, dt))

        def sem(name):
            return ctx.enter_context(nc.semaphore(name))

        x_hi = sb("x_hi", [P, KC, GT], F32R)
        x_lo = sb("x_lo", [P, KC, GT], F32R)
        gu_raw = sb("gu_raw", [P, KC, 2 * I])
        dn_raw = sb("dn_raw", [P, NM, HID])
        gu_hi = sb("gu_hi", [P, 2, KC, 2 * I], F32R)
        gu_lo = sb("gu_lo", [P, 2, KC, 2 * I], F32R)
        dn_hi = sb("dn_hi", [P, 2, NM, HID], F32R)
        dn_lo = sb("dn_lo", [P, 2, NM, HID], F32R)
        gated = sb("gated", [P, 2, GT])
        h = sb("h", [P, NM, GT])
        h_hi = sb("h_hi", [P, NM, GT], F32R)
        h_lo = sb("h_lo", [P, NM, GT], F32R)
        idx = sb("idx", [P, TT, TOPK], I32)
        idx_f = sb("idx_f", [P, TT, TOPK])
        top_w = sb("top_w", [P, TT, TOPK])
        number = sb("number", [P, E])
        share = sb("share", [P, TT, TOPK, E])
        route = sb("route", [P, TT, E])
        x_loaded = sem("mx_loaded")
        top_loaded = sem("top_loaded")
        gu_loaded = sem("gu_loaded")
        dn_loaded = sem("dn_loaded")
        number_built = sem("number_built")
        dn_cleared = sem("dn_cleared")
        idx_done = sem("idx_done")
        share_done = sem("share_done")
        route_done = sem("route_done")
        gu_hi_done = sem("gu_hi_done")
        gu_lo_done = sem("gu_lo_done")
        dn_hi_done = sem("dn_hi_done")
        dn_lo_done = sem("dn_lo_done")
        gu_done = sem("gu_done")
        gated_done = sem("gated_done")
        h_done = sem("h_done")
        h_hi_done = sem("h_hi_done")
        h_lo_done = sem("h_lo_done")
        down_done = sem("down_done")
        moe_done = sem("moe_done")
        block = ctx.enter_context(nc.Block())

        @block.sync
        def _(sp):
            sp.dma_start(x_hi[:].bitcast(F32), xT_hi_d[:, :, 0:GT]).then_inc(x_loaded, 16)
            sp.dma_start(x_lo[:].bitcast(F32), xT_lo_d[:, :, 0:GT]).then_inc(x_loaded, 16)
            sp.dma_start(idx[:], topk_idx.rearrange("(t p) k -> p t k", p=P)).then_inc(top_loaded, 16)
            sp.dma_start(top_w[:], topk_weight.rearrange("(t p) k -> p t k", p=P)).then_inc(top_loaded, 16)
            wait(sp, dn_cleared, 1)

            def turn(i):
                e = fixed(sp, i & (E - 1), E - 1)
                wait(sp, gu_lo_done, i)
                sp.dma_start(gu_raw[:], gate_up[bass.ds(e, 1)].rearrange("o (k p) n -> p (o k) n", p=P))\
                  .then_inc(gu_loaded, 16)
                wait(sp, dn_lo_done, i)
                sp.dma_start(dn_raw[:, 0:2], down[bass.ds(e, 1), 0:2 * P].rearrange("o (k p) n -> p (o k) n", p=P))\
                  .then_inc(dn_loaded, 16)
                sp.dma_start(dn_raw[0:I - 2 * P, 2], down[bass.ds(e, 1), 2 * P:I].rearrange("o p n -> (o p) n"))\
                  .then_inc(dn_loaded, 16)

            loop(sp, E + 1, turn)

        @block.gpsimd
        def _(pool):
            pool.memset(dn_raw[:, 2], 0.0).then_inc(dn_cleared, 1)
            pool.iota(number[:], pattern=[[1, E]], base=0, channel_multiplier=0,
                      allow_small_or_imprecise_dtypes=True).then_inc(number_built, 1)

            def cut_low(e, q):
                wait(pool, dn_hi_done, e + 1)
                pool.tensor_tensor(dn_lo[:, q], dn_raw[:], dn_hi[:, q].bitcast(F32), ALU.subtract)\
                    .then_inc(dn_lo_done, 1)

            cut_low(0, 0)

            def turn(j):
                for q in range(2):
                    e = 2 * j + q
                    for m in range(NM):
                        n = IC[m][1]
                        wait(pool, h_hi_done, NM * e + m + 1)
                        pool.tensor_tensor(h_lo[0:n, m], h[0:n, m], h_hi[0:n, m].bitcast(F32), ALU.subtract)\
                            .then_inc(h_lo_done, 1)
                    cut_low(e + 1, 1 - q)

            loop(pool, E // 2, turn)

        @block.vector
        def _(dve):
            dve.memset(moe[:], 0.0).then_inc(moe_done, 1)
            wait(dve, top_loaded, 32)
            wait(dve, number_built, 1)
            dve.tensor_copy(idx_f[:], idx[:]).then_inc(idx_done, 1)
            wait(dve, idx_done, 1)
            for t in range(TT):
                for k in range(TOPK):
                    dve.tensor_scalar(share[:, t, k], number[:], idx_f[:, t, k:k + 1], top_w[:, t, k:k + 1],
                                      ALU.is_equal, ALU.mult).then_inc(share_done, 1)
            wait(dve, share_done, TT * TOPK)
            dve.tensor_reduce(route[:], share[:].rearrange("p t k e -> p t e k"), mybir.AxisListType.X, ALU.add)\
                .then_inc(route_done, 1)
            wait(dve, route_done, 1)

            def cut_low(e, q):
                wait(dve, gu_hi_done, e + 1)
                dve.tensor_tensor(gu_lo[:, q], gu_raw[:], gu_hi[:, q].bitcast(F32), ALU.subtract)\
                   .then_inc(gu_lo_done, 1)

            cut_low(0, 0)

            def turn(j):
                for q in range(2):
                    e = 2 * j + q
                    for m in range(NM):
                        n = IC[m][1]
                        wait(dve, gated_done, NM * e + m + 1)
                        wait(dve, h_lo_done, NM * e)
                        dve.tensor_tensor(h[0:n, m], gated[0:n, m % 2], bank[2 * (m % 2) + 1][0:n, :], ALU.mult)\
                           .then_inc(h_done, 1)
                    cut_low(e + 1, 1 - q)
                    for t in range(TT):
                        wait(dve, down_done, TT * e + t + 1)
                        wait(dve, moe_done, TT * e + 1)
                        dve.scalar_tensor_tensor(out=moe[:, t], in0=bank[4 + t][:], scalar=route[:, t, bass.ds(e, 1)],
                                                 in1=moe[:, t], op0=ALU.mult, op1=ALU.add).then_inc(moe_done, 1)

            loop(dve, E // 2, turn)

        @block.scalar
        def _(act):
            def cut_high(e, q):
                wait(act, gu_loaded, 16 * e + 16)
                act.activation(gu_hi[:, q], gu_raw[:], ACT.Copy).then_inc(gu_hi_done, 1)
                wait(act, dn_loaded, 32 * e + 32)
                act.activation(dn_hi[:, q], dn_raw[:], ACT.Copy).then_inc(dn_hi_done, 1)

            cut_high(0, 0)

            def turn(j):
                for q in range(2):
                    e = 2 * j + q
                    for m in range(NM):
                        n = IC[m][1]
                        wait(act, gu_done, NM * e + m + 1)
                        wait(act, h_done, NM * e + max(m - 1, 0))
                        act.activation(gated[0:n, m % 2], bank[2 * (m % 2)][0:n, :], ACT.Silu).then_inc(gated_done, 1)
                        wait(act, h_done, NM * e + m + 1)
                        wait(act, down_done, TT * e)
                        act.activation(h_hi[0:n, m], h[0:n, m], ACT.Copy).then_inc(h_hi_done, 1)
                    cut_high(e + 1, 1 - q)

            loop(act, E // 2, turn)

        @block.tensor
        def _(pe):
            wait(pe, x_loaded, 32)

            def turn(j):
                for q in range(2):
                    e = 2 * j + q
                    wait(pe, gu_hi_done, e + 1)
                    wait(pe, gu_lo_done, e + 1)
                    for m in range(NM):
                        i0, n = IC[m]
                        wait(pe, h_done, NM * e + max(m - 1, 0))
                        for u in range(2):
                            dst = bank[2 * (m % 2) + u][0:n, :]
                            cols = slice(u * I + i0, u * I + i0 + n)
                            for k in range(KC):
                                pe.matmul(dst, gu_hi[:, q, k, cols], x_hi[:, k], start=(k == 0), stop=False)
                                pe.matmul(dst, gu_hi[:, q, k, cols], x_lo[:, k], start=False, stop=False)
                                last = pe.matmul(dst, gu_lo[:, q, k, cols], x_hi[:, k], start=False,
                                                 stop=(k == KC - 1))
                        last.then_inc(gu_done, 1)
                    wait(pe, dn_hi_done, e + 1)
                    wait(pe, dn_lo_done, e + 1)
                    wait(pe, moe_done, TT * e + 1)
                    for m in range(NM):
                        n = IC[m][1]
                        wait(pe, h_hi_done, NM * e + m + 1)
                        wait(pe, h_lo_done, NM * e + m + 1)
                        for t in range(TT):
                            rows = slice(t * P, (t + 1) * P)
                            pe.matmul(bank[4 + t][:], h_hi[0:n, m, rows], dn_hi[0:n, q, m], start=(m == 0), stop=False)
                            pe.matmul(bank[4 + t][:], h_hi[0:n, m, rows], dn_lo[0:n, q, m], start=False, stop=False)
                            last = pe.matmul(bank[4 + t][:], h_lo[0:n, m, rows], dn_hi[0:n, q, m], start=False,
                                             stop=(m == NM - 1))
                            if m == NM - 1:
                                last.then_inc(down_done, 1)

            loop(pe, E // 2, turn)


def heads(nc, bank, ident, pow_half, xT_hi_d, xT_lo_d, alpha_d, beta_d, oT_d, weights, taps, ln_w, ln_b):
    QK, KQ = 1, 0
    NPROJ = len(weights)
    with ExitStack() as ctx:
        def sb(name, shape, dt=F32):
            return ctx.enter_context(nc.sbuf_tensor(name, shape, dt))

        def sem(name):
            return ctx.enter_context(nc.semaphore(name))

        mask = [sb(f"mask{b}", [P, 2, P]) for b in [1] + LEVELS + [64]]
        zeros = sb("zeros", [P, C])
        lnw = sb("lnw", [P, 1])
        lnb = sb("lnb", [P, 1])
        x_hi = sb("hx_hi", [P, KC, T], F32R)
        x_lo = sb("hx_lo", [P, KC, T], F32R)
        w_raw = sb("w_raw", [P, NPROJ, KC, D])
        w_hi = sb("w_hi", [P, NPROJ, KC, D], F32R)
        w_lo = sb("w_lo", [P, NPROJ, KC, D], F32R)
        tap_next = sb("tap_next", [P, 3, KS + 1])
        tap = sb("tap", [P, 3, KS + 1])
        y = [[sb(f"y{i}_{j}", [P, KS - 1 + GT]) for j in range(3)] for i in range(3)]
        conv = sb("conv", [P, GT])
        kq = sb("kq", [P, 2, 2, GT])
        vT = sb("vT", [P, GT])
        gT = sb("gT", [P, GROUPS, GT])
        alpha = sb("alpha", [P, 2, GT])
        beta = sb("beta", [P, 2, GT])
        decay = sb("decay", [P, G, 1 + C])
        gamma = sb("gamma", [P, 2, G, 1 + C])
        k_beta = sb("k_beta", [P, GT])
        k_gamma = sb("k_gamma", [P, 2, GT])
        q_gamma = sb("q_gamma", [P, 2, GT])
        LT = sb("LT", [P, G, C])
        AT = sb("AT", [P, 2, G, C])
        first = sb("first", [P, G, C])
        masked = sb("masked", [P, 2, G, C])
        TT = sb("TT", [P, 2, G, C])
        Tn = sb("Tn", [P, G, C])
        MT = sb("MT", [P, G, C])
        k_rows = sb("k_rows", [P, 2, G, D])
        v_rows = sb("v_rows", [P, 2, G, D])
        S = sb("S", [P, D])
        R = sb("R", [P, D])
        Wc = sb("Wc", [P, D])
        stats = sb("hstats", [P, G, 6])
        mv = sb("hmv", [P, G, 2])
        veps = sb("hveps", [P, G])
        rstd = sb("hrstd", [P, G])
        on = sb("on", [P, G, D])
        oT = sb("oT", [P, GT])
        oG = sb("oG", [P, GT])

        PJ, IB, TR, CH, OB = bank[0:2], bank[2:4], bank[4], bank[5], bank[6:8]

        built = sem("hbuilt")
        ln_loaded = sem("ln_loaded")
        x_loaded = [sem(f"hx_loaded{g}") for g in range(GROUPS)]
        w_loaded = [sem(f"w_loaded{i}") for i in range(NPROJ)]
        tap_loaded = sem("tap_loaded")
        alpha_loaded = [sem(f"alpha_loaded{i}") for i in range(2)]
        beta_loaded = [sem(f"beta_loaded{i}") for i in range(2)]
        o_stored = sem("o_stored")
        proj_done = sem("proj_done")
        step_done = [sem("step_done_a"), sem("step_done_b")]
        chain_done = sem("chain_done")
        k_turned = sem("k_turned")
        v_turned = sem("v_turned")
        o_turned = sem("o_turned")
        y_done = sem("hy_done")
        silu_done = sem("silu_done")
        tanh_done = sem("tanh_done")
        copied = [sem("copied_a"), sem("copied_b")]
        w_done = sem("w_done")
        v_done = sem("v_done")
        oT_done = sem("oT_done")
        whi_done = sem("whi_done")
        wlo_done = sem("wlo_done")
        tap_copied = sem("tap_copied")
        decay_done = sem("decay_done")
        gamma_done = sem("gamma_done")
        lt_done = [sem("lt_done_a"), sem("lt_done_b")]
        at_done = sem("at_done")
        first_done = [sem("first_done_a"), sem("first_done_b")]
        tt_done = [sem("tt_done_a"), sem("tt_done_b")]
        k_done = sem("k_done")
        r_done = sem("r_done")
        s_done = sem("s_done")
        conv_done = sem("conv_done")
        gate_done = sem("gate_done")
        stats_done = sem("hstats_done")
        mv_done = sem("hmv_done")
        veps_done = sem("hveps_done")
        on_done = sem("on_done")
        mask_done = [sem("mask_done_a"), sem("mask_done_b")]
        tap_done = sem("tap_done")
        kb_done = sem("kb_done")
        kq_gamma_done = sem("kq_gamma_done")
        rstd_done = sem("hrstd_done")
        oG_done = sem("oG_done")
        block = ctx.enter_context(nc.Block())

        def turns(eng, turn):
            turn(eng, -1, 2, False, False, True, False)
            turn(eng, -1, 3, False, True, True, False)
            for g in range(GROUPS):
                turn(eng, 0, g, True, True, True, g > 0)
            with eng.Fori(1, NH - 1) as hh:
                for g in range(GROUPS):
                    turn(eng, hh, g, True, True, True, True)
            for g in range(GROUPS):
                turn(eng, NH - 1, g, True, g < 3, g < 2, True)
            turn(eng, NH, 0, False, False, False, True)

        def counter(hh, g):
            def at(per, d, c=0):
                return hh * (GROUPS * per) + ((g + d) * per + c)
            return at

        def half(c):
            return slice(2 * c, 2 * c + 2)

        def chunk(c):
            return slice(c * C, (c + 1) * C)

        def has_next(hh):
            return not isinstance(hh, int) or 0 <= hh < NH - 1

        def row_loads(hh, g):
            return (hh * (GROUPS // 2)) * 16 + ((g + 2) // 2 + 1) * 16

        @block.sync
        def _(sp):
            def load_x(b, g):
                cols = slice(b * T + g * GT, b * T + (g + 1) * GT)
                sp.dma_start(x_hi[:, :, g * GT:(g + 1) * GT].bitcast(F32), xT_hi_d[:, :, cols]).then_inc(x_loaded[g], 16)
                sp.dma_start(x_lo[:, :, g * GT:(g + 1) * GT].bitcast(F32), xT_lo_d[:, :, cols]).then_inc(x_loaded[g], 16)

            def load_w(i, h):
                sp.dma_start(w_raw[:, i], weights[i][:, bass.ds(h * D, D)].rearrange("(k p) n -> p k n", p=P))\
                  .then_inc(w_loaded[i], 16)

            def load_tap(h):
                sp.dma_start(tap_next[:], taps[bass.ds(h, 1)].rearrange("o p (i j) -> (o p) i j", i=3))\
                  .then_inc(tap_loaded, 16)

            def load_rows(dst, src, hh, g, q, sem):
                rows = src.rearrange("b h t -> (b h) t")[bass.ds(hh, 1), g * GT:(g + 1) * GT]
                sp.dma_start(dst[:, q], rows.to_broadcast([P, GT])).then_inc(sem[q], 16)

            def turn(hh, g, x_next=None, after_next=True, last=False):
                at = counter(hh, g)
                later, q = (hh, 3) if g == 0 else (hh + 1, g - 1), (g + 3) % 2
                if not (last and g > 0):
                    sp.wait_ge(kb_done, at(1, 2))
                    load_rows(beta, beta_d, *later, q, beta_loaded)
                    sp.wait_ge(gamma_done, at(1, 2))
                    load_rows(alpha, alpha_d, *later, q, alpha_loaded)
                if not (isinstance(hh, int) and hh == 0 and g == 0):
                    sp.wait_ge(oG_done, at(1, 0))
                    where, gw = (hh, g - 1) if g > 0 else (hh - 1, 3)
                    sp.dma_start(oT_d[bass.ds(where, 1), :, gw * GT:(gw + 1) * GT].rearrange("o p t -> (o p) t"), oG[:])\
                      .then_inc(o_stored, 16)
                if g == 3 and after_next:
                    h2 = (hh + 2) & (H - 1)
                    h2 = fixed(sp, h2, H - 1)
                    for i in range(NPROJ):
                        sp.wait_ge(wlo_done, hh * NPROJ + (NPROJ + i + 1))
                        load_w(i, h2)
                    sp.wait_ge(tap_copied, hh + 2)
                    load_tap(h2)
                if x_next is not None:
                    sp.wait_ge(proj_done, NPROJ * ((H - 1) * GROUPS + x_next + 1))
                    load_x(1, x_next)

            sp.dma_start(lnw[:], ln_w).then_inc(ln_loaded, 16)
            sp.dma_start(lnb[:], ln_b).then_inc(ln_loaded, 16)
            for i in range(NPROJ):
                load_w(i, 0)
            load_tap(0)
            for g in range(GROUPS):
                load_x(0, g)
            for g in range(2):
                load_rows(beta, beta_d, 0, g, g, beta_loaded)
                load_rows(alpha, alpha_d, 0, g, g, alpha_loaded)
            sp.wait_ge(kb_done, 1)
            load_rows(beta, beta_d, 0, 2, 0, beta_loaded)
            for i in range(NPROJ):
                sp.wait_ge(wlo_done, i + 1)
                load_w(i, 1)
            sp.wait_ge(tap_copied, 1)
            load_tap(1)
            sp.wait_ge(gamma_done, 1)
            load_rows(alpha, alpha_d, 0, 2, 0, alpha_loaded)
            for g in range(GROUPS):
                turn(0, g)
            with sp.Fori(1, H - 2) as hh:
                for g in range(GROUPS):
                    turn(hh, g)
            for g in range(GROUPS):
                turn(H - 2, g, x_next={2: 0, 3: 1}.get(g))
            for g in range(GROUPS):
                turn(H - 1, g, x_next={0: 2, 1: 3}.get(g))
            with sp.Fori(H, NH - 2) as hh:
                for g in range(GROUPS):
                    turn(hh, g)
            for g in range(GROUPS):
                turn(NH - 2, g, after_next=False)
            for g in range(GROUPS):
                turn(NH - 1, g, after_next=False, last=True)
            sp.wait_ge(oG_done, NH * GROUPS)
            sp.dma_start(oT_d[NH - 1, :, 3 * GT:4 * GT], oG[:]).then_inc(o_stored, 16)
            sp.wait_ge(o_stored, 16 * NH * GROUPS)

        @block.gpsimd
        def _(pool):
            n = 0
            for tile in [*mask, zeros]:
                pool.memset(tile[:], 0.0).then_inc(built, 1)
                n += 1
            pool.memset(decay[:, :, 0:1], 0.0).then_inc(built, 1)
            pool.memset(gamma[:, :, :, 0:1], 1.0).then_inc(built, 1)
            for i in range(3):
                pool.memset(y[i][0][:, 0:KS - 1], 0.0).then_inc(built, 1)
            n += 5
            pool.wait_ge(built, n)
            for tile, b in zip(mask, [1] + LEVELS + [64]):
                part = tile[:].rearrange("p c (q r) -> p c q r", r=2 * b)[:, :, :, b:2 * b]
                pool.memset(part, 1.0).then_inc(built, 1)
                n += 1
                for base, step, mult in ((0, -2 * b, 1), (b - 1, 2 * b, -1)):
                    pool.wait_ge(built, n)
                    for c in range(2):
                        pool.affine_select(out=part[:, c], in_=part[:, c], compare_op=ALU.is_ge, fill=0.0, base=base,
                                           pattern=[[step, P // (2 * b)], [0, b]], channel_multiplier=mult)\
                            .then_inc(built, 1)
                        n += 1
            assert n == BUILT

            def cut_low(i, value):
                pool.wait_ge(whi_done, value)
                pool.tensor_tensor(w_lo[:, i], w_raw[:, i], w_hi[:, i].bitcast(F32), ALU.subtract).then_inc(wlo_done, 1)

            for i in range(NPROJ):
                cut_low(i, i + 1)

            def turn(pool, hh, g, chain, inv, proj, ln):
                at = counter(hh, g)
                for s in range(STEPS):
                    if inv and s in MASK_AT:
                        i = MASK_AT[s]
                        for c in range(2):
                            if i == 0:
                                pool.wait_ge(lt_done[c], at(1, 2))
                            if i >= 2:
                                pool.wait_ge(step_done[c], at(STEPS, 1, 2 + 3 * (i - 2) + 1))
                            pool.tensor_tensor(masked[:, i % 2, half(c)], LT[:, half(c)], mask[1 + i][:], ALU.mult)\
                                .then_inc(mask_done[c], 1)
                    if ln and s == 2:
                        pool.wait_ge(veps_done, at(1, 0))
                        pool.tensor_tensor(rstd[:], veps[:], pow_half[:], ALU.pow).then_inc(rstd_done, 1)
                    if inv and s in (4, 5):
                        i, par = s - 4, (g + 1) % 2
                        if i == 0:
                            pool.wait_ge(gamma_done, at(1, 2))
                            wait(pool, chain_done, at(12, 0))
                        dst = (k_gamma, q_gamma)[i][:, par].rearrange("p (c t) -> p c t", c=G)
                        pool.tensor_tensor(dst, kq[:, par, i].rearrange("p (c t) -> p c t", c=G),
                                           gamma[:, par, :, i:i + C], ALU.mult).then_inc(kq_gamma_done, 1)
                    if proj and s in (5, 10, 15):
                        i = (5, 10, 15).index(s)
                        pool.wait_ge(y_done, at(3, 2, i + 1))
                        if i == 0:
                            pool.wait_ge(tap_copied, (hh + 1) + (1 if g >= 2 else 0))
                        wait(pool, silu_done, at(3, 2, i))
                        pool.tensor_tensor(conv[:], y[i][Y_AT[(g + 2) % 4]][:, KS - 1:],
                                           tap[:, i, KS - 1:KS].to_broadcast([P, GT]), ALU.mult).then_inc(tap_done, 1)
                    if proj and s == 10:
                        pool.wait_ge(silu_done, at(3, 2, 1))
                        pool.wait_ge(beta_loaded[g % 2], row_loads(hh, g))
                        wait(pool, k_turned, at(1, 2))
                        pool.tensor_tensor(k_beta[:], kq[:, g % 2, KQ], beta[:, g % 2], ALU.mult).then_inc(kb_done, 1)
                    if ln and s == 11:
                        pool.wait_ge(oT_done, at(1, 0))
                        wait(pool, o_stored, at(16, -1))
                        pool.wait_ge(gate_done, at(1, 0))
                        pool.tensor_tensor(oG[:], oT[:], gT[:, (g - 1) % 4], ALU.mult).then_inc(oG_done, 1)
                    if proj and (g == 1 and s in (7, 12, 17) or g == 2 and s == 1) and has_next(hh):
                        i = {7: 0, 12: 1, 17: 2, 1: 3}[s]
                        cut_low(i, hh * NPROJ + (NPROJ + i + 1))

            turns(pool, turn)

        @block.vector
        def _(dve):
            dve.memset(S[:], 0.0).then_inc(s_done, 1)
            dve.wait_ge(built, BUILT)
            dve.wait_ge(tap_loaded, 16)
            dve.tensor_copy(tap[:], tap_next[:]).then_inc(tap_copied, 1)

            def turn(dve, hh, g, chain, inv, proj, ln):
                at = counter(hh, g)
                par, cur = (g + 1) % 2, g % 2
                for s in range(STEPS):
                    if inv and s == 0:
                        for c in range(2):
                            prod = IB[c][:].rearrange("p (c i t) -> p c i t", c=2, i=2)
                            dve.wait_ge(step_done[c], at(STEPS, 1, 1))
                            wait(dve, mask_done[c], at(MK_PER, 1))
                            if c == 0:
                                dve.wait_ge(decay_done, at(1, 2))
                            dve.scalar_tensor_tensor(out=LT[:, half(c)], in0=prod[:, :, 0], scalar=S_K * S_K,
                                                     in1=decay[:, half(c), 0:C], op0=ALU.mult, op1=ALU.mult)\
                               .then_inc(lt_done[c], 1)
                            wait(dve, chain_done, at(12, 0))
                            dve.tensor_tensor(AT[:, par, half(c)], prod[:, :, 1], decay[:, half(c), 1:1 + C],
                                              ALU.mult).then_inc(at_done, 1)
                        for c in range(2):
                            dve.wait_ge(lt_done[c], at(1, 2))
                            dve.tensor_tensor(first[:, half(c)], LT[:, half(c)], mask[0][:], ALU.mult)\
                               .then_inc(first_done[c], 1)
                        for c in range(2):
                            dve.wait_ge(first_done[c], at(1, 2))
                            dve.tensor_tensor(TT[:, par, half(c)], ident[:], first[:, half(c)], ALU.subtract)\
                               .then_inc(tt_done[c], 1)
                    if g == 2 and s == 0 and proj and has_next(hh):
                        dve.wait_ge(tap_loaded, (hh + 2) * 16)
                        dve.wait_ge(silu_done, at(3, 2))
                        dve.tensor_copy(tap[:], tap_next[:]).then_inc(tap_copied, 1)
                    if ln and s == 1:
                        dve.wait_ge(chain_done, at(12, 0))
                        wait(dve, on_done, at(4, -1))
                        for c in range(G):
                            dve.bn_stats(stats[:, c], OB[(g - 1) % 2][:, chunk(c)]).then_inc(stats_done, 1)
                        dve.wait_ge(stats_done, at(4, 0))
                    if inv and s == 1:
                        dve.wait_ge(k_turned, at(1, 2))
                        dve.tensor_tensor(k_rows[:, par], TR[:].rearrange("p (c d) -> p c d", c=G),
                                          decay[:, :, C:C + 1].to_broadcast([P, G, D]), ALU.mult).then_inc(k_done, 1)
                    if ln and s == 1:
                        for c in range(G):
                            dve.bn_aggr(mv[:, c], stats[:, c]).then_inc(mv_done, 1)
                        dve.wait_ge(mv_done, at(4, 0))
                        dve.tensor_scalar(veps[:], mv[:, :, 1], EPS, None, ALU.add).then_inc(veps_done, 1)
                    if s == 2 and inv:
                        dve.wait_ge(tanh_done, at(1, 2))
                        dve.tensor_scalar(gT[:, (g + 1) % 4], gT[:, (g + 1) % 4], 0.5, 0.5, ALU.mult, ALU.add)\
                           .then_inc(gate_done, 1)
                    if s == 3 and inv:
                        dve.wait_ge(alpha_loaded[par], row_loads(hh, g - 1))
                        wait(dve, s_done, at(4, 0, 1))
                        wait(dve, kq_gamma_done, at(2, 0))
                        for c in range(G):
                            last = dve.tensor_tensor_scan(gamma[:, par, c, 1:1 + C], alpha[:, par, chunk(c)], zeros[:],
                                                          1.0, ALU.mult, ALU.add)
                        last.then_inc(gamma_done, 1)
                    if ln and s == 5:
                        dve.wait_ge(rstd_done, at(1, 0))
                        wait(dve, o_turned, at(1, -1))
                        for c in range(G):
                            dve.tensor_scalar(on[:, c], OB[(g - 1) % 2][:, chunk(c)], mv[:, c, 0:1], rstd[:, c:c + 1],
                                              ALU.subtract, ALU.mult).then_inc(on_done, 1)
                    if inv and (s in TT_AT):
                        lvl = TT_AT[s]
                        for c in range(2):
                            dve.wait_ge(step_done[c], at(STEPS, 1, s + 1))
                            dve.wait_ge(tt_done[c], at(TT_PER, 1, lvl + 1))
                            dve.tensor_tensor(TT[:, par, half(c)], TT[:, par, half(c)],
                                              IB[c][:, 0:2 * C].rearrange("p (c t) -> p c t", c=2), ALU.subtract)\
                               .then_inc(tt_done[c], 1)
                    if chain and s in CHAIN:
                        k = CHAIN[s]
                        c, r = k // 3, k % 3
                        if r == 0:
                            dve.wait_ge(chain_done, at(12, 0, k + 1))
                            if c == 0:
                                dve.wait_ge(v_done, at(1, 1))
                            dve.scalar_tensor_tensor(out=R[:], in0=CH[:, 0:D], scalar=-S_K, in1=v_rows[:, cur, c],
                                                     op0=ALU.mult, op1=ALU.add).then_inc(r_done, 1)
                        if r == 2:
                            dve.wait_ge(chain_done, at(12, 0, k + 1))
                            dve.wait_ge(s_done, at(4, 0, c + 1))
                            if g == 3 and c == 3:
                                dve.memset(S[:], 0.0).then_inc(s_done, 1)
                            else:
                                dve.scalar_tensor_tensor(out=S[:], in0=S[:], scalar=gamma[:, cur, c, C:C + 1],
                                                         in1=CH[:, 2 * D:3 * D], op0=ALU.mult, op1=ALU.add)\
                                   .then_inc(s_done, 1)
                    if proj and s in CONV_AT:
                        i, j = CONV_AT[s]
                        if j == 0:
                            dve.wait_ge(tap_done, at(3, 2, i + 1))
                        else:
                            dve.wait_ge(conv_done, at(9, 2, 3 * i + j))
                        dve.scalar_tensor_tensor(out=conv[:], in0=y[i][Y_AT[(g + 2) % 4]][:, j:j + GT],
                                                 scalar=tap[:, i, j:j + 1], in1=conv[:], op0=ALU.mult, op1=ALU.add)\
                           .then_inc(conv_done, 1)
                    if proj and s == STEPS - 1:
                        dve.wait_ge(alpha_loaded[cur], row_loads(hh, g))
                        wait(dve, k_done, at(1, 2))
                        for c in range(G):
                            last = dve.tensor_tensor_scan(decay[:, c, 1:1 + C], alpha[:, cur, chunk(c)], ident[:, 0],
                                                          0.0, ALU.mult, ALU.add)
                        last.then_inc(decay_done, 1)

            turns(dve, turn)

        @block.scalar
        def _(act):
            act.wait_ge(built, BUILT)
            act.wait_ge(ln_loaded, 32)

            def cut_high(i, loads):
                act.wait_ge(w_loaded[i], loads)
                act.activation(w_hi[:, i], w_raw[:, i], ACT.Copy).then_inc(whi_done, 1)

            for i in range(NPROJ):
                cut_high(i, 16)

            def turn(act, hh, g, chain, inv, proj, ln):
                at = counter(hh, g)
                par, cur = (g + 1) % 2, g % 2
                for s in range(STEPS):
                    if s == 0 and inv:
                        act.wait_ge(conv_done, at(9, 2))
                        wait(act, v_turned, at(1, 1))
                        act.activation(vT[:], conv[:], ACT.Silu, bias=tap[:, 2, KS:KS + 1]).then_inc(silu_done, 1)
                        act.wait_ge(proj_done, at(NPROJ, 2))
                        wait(act, oG_done, at(1, -2))
                        act.activation(gT[:, (g + 1) % 4], PJ[1][:], ACT.Tanh, scale=0.5).then_inc(tanh_done, 1)
                    if inv and s in COPY_AT:
                        which, n = COPY_AT[s]
                        dst = (Tn, MT)[which]
                        for c in range(2):
                            act.wait_ge(step_done[c], at(STEPS, 1, s + 1))
                            act.activation(dst[:, half(c)], IB[c][:, 0:2 * C].rearrange("p (c t) -> p c t", c=2),
                                           ACT.Copy).then_inc(copied[c], 1)
                    if chain and s in CHAIN and CHAIN[s] % 3 == 1:
                        k = CHAIN[s]
                        act.wait_ge(chain_done, at(12, 0, k + 1))
                        act.activation(Wc[:], CH[:, D:2 * D], ACT.Copy, scale=S_K).then_inc(w_done, 1)
                    if proj and s in (5, 10, 15):
                        i = (5, 10, 15).index(s)
                        ahead = (g + 2) % 4
                        act.wait_ge(proj_done, at(NPROJ, 2, i + 1))
                        wait(act, conv_done, at(9, 1, 3 * i + 3))
                        if ahead < 3:
                            act.activation(y[i][Y_AT[ahead + 1]][:, 0:KS - 1], PJ[i % 2][:, GT - KS + 1:GT], ACT.Copy)
                        act.activation(y[i][Y_AT[ahead]][:, KS - 1:], PJ[i % 2][:], ACT.Copy).then_inc(y_done, 1)
                    if inv and s == 6:
                        act.wait_ge(v_turned, at(1, 2))
                        wait(act, r_done, at(4, -1, 4))
                        act.activation(v_rows[:, par], TR[:].rearrange("p (c d) -> p c d", c=G), ACT.Copy)\
                           .then_inc(v_done, 1)
                    if proj and s in (9, 14):
                        i = (9, 14).index(s)
                        act.wait_ge(conv_done, at(9, 2, 3 * i + 3))
                        wait(act, kq_gamma_done, at(2, 1))
                        act.activation(kq[:, cur, i], conv[:], ACT.Silu, bias=tap[:, i, KS:KS + 1]).then_inc(silu_done, 1)
                    if ln and s == 10:
                        act.wait_ge(o_turned, at(1, 0))
                        wait(act, oG_done, at(1, -1))
                        act.activation(oT[:], TR[:], ACT.Identity, bias=lnb[:, 0:1], scale=lnw[:, 0:1])\
                           .then_inc(oT_done, 1)
                    if proj and (g == 1 and s in (7, 12, 17) or g == 2 and s == 1) and has_next(hh):
                        i = {7: 0, 12: 1, 17: 2, 1: 3}[s]
                        act.wait_ge(proj_done, hh * (GROUPS * NPROJ) + (3 * NPROJ + i + 1))
                        cut_high(i, (hh + 2) * 16)

            turns(act, turn)

        @block.tensor
        def _(pe):
            def turn(pe, hh, g, chain, inv, proj, ln):
                at = counter(hh, g)
                par, cur = (g + 1) % 2, g % 2
                sent = [0]

                def project_some(n):
                    cols = slice((g + 2) % 4 * GT, (g + 2) % 4 * GT + GT)
                    for _ in range(n):
                        i, j = divmod(sent[0], 3 * KC)
                        k, part = divmod(j, 3)
                        sent[0] += 1
                        dst = PJ[i % 2][:]
                        if j == 0:
                            if i == 0:
                                wait(pe, y_done, at(3, 2))
                                pe.wait_ge(x_loaded[(g + 2) % 4], (((hh + (1 if g >= 2 else 0)) >> 4) + 1) * 32)
                            if i == 1:
                                wait(pe, tanh_done, at(1, 2))
                            if i >= 2:
                                pe.wait_ge(y_done, at(3, 2, i - 1))
                            pe.wait_ge(wlo_done, (hh + (1 if g >= 2 else 0)) * NPROJ + (i + 1))
                        a, b = ((w_hi, x_hi), (w_hi, x_lo), (w_lo, x_hi))[part]
                        last = pe.matmul(dst, a[:, i, k], b[:, k, cols], start=(j == 0), stop=(j == 3 * KC - 1))
                        if j == 3 * KC - 1:
                            last.then_inc(proj_done, 1)

                def step(c, s):
                    w = IB[c]
                    if s == 0:
                        pe.wait_ge(kb_done, at(1, 2))
                        pe.wait_ge(silu_done, at(3, 1, 2))
                        wait(pe, tt_done[c], at(TT_PER, 1))
                        for j in range(2):
                            n = 2 * c + j
                            last = pe.matmul(w[:, j * 2 * C:(j + 1) * 2 * C], k_beta[:, chunk(n)],
                                             kq[:, par, :, chunk(n)], start=True, stop=True)
                    elif s == 1 or (s < STEPS - 2 and (s - 2) % 3 == 2):
                        lvl = (s - 1) // 3
                        pe.wait_ge(tt_done[c], at(TT_PER, 1, lvl + 1))
                        for j in range(2):
                            last = pe.transpose(w[:, chunk(j)], TT[:, par, 2 * c + j], ident[:, 0])
                    elif (s - 2) % 3 == 0:
                        lvl = (s - 2) // 3
                        pe.wait_ge(copied[c], at(ACT_PER, 1, 2 * lvl + 1))
                        pe.wait_ge(mask_done[c], at(MK_PER, 1, lvl + 1))
                        for j in range(2):
                            last = pe.matmul(w[:, chunk(j)], masked[:, lvl % 2, 2 * c + j], Tn[:, 2 * c + j],
                                             start=True, stop=True)
                    else:
                        lvl = (s - 3) // 3
                        pe.wait_ge(copied[c], at(ACT_PER, 1, 2 * lvl + 2))
                        for j in range(2):
                            last = pe.matmul(w[:, chunk(j)], MT[:, 2 * c + j], TT[:, par, 2 * c + j],
                                             start=True, stop=True)
                    last.then_inc(step_done[c], 1)

                def chain_step(k):
                    c, r = divmod(k, 3)
                    o = OB[cur][:, chunk(c)]
                    if r == 0:
                        pe.wait_ge(s_done, at(4, 0, c + 1))
                        if c == 0:
                            pe.wait_ge(kq_gamma_done, at(2, 1))
                            wait(pe, on_done, at(4, -1))
                        pe.matmul(o, q_gamma[:, cur, chunk(c)], S[:], start=True, stop=False)
                        pe.matmul(CH[:, 0:D], k_gamma[:, cur, chunk(c)], S[:], start=True, stop=True)\
                          .then_inc(chain_done, 1)
                    if r == 1:
                        pe.wait_ge(r_done, at(4, 0, c + 1))
                        if c == 0:
                            for i in range(2):
                                pe.wait_ge(tt_done[i], at(TT_PER, 1))
                        pe.matmul(CH[:, D:2 * D], TT[:, cur, c], R[:], start=True, stop=True).then_inc(chain_done, 1)
                    if r == 2:
                        pe.wait_ge(w_done, at(4, 0, c + 1))
                        if c == 0:
                            pe.wait_ge(k_done, at(1, 1))
                            pe.wait_ge(at_done, at(2, 1))
                        pe.matmul(o, AT[:, cur, c], Wc[:], start=False, stop=True)
                        pe.matmul(CH[:, 2 * D:3 * D], k_rows[:, cur, c], Wc[:], start=True, stop=True)\
                          .then_inc(chain_done, 1)

                for s in range(STEPS):
                    if inv:
                        step(0, s)
                    if proj:
                        project_some(PIECES[2 * s])
                    if chain and s in CHAIN:
                        chain_step(CHAIN[s])
                    if inv:
                        step(1, s)
                    if proj:
                        project_some(PIECES[2 * s + 1])
                    if inv and s == 0:
                        wait(pe, oT_done, at(1, -1))
                        for c in range(G):
                            last = pe.transpose(TR[:, chunk(c)], k_beta[:, chunk(c)], ident[:, 0])
                        last.then_inc(k_turned, 1)
                    if inv and s == 5:
                        pe.wait_ge(silu_done, at(3, 2))
                        pe.wait_ge(k_done, at(1, 2))
                        for c in range(G):
                            last = pe.transpose(TR[:, chunk(c)], vT[:, chunk(c)], ident[:, 0])
                        last.then_inc(v_turned, 1)
                    if ln and s == 9:
                        pe.wait_ge(on_done, at(4, 0))
                        if inv:
                            pe.wait_ge(v_done, at(1, 2))
                        wait(pe, oT_done, at(1, -1))
                        for c in range(G):
                            last = pe.transpose(TR[:, chunk(c)], on[:, c], ident[:, 0])
                        last.then_inc(o_turned, 1)

            turns(pe, turn)


def project(nc, bank, moe, x_rows, oT_d, Wo, out_rows):
    HQ = 4
    with ExitStack() as ctx:
        def sb(name, shape, dt=F32):
            return ctx.enter_context(nc.sbuf_tensor(name, shape, dt))

        def sem(name):
            return ctx.enter_context(nc.semaphore(name))

        wo_raw = sb("wo_raw", [P, H, HID])
        wo_hi = sb("wo_hi", [P, H, HID], F32R)
        wo_lo = sb("wo_lo", [P, H, HID], F32R)
        o_raw = sb("o_raw", [P, 2, H, P])
        o_hi = sb("o_hi", [P, 2, H, P], F32R)
        o_lo = sb("o_lo", [P, 2, H, P], F32R)
        x_t = sb("x_t", [P, 2, HID])
        y = sb("y", [P, 2, HID])
        wo_loaded = sem("wo_loaded")
        wo_hi_done = sem("wo_hi_done")
        wo_lo_done = sem("wo_lo_done")
        o_loaded = [sem(f"o_loaded{q}") for q in range(2)]
        x_loaded = [sem(f"xr_loaded{q}") for q in range(2)]
        o_hi_done = sem("o_hi_done")
        o_lo_done = sem("o_lo_done")
        tile_done = sem("tile_done")
        x_moe_done = sem("x_moe_done")
        y_done = sem("y_done")
        y_stored = [sem(f"y_stored{q}") for q in range(2)]
        oT = oT_d.rearrange("(b h) p t -> b p h t", b=B)
        PAIRS = NT // P // 2
        MOE_PAIRS = GT // P // 2
        block = ctx.enter_context(nc.Block())

        @block.sync
        def _(sp):
            sp.dma_start(wo_raw[:], Wo.rearrange("(h p) n -> p h n", p=P)).then_inc(wo_loaded, 16)

            def turn(b, i):
                j = b * (PAIRS // B) + i
                for q in range(2):
                    wait(sp, o_lo_done, 2 * j)
                    sp.dma_start(o_raw[:, q], oT[bass.ds(b, 1), :, :, bass.ds(i * (2 * P) + q * P, P)]
                                 .rearrange("o p h t -> (o p) h t")).then_inc(o_loaded[q], 16)
                    wait(sp, y_done, 2 * j)
                    sp.dma_start(x_t[:, q], x_rows[bass.ds(j * (2 * P) + q * P, P), :]).then_inc(x_loaded[q], 16)

            turn(0, 0)
            with sp.Fori(1, PAIRS // B) as i:
                turn(0, i)
            with sp.Fori(0, PAIRS // B) as i:
                turn(1, i)

        @block.gpsimd
        def _(pool):
            def turn(j):
                for q in range(2):
                    wait(pool, y_done, 2 * j + q + 1)
                    pool.dma_start(out_rows[bass.ds(j * (2 * P) + q * P, P), :], y[:, q]).then_inc(y_stored[q], 16)

            loop(pool, PAIRS, turn)
            for q in range(2):
                wait(pool, y_stored[q], 16 * PAIRS)

        @block.scalar
        def _(act):
            wait(act, wo_loaded, 16)
            for i in range(0, H, HQ):
                act.activation(wo_hi[:, i:i + HQ], wo_raw[:, i:i + HQ], ACT.Copy).then_inc(wo_hi_done, 1)

            def turn(j):
                for q in range(2):
                    wait(act, o_loaded[q], 16 * j + 16)
                    wait(act, tile_done, 2 * j)
                    act.activation(o_hi[:, q], o_raw[:, q], ACT.Copy).then_inc(o_hi_done, 1)

            loop(act, PAIRS, turn)

        @block.vector
        def _(dve):
            for i in range(0, H, HQ):
                wait(dve, wo_hi_done, i // HQ + 1)
                dve.tensor_tensor(wo_lo[:, i:i + HQ], wo_raw[:, i:i + HQ], wo_hi[:, i:i + HQ].bitcast(F32),
                                  ALU.subtract).then_inc(wo_lo_done, 1)

            def cut(j, q):
                wait(dve, o_hi_done, 2 * j + q + 1)
                wait(dve, tile_done, 2 * j)
                dve.tensor_tensor(o_lo[:, q], o_raw[:, q], o_hi[:, q].bitcast(F32), ALU.subtract)\
                   .then_inc(o_lo_done, 1)

            def finish(j, q):
                wait(dve, tile_done, 2 * j + q + 1)
                wait(dve, y_stored[q], 16 * j)
                dve.tensor_tensor(y[:, q], bank[q][:], x_t[:, q], ALU.add).then_inc(y_done, 1)

            for j in range(MOE_PAIRS):
                for q in range(2):
                    cut(j, q)
                for q in range(2):
                    wait(dve, x_loaded[q], 16 * j + 16)
                    dve.tensor_tensor(x_t[:, q], x_t[:, q], moe[:, 2 * j + q], ALU.add).then_inc(x_moe_done, 1)
                    wait(dve, x_moe_done, 2 * j + q + 1)
                    finish(j, q)
            with dve.Fori(MOE_PAIRS, PAIRS) as j:
                for q in range(2):
                    cut(j, q)
                for q in range(2):
                    wait(dve, x_loaded[q], 16 * j + 16)
                    finish(j, q)

        @block.tensor
        def _(pe):
            wait(pe, wo_lo_done, H // HQ)

            def turn(j):
                for q in range(2):
                    wait(pe, o_hi_done, 2 * j + q + 1)
                    wait(pe, o_lo_done, 2 * j + q + 1)
                    wait(pe, y_done, 2 * j)
                    for i in range(H):
                        pe.matmul(bank[q][:], o_hi[:, q, i], wo_hi[:, i], start=(i == 0), stop=False)
                        pe.matmul(bank[q][:], o_hi[:, q, i], wo_lo[:, i], start=False, stop=False)
                        last = pe.matmul(bank[q][:], o_lo[:, q, i], wo_hi[:, i], start=False, stop=(i == H - 1))
                    last.then_inc(tile_done, 1)

            loop(pe, PAIRS, turn)


def kernel(**inputs):
    import numpy as np
    import concourse.bacc as bacc
    from concourse import mybir as _mybir
    from concourse.bass_utils import run_bass_kernel_spmd

    a = {n.removeprefix("L0_"): np.asarray(v) for n, v in inputs.items()}
    heads_last = lambda v: v.reshape(H, D, -1)
    laid = {
        "x": a["attn_x"], "Wq": a["attn_Wq"], "Wk": a["attn_Wk"], "Wv": a["attn_Wv"],
        "Wab": np.concatenate([a["attn_Wa"], a["attn_Wb"]], axis=1),
        "bab": np.concatenate([a["attn_ba"], a["attn_bb"]])[:, None],
        "Wg": a["attn_Wg"], "Wo": a["attn_Wo"],
        "taps": np.concatenate([np.concatenate([heads_last(a[f"attn_{n}cw"]), heads_last(a[f"attn_{n}cb"])], axis=2)
                                for n in "kqv"], axis=2),
        "ln_w": a["attn_ln_w"][:, None], "ln_b": a["attn_ln_b"][:, None],
        "topk_idx": a["ffn_topk_idx"].reshape(-1, TOPK), "topk_weight": a["ffn_topk_weight"].reshape(-1, TOPK),
        "gate_up": np.concatenate([a["ffn_gate_weight"].transpose(0, 2, 1), a["ffn_up_weight"].transpose(0, 2, 1)], axis=2),
        "down": a["ffn_down_weight"].transpose(0, 2, 1),
    }
    nc = bacc.Bacc("TRN2", target_bir_lowering=False, num_devices=1)
    arrays, args = {}, {}
    for name, v in laid.items():
        v = np.ascontiguousarray(v)
        arrays[f"in_{name}"] = v
        args[name] = nc.dram_tensor(f"in_{name}", v.shape, _mybir.dt.from_np(v.dtype), kind="ExternalInput").ap()
    args["out"] = nc.dram_tensor("out_0", laid["x"].shape, F32, kind="ExternalOutput").ap()
    program(nc, **args)
    r = run_bass_kernel_spmd(nc, [arrays], core_ids=[0])
    return r.results[0]["out_0"]
```

```python
from contextlib import ExitStack

import concourse.bass as bass
import concourse.mybir as mybir

F32 = mybir.dt.float32
F32R = mybir.dt.float32r
I32 = mybir.dt.int32
ALU = mybir.AluOpType
ACT = mybir.ActivationFunctionType

P = 128
B, T, HID = 2, 2048, 512
H, D = 16, 128
KS = 4
NT = B * T
KC = HID // P
C = 128
G = 4
GT = G * C
GROUPS = T // GT
NH = B * H
E, I, TOPK = 16, 352, 4
IC = [(0, 128), (128, 128), (256, 96)]
S_K = float(D) ** -0.5
EPS = 1e-5

SB = 8
LEVELS = [8, 16]
STEPS = 19
CHAIN = {1: 0, 2: 1, 4: 2, 5: 3, 7: 4, 8: 5, 10: 6, 11: 7, 13: 8, 14: 9, 16: 10, 17: 11}
PIECES = [len(range(-(-48 * i // (2 * STEPS)), -(-48 * (i + 1) // (2 * STEPS)))) for i in range(2 * STEPS)]
A_AT, T8_AT = 0, 4
SOLVE_AT = {17: (0, 2), 18: (2, 4), 0: (4, 6), 1: (6, 7)}
MT_AT = {6: 0, 9: 1}
TT_AT = {7: 0, 10: 1}
Y32_AT, T32_AT, Y64_AT, T64_AT = 13, 14, 16, 17
L_AT, BASE_AT, DECAY_AT = 12, 16, 8
MASK_AT = {14: 0, 15: 1}
STEP_PER = 1 + 2 * len(LEVELS)
LATE_PER = 4
SOLVE_PER = 2 * (SB - 1)
Y_AT = [0, 1, 2, 1]
BUILT = 12 + 5 * len(LEVELS)
CONV_AT = {6: (0, 0), 7: (0, 1), 8: (0, 2), 11: (1, 0), 12: (1, 1), 13: (1, 2), 16: (2, 0), 17: (2, 1), 18: (2, 2)}


def wait(eng, sem, value):
    if isinstance(value, int) and value <= 0:
        return
    eng.wait_ge(sem, value)


def fixed(eng, value, most):
    return value if isinstance(value, int) else eng.snap(eng.to_reg(value), max_val=most)


def loop(eng, n, turn):
    turn(0)
    with eng.Fori(1, n) as i:
        turn(i)


def program(nc, x, Wq, Wk, Wv, Wab, bab, Wg, Wo, taps, ln_w, ln_b, topk_idx, topk_weight, gate_up, down, out):
    with ExitStack() as ctx:
        def sb(name, shape, dt=F32):
            return ctx.enter_context(nc.sbuf_tensor(name, shape, dt))

        xT_hi_d = nc.dram_tensor("xT_hi_d", (P, KC, NT), F32, kind="Internal").ap()
        xT_lo_d = nc.dram_tensor("xT_lo_d", (P, KC, NT), F32, kind="Internal").ap()
        alpha_d = nc.dram_tensor("alpha_d", (B, H, T), F32, kind="Internal").ap()
        beta_d = nc.dram_tensor("beta_d", (B, H, T), F32, kind="Internal").ap()
        oT_d = nc.dram_tensor("oT_d", (NH, P, T), F32, kind="Internal").ap()
        x_rows = x.rearrange("b t n -> (b t) n")
        out_rows = out.rearrange("b t n -> (b t) n")

        ident = sb("ident", [P, 2, P])
        pow_half = sb("pow_half", [P, G])
        moe = sb("moe", [P, GT // P, HID])
        bank = [ctx.enter_context(nc.psum_tensor(f"bank{i}", [P, 512], F32)) for i in range(8)]

        prepare(nc, bank, ident, pow_half, x_rows, Wab, bab, xT_hi_d, xT_lo_d, alpha_d, beta_d)
        experts(nc, bank, moe, xT_hi_d, xT_lo_d, topk_idx, topk_weight, gate_up, down)
        heads(nc, bank, ident, pow_half, xT_hi_d, xT_lo_d, alpha_d, beta_d, oT_d, (Wk, Wq, Wv, Wg), taps, ln_w, ln_b)
        project(nc, bank, moe, x_rows, oT_d, Wo, out_rows)


def prepare(nc, bank, ident, pow_half, x_rows, Wab, bab, xT_hi_d, xT_lo_d, alpha_d, beta_d):
    NG = NT // GT
    TILES = GT // P
    with ExitStack() as ctx:
        def sb(name, shape, dt=F32):
            return ctx.enter_context(nc.sbuf_tensor(name, shape, dt))

        def sem(name):
            return ctx.enter_context(nc.semaphore(name))

        x_in = sb("x_in", [P, TILES, HID])
        stats = sb("stats", [P, TILES, 6])
        mv = sb("mv", [P, TILES, 2])
        veps = sb("veps", [P, TILES])
        rstd = sb("rstd", [P, TILES])
        xn = sb("xn", [P, 2, HID])
        xT = sb("xT", [P, KC, GT])
        xT_hi = sb("xT_hi", [P, KC, GT], F32R)
        xT_lo = sb("xT_lo", [P, KC, GT], F32R)
        wab = sb("wab", [P, KC, 2 * H])
        bab_s = sb("bab_s", [2 * H, 1])
        ab = sb("ab", [2 * H, GT])
        x_loaded = [sem(f"x_loaded{i}") for i in range(TILES)]
        const_built = sem("const_built")
        small_loaded = sem("small_loaded")
        stats_done = sem("stats_done")
        mv_done = sem("mv_done")
        veps_done = sem("veps_done")
        rstd_done = sem("rstd_done")
        xn_done = sem("xn_done")
        turned = sem("turned")
        hi_done = sem("hi_done")
        lo_done = sem("lo_done")
        z_done = sem("z_done")
        ab_done = sem("ab_done")
        xT_stored = sem("xT_stored")
        ab_stored = sem("ab_stored")
        block = ctx.enter_context(nc.Block())

        @block.sync
        def _(sp):
            sp.dma_start(wab[:], Wab.rearrange("(k p) n -> p k n", p=P)).then_inc(small_loaded, 16)
            sp.dma_start(bab_s[:], bab).then_inc(small_loaded, 16)

            def turn(b, q):
                g = b * GROUPS + q
                for i in range(TILES):
                    wait(sp, xn_done, g * TILES)
                    sp.dma_start(x_in[:, i], x_rows[bass.ds(g * GT + i * P, P), :]).then_inc(x_loaded[i], 16)
                wait(sp, hi_done, g * TILES + TILES)
                sp.dma_start(xT_hi_d[:, :, bass.ds(b * T + q * GT, GT)], xT_hi[:].bitcast(F32)).then_inc(xT_stored, 16)
                wait(sp, lo_done, g * TILES + TILES)
                sp.dma_start(xT_lo_d[:, :, bass.ds(b * T + q * GT, GT)], xT_lo[:].bitcast(F32)).then_inc(xT_stored, 16)
                wait(sp, ab_done, g + 1)
                for part, dst in ((0, alpha_d), (1, beta_d)):
                    sp.dma_start(dst[bass.ds(b, 1), :, bass.ds(q * GT, GT)].rearrange("o h t -> (o h) t"),
                                 ab[part * H:(part + 1) * H, :]).then_inc(ab_stored, 16)

            turn(0, 0)
            with sp.Fori(1, GROUPS) as q:
                turn(sp.snap(sp.to_reg(0), max_val=B - 1), q)
            with sp.Fori(0, GROUPS) as q:
                turn(sp.snap(sp.to_reg(1), max_val=B - 1), q)
            wait(sp, xT_stored, NG * 32)
            wait(sp, ab_stored, NG * 32)

        @block.gpsimd
        def _(pool):
            pool.memset(ident[:], 0.0).then_inc(const_built, 1)
            pool.memset(pow_half[:], -0.5).then_inc(const_built, 1)
            wait(pool, const_built, 2)
            for c in range(2):
                pool.affine_select(out=ident[:, c], in_=ident[:, c], compare_op=ALU.not_equal, fill=1.0, base=0,
                                   pattern=[[-1, P]], channel_multiplier=1).then_inc(const_built, 1)

            def turn(g):
                wait(pool, veps_done, 2 * g + 2)
                pool.tensor_tensor(rstd[:], veps[:], pow_half[:], ALU.pow).then_inc(rstd_done, 1)
                wait(pool, xT_stored, g * 32)
                for i in range(TILES):
                    cols = slice(i * P, (i + 1) * P)
                    wait(pool, hi_done, g * TILES + i + 1)
                    pool.tensor_tensor(xT_lo[:, :, cols], xT[:, :, cols], xT_hi[:, :, cols].bitcast(F32),
                                       ALU.subtract).then_inc(lo_done, 1)

            loop(pool, NG, turn)

        @block.vector
        def _(dve):
            def turn(g):
                last_tile = TILES - 1
                for i in range(TILES):
                    if i:
                        wait(dve, stats_done, g * TILES + i)
                    wait(dve, x_loaded[i], g * 16 + 16)
                    dve.bn_stats(stats[:, i], x_in[:, i]).then_inc(stats_done, 1)
                    if i:
                        dve.bn_aggr(mv[:, i - 1], stats[:, i - 1]).then_inc(mv_done, 1)
                wait(dve, stats_done, g * TILES + TILES)
                wait(dve, mv_done, g * TILES + last_tile)
                dve.tensor_scalar(veps[:, 0:last_tile], mv[:, 0:last_tile, 1], EPS, None, ALU.add)\
                   .then_inc(veps_done, 1)
                dve.bn_aggr(mv[:, last_tile], stats[:, last_tile]).then_inc(mv_done, 1)
                wait(dve, mv_done, g * TILES + TILES)
                dve.tensor_scalar(veps[:, last_tile:], mv[:, last_tile:, 1], EPS, None, ALU.add)\
                   .then_inc(veps_done, 1)
                wait(dve, rstd_done, g + 1)
                for i in range(TILES):
                    wait(dve, turned, g * TILES + max(i - 1, 0))
                    dve.tensor_scalar(xn[:, i % 2], x_in[:, i], mv[:, i, 0:1], rstd[:, i:i + 1],
                                      ALU.subtract, ALU.mult).then_inc(xn_done, 1)

            loop(dve, NG, turn)

        @block.tensor
        def _(pe):
            wait(pe, const_built, 4)
            wait(pe, small_loaded, 32)

            def turn(g):
                for i in range(TILES):
                    wait(pe, xn_done, g * TILES + i + 1)
                    wait(pe, hi_done, g * TILES + max(i - 1, 0))
                    for k in range(KC):
                        last = pe.transpose(bank[i % 2][:, k * P:(k + 1) * P], xn[:, i % 2, k * P:(k + 1) * P],
                                            ident[:, 0])
                    last.then_inc(turned, 1)
                wait(pe, hi_done, g * TILES + TILES)
                wait(pe, ab_done, g)
                for k in range(KC):
                    last = pe.matmul(bank[2][0:2 * H, :], wab[:, k], xT[:, k], start=(k == 0), stop=(k == KC - 1))
                last.then_inc(z_done, 1)

            loop(pe, NG, turn)

        @block.scalar
        def _(act):
            wait(act, small_loaded, 32)

            def turn(g):
                wait(act, xT_stored, g * 32)
                wait(act, lo_done, g * TILES)
                wait(act, z_done, g)
                for i in range(TILES):
                    cols = slice(i * P, (i + 1) * P)
                    tile = bank[i % 2][:, :].rearrange("p (k n) -> p k n", k=KC)
                    wait(act, turned, g * TILES + i + 1)
                    act.activation(xT[:, :, cols], tile, ACT.Copy)
                    act.activation(xT_hi[:, :, cols], tile, ACT.Copy).then_inc(hi_done, 1)
                wait(act, z_done, g + 1)
                wait(act, ab_stored, g * 32)
                act.activation(ab[:], bank[2][0:2 * H, :], ACT.Sigmoid, bias=bab_s[:, 0:1]).then_inc(ab_done, 1)

            loop(act, NG, turn)


def experts(nc, bank, moe, xT_hi_d, xT_lo_d, topk_idx, topk_weight, gate_up, down):
    NM = len(IC)
    TT = GT // P
    with ExitStack() as ctx:
        def sb(name, shape, dt=F32):
            return ctx.enter_context(nc.sbuf_tensor(name, shape, dt))

        def sem(name):
            return ctx.enter_context(nc.semaphore(name))

        x_hi = sb("x_hi", [P, KC, GT], F32R)
        x_lo = sb("x_lo", [P, KC, GT], F32R)
        gu_raw = sb("gu_raw", [P, KC, 2 * I])
        dn_raw = sb("dn_raw", [P, NM, HID])
        gu_hi = sb("gu_hi", [P, 2, KC, 2 * I], F32R)
        gu_lo = sb("gu_lo", [P, 2, KC, 2 * I], F32R)
        dn_hi = sb("dn_hi", [P, 2, NM, HID], F32R)
        dn_lo = sb("dn_lo", [P, 2, NM, HID], F32R)
        gated = sb("gated", [P, 2, GT])
        h = sb("h", [P, NM, GT])
        h_hi = sb("h_hi", [P, NM, GT], F32R)
        h_lo = sb("h_lo", [P, NM, GT], F32R)
        idx = sb("idx", [P, TT, TOPK], I32)
        idx_f = sb("idx_f", [P, TT, TOPK])
        top_w = sb("top_w", [P, TT, TOPK])
        number = sb("number", [P, E])
        share = sb("share", [P, TT, TOPK, E])
        route = sb("route", [P, TT, E])
        x_loaded = sem("mx_loaded")
        top_loaded = sem("top_loaded")
        gu_loaded = sem("gu_loaded")
        dn_loaded = sem("dn_loaded")
        number_built = sem("number_built")
        dn_cleared = sem("dn_cleared")
        idx_done = sem("idx_done")
        share_done = sem("share_done")
        route_done = sem("route_done")
        gu_hi_done = sem("gu_hi_done")
        gu_lo_done = sem("gu_lo_done")
        dn_hi_done = sem("dn_hi_done")
        dn_lo_done = sem("dn_lo_done")
        gu_done = sem("gu_done")
        gated_done = sem("gated_done")
        h_done = sem("h_done")
        h_hi_done = sem("h_hi_done")
        h_lo_done = sem("h_lo_done")
        down_done = sem("down_done")
        moe_done = sem("moe_done")
        block = ctx.enter_context(nc.Block())

        @block.sync
        def _(sp):
            sp.dma_start(x_hi[:].bitcast(F32), xT_hi_d[:, :, 0:GT]).then_inc(x_loaded, 16)
            sp.dma_start(x_lo[:].bitcast(F32), xT_lo_d[:, :, 0:GT]).then_inc(x_loaded, 16)
            sp.dma_start(idx[:], topk_idx.rearrange("(t p) k -> p t k", p=P)).then_inc(top_loaded, 16)
            sp.dma_start(top_w[:], topk_weight.rearrange("(t p) k -> p t k", p=P)).then_inc(top_loaded, 16)
            wait(sp, dn_cleared, 1)

            def turn(i):
                e = fixed(sp, i & (E - 1), E - 1)
                wait(sp, gu_lo_done, i)
                sp.dma_start(gu_raw[:], gate_up[bass.ds(e, 1)].rearrange("o (k p) n -> p (o k) n", p=P))\
                  .then_inc(gu_loaded, 16)
                wait(sp, dn_lo_done, i)
                sp.dma_start(dn_raw[:, 0:2], down[bass.ds(e, 1), 0:2 * P].rearrange("o (k p) n -> p (o k) n", p=P))\
                  .then_inc(dn_loaded, 16)
                sp.dma_start(dn_raw[0:I - 2 * P, 2], down[bass.ds(e, 1), 2 * P:I].rearrange("o p n -> (o p) n"))\
                  .then_inc(dn_loaded, 16)

            loop(sp, E + 1, turn)

        @block.gpsimd
        def _(pool):
            pool.memset(dn_raw[:, 2], 0.0).then_inc(dn_cleared, 1)
            pool.iota(number[:], pattern=[[1, E]], base=0, channel_multiplier=0,
                      allow_small_or_imprecise_dtypes=True).then_inc(number_built, 1)

            def cut_low(e, q):
                wait(pool, dn_hi_done, e + 1)
                pool.tensor_tensor(dn_lo[:, q], dn_raw[:], dn_hi[:, q].bitcast(F32), ALU.subtract)\
                    .then_inc(dn_lo_done, 1)

            cut_low(0, 0)

            def turn(j):
                for q in range(2):
                    e = 2 * j + q
                    for m in range(NM):
                        n = IC[m][1]
                        wait(pool, h_hi_done, NM * e + m + 1)
                        pool.tensor_tensor(h_lo[0:n, m], h[0:n, m], h_hi[0:n, m].bitcast(F32), ALU.subtract)\
                            .then_inc(h_lo_done, 1)
                    cut_low(e + 1, 1 - q)

            loop(pool, E // 2, turn)

        @block.vector
        def _(dve):
            dve.memset(moe[:], 0.0).then_inc(moe_done, 1)
            wait(dve, top_loaded, 32)
            wait(dve, number_built, 1)
            dve.tensor_copy(idx_f[:], idx[:]).then_inc(idx_done, 1)
            wait(dve, idx_done, 1)
            for t in range(TT):
                for k in range(TOPK):
                    dve.tensor_scalar(share[:, t, k], number[:], idx_f[:, t, k:k + 1], top_w[:, t, k:k + 1],
                                      ALU.is_equal, ALU.mult).then_inc(share_done, 1)
            wait(dve, share_done, TT * TOPK)
            dve.tensor_reduce(route[:], share[:].rearrange("p t k e -> p t e k"), mybir.AxisListType.X, ALU.add)\
                .then_inc(route_done, 1)
            wait(dve, route_done, 1)

            def cut_low(e, q):
                wait(dve, gu_hi_done, e + 1)
                dve.tensor_tensor(gu_lo[:, q], gu_raw[:], gu_hi[:, q].bitcast(F32), ALU.subtract)\
                   .then_inc(gu_lo_done, 1)

            cut_low(0, 0)

            def turn(j):
                for q in range(2):
                    e = 2 * j + q
                    for m in range(NM):
                        n = IC[m][1]
                        wait(dve, gated_done, NM * e + m + 1)
                        wait(dve, h_lo_done, NM * e)
                        dve.tensor_tensor(h[0:n, m], gated[0:n, m % 2], bank[2 * (m % 2) + 1][0:n, :], ALU.mult)\
                           .then_inc(h_done, 1)
                    cut_low(e + 1, 1 - q)
                    for t in range(TT):
                        wait(dve, down_done, TT * e + t + 1)
                        wait(dve, moe_done, TT * e + 1)
                        dve.scalar_tensor_tensor(out=moe[:, t], in0=bank[4 + t][:], scalar=route[:, t, bass.ds(e, 1)],
                                                 in1=moe[:, t], op0=ALU.mult, op1=ALU.add).then_inc(moe_done, 1)

            loop(dve, E // 2, turn)

        @block.scalar
        def _(act):
            def cut_high(e, q):
                wait(act, gu_loaded, 16 * e + 16)
                act.activation(gu_hi[:, q], gu_raw[:], ACT.Copy).then_inc(gu_hi_done, 1)
                wait(act, dn_loaded, 32 * e + 32)
                act.activation(dn_hi[:, q], dn_raw[:], ACT.Copy).then_inc(dn_hi_done, 1)

            cut_high(0, 0)

            def turn(j):
                for q in range(2):
                    e = 2 * j + q
                    for m in range(NM):
                        n = IC[m][1]
                        wait(act, gu_done, NM * e + m + 1)
                        wait(act, h_done, NM * e + max(m - 1, 0))
                        act.activation(gated[0:n, m % 2], bank[2 * (m % 2)][0:n, :], ACT.Silu).then_inc(gated_done, 1)
                        wait(act, h_done, NM * e + m + 1)
                        wait(act, down_done, TT * e)
                        act.activation(h_hi[0:n, m], h[0:n, m], ACT.Copy).then_inc(h_hi_done, 1)
                    cut_high(e + 1, 1 - q)

            loop(act, E // 2, turn)

        @block.tensor
        def _(pe):
            wait(pe, x_loaded, 32)

            def turn(j):
                for q in range(2):
                    e = 2 * j + q
                    wait(pe, gu_hi_done, e + 1)
                    wait(pe, gu_lo_done, e + 1)
                    for m in range(NM):
                        i0, n = IC[m]
                        wait(pe, h_done, NM * e + max(m - 1, 0))
                        for u in range(2):
                            dst = bank[2 * (m % 2) + u][0:n, :]
                            cols = slice(u * I + i0, u * I + i0 + n)
                            for k in range(KC):
                                pe.matmul(dst, gu_hi[:, q, k, cols], x_hi[:, k], start=(k == 0), stop=False)
                                pe.matmul(dst, gu_hi[:, q, k, cols], x_lo[:, k], start=False, stop=False)
                                last = pe.matmul(dst, gu_lo[:, q, k, cols], x_hi[:, k], start=False,
                                                 stop=(k == KC - 1))
                        last.then_inc(gu_done, 1)
                    wait(pe, dn_hi_done, e + 1)
                    wait(pe, dn_lo_done, e + 1)
                    wait(pe, moe_done, TT * e + 1)
                    for m in range(NM):
                        n = IC[m][1]
                        wait(pe, h_hi_done, NM * e + m + 1)
                        wait(pe, h_lo_done, NM * e + m + 1)
                        for t in range(TT):
                            rows = slice(t * P, (t + 1) * P)
                            pe.matmul(bank[4 + t][:], h_hi[0:n, m, rows], dn_hi[0:n, q, m], start=(m == 0), stop=False)
                            pe.matmul(bank[4 + t][:], h_hi[0:n, m, rows], dn_lo[0:n, q, m], start=False, stop=False)
                            last = pe.matmul(bank[4 + t][:], h_lo[0:n, m, rows], dn_hi[0:n, q, m], start=False,
                                             stop=(m == NM - 1))
                            if m == NM - 1:
                                last.then_inc(down_done, 1)

            loop(pe, E // 2, turn)


def heads(nc, bank, ident, pow_half, xT_hi_d, xT_lo_d, alpha_d, beta_d, oT_d, weights, taps, ln_w, ln_b):
    NPROJ = len(weights)
    with ExitStack() as ctx:
        def sb(name, shape, dt=F32):
            return ctx.enter_context(nc.sbuf_tensor(name, shape, dt))

        def sem(name):
            return ctx.enter_context(nc.semaphore(name))

        mask = [sb(f"mask{b}", [P, 2, P]) for b in LEVELS]
        same = sb("same", [P, P])
        sel = sb("sel", [P, G, SB])
        zeros = sb("zeros", [P, C])
        lnw = sb("lnw", [P, 1])
        lnb = sb("lnb", [P, 1])
        x_hi = sb("hx_hi", [P, KC, T], F32R)
        x_lo = sb("hx_lo", [P, KC, T], F32R)
        w_raw = sb("w_raw", [P, NPROJ, KC, D])
        w_hi = sb("w_hi", [P, NPROJ, KC, D], F32R)
        w_lo = sb("w_lo", [P, NPROJ, KC, D], F32R)
        tap_next = sb("tap_next", [P, 3, KS + 1])
        tap = sb("tap", [P, 3, KS + 1])
        y = [[sb(f"y{i}_{j}", [P, KS - 1 + GT]) for j in range(3)] for i in range(3)]
        conv = sb("conv", [P, GT])
        kq = sb("kq", [P, 2, 2, GT])
        vT = sb("vT", [P, GT])
        gT = sb("gT", [P, GROUPS, GT])
        alpha = sb("alpha", [P, 2, GT])
        beta = sb("beta", [P, 2, GT])
        decay = sb("decay", [P, G, 1 + C])
        gamma = sb("gamma", [P, 2, G, 1 + C])
        k_beta = sb("k_beta", [P, GT])
        k_gamma = sb("k_gamma", [P, 2, GT])
        q_gamma = sb("q_gamma", [P, 2, GT])
        LT = sb("LT", [P, 2, G, C])
        diag = sb("diag", [P, G, C])
        Lc = sb("Lc", [P, G, SB])
        Lx = sb("Lx", [P, G, SB, SB])
        Lb = sb("Lb", [P, G, SB, SB])
        prods = sb("prods", [P, G, SB])
        Tc = sb("Tc", [P, G, SB])
        AT = sb("AT", [P, 2, G, C])
        masked = sb("masked", [P, len(LEVELS), G, C])
        TT = sb("TT", [P, 2, G, C])
        Tn = sb("Tn", [P, G, C])
        MT = sb("MT", [P, G, C])
        k_rows = sb("k_rows", [P, 2, G, D])
        v_rows = sb("v_rows", [P, 2, G, D])
        S = sb("S", [P, D])
        R = sb("R", [P, D])
        Wc = sb("Wc", [P, D])
        stats = sb("hstats", [P, G, 6])
        mv = sb("hmv", [P, G, 2])
        veps = sb("hveps", [P, G])
        rstd = sb("hrstd", [P, G])
        on = sb("on", [P, G, D])
        oT = sb("oT", [P, GT])
        oG = sb("oG", [P, GT])

        PJ, IB, TR, CH, OB = bank[0:2], bank[2:4], bank[4], bank[5], bank[6:8]

        built = sem("hbuilt")
        ln_loaded = sem("ln_loaded")
        x_loaded = [sem(f"hx_loaded{g}") for g in range(GROUPS)]
        w_loaded = [sem(f"w_loaded{i}") for i in range(NPROJ)]
        tap_loaded = sem("tap_loaded")
        alpha_loaded = [sem(f"alpha_loaded{i}") for i in range(2)]
        beta_loaded = [sem(f"beta_loaded{i}") for i in range(2)]
        o_stored = sem("o_stored")
        proj_done = sem("proj_done")
        step_done = [sem("step_done_a"), sem("step_done_b")]
        late_done = sem("late_done")
        l_done = sem("l_done")
        spread_done = sem("spread_done")
        chain_done = sem("chain_done")
        k_turned = sem("k_turned")
        v_turned = sem("v_turned")
        o_turned = sem("o_turned")
        y_done = sem("hy_done")
        silu_done = sem("silu_done")
        tanh_done = sem("tanh_done")
        copied = [sem("copied_a"), sem("copied_b")]
        lb_done = sem("lb_done")
        mt32_done = sem("mt32_done")
        tt64_done = sem("tt64_done")
        mt64_done = sem("mt64_done")
        tt128_done = sem("tt128_done")
        tap_done = sem("tap_done")
        gate_done = sem("gate_done")
        w_done = sem("w_done")
        v_done = sem("v_done")
        oT_done = sem("oT_done")
        whi_done = sem("whi_done")
        wlo_done = sem("wlo_done")
        tap_copied = sem("tap_copied")
        decay_done = sem("decay_done")
        gamma_done = sem("gamma_done")
        sel_built = sem("sel_built")
        lt_done = sem("lt_done")
        diag_done = sem("diag_done")
        lc_done = sem("lc_done")
        lx_done = sem("lx_done")
        at_done = sem("at_done")
        tt_done = [sem("tt_done_a"), sem("tt_done_b")]
        tn_done = [sem("tn_done_a"), sem("tn_done_b")]
        tn64_done = sem("tn64_done")
        k_done = sem("k_done")
        r_done = sem("r_done")
        s_done = sem("s_done")
        conv_done = sem("conv_done")
        stats_done = sem("hstats_done")
        mv_done = sem("hmv_done")
        veps_done = sem("hveps_done")
        on_done = sem("on_done")
        mask_done = sem("mask_done")
        solve_done = sem("solve_done")
        t8_done = sem("t8_done")
        kb_done = sem("kb_done")
        kq_gamma_done = sem("kq_gamma_done")
        rstd_done = sem("hrstd_done")
        oG_done = sem("oG_done")
        block = ctx.enter_context(nc.Block())

        def turns(eng, turn):
            turn(eng, -1, 2, False, False, True, False)
            turn(eng, -1, 3, False, True, True, False)
            for g in range(GROUPS):
                turn(eng, 0, g, True, True, True, g > 0)
            with eng.Fori(1, NH - 1) as hh:
                for g in range(GROUPS):
                    turn(eng, hh, g, True, True, True, True)
            for g in range(GROUPS):
                turn(eng, NH - 1, g, True, g < 3, g < 2, True)
            turn(eng, NH, 0, False, False, False, True)

        def counter(hh, g):
            def at(per, d, c=0):
                return hh * (GROUPS * per) + ((g + d) * per + c)
            return at

        def half(c):
            return slice(2 * c, 2 * c + 2)

        def chunk(c):
            return slice(c * C, (c + 1) * C)

        def has_next(hh):
            return not isinstance(hh, int) or 0 <= hh < NH - 1

        def row_loads(hh, g):
            return (hh * (GROUPS // 2)) * 16 + ((g + 2) // 2 + 1) * 16

        @block.sync
        def _(sp):
            def load_x(b, g):
                cols = slice(b * T + g * GT, b * T + (g + 1) * GT)
                sp.dma_start(x_hi[:, :, g * GT:(g + 1) * GT].bitcast(F32), xT_hi_d[:, :, cols]).then_inc(x_loaded[g], 16)
                sp.dma_start(x_lo[:, :, g * GT:(g + 1) * GT].bitcast(F32), xT_lo_d[:, :, cols]).then_inc(x_loaded[g], 16)

            def load_w(i, h):
                sp.dma_start(w_raw[:, i], weights[i][:, bass.ds(h * D, D)].rearrange("(k p) n -> p k n", p=P))\
                  .then_inc(w_loaded[i], 16)

            def load_tap(h):
                sp.dma_start(tap_next[:], taps[bass.ds(h, 1)].rearrange("o p (i j) -> (o p) i j", i=3))\
                  .then_inc(tap_loaded, 16)

            def load_rows(dst, src, hh, g, q, sem):
                rows = src.rearrange("b h t -> (b h) t")[bass.ds(hh, 1), g * GT:(g + 1) * GT]
                sp.dma_start(dst[:, q], rows.to_broadcast([P, GT])).then_inc(sem[q], 16)

            def turn(hh, g, x_next=None, after_next=True, last=False):
                at = counter(hh, g)
                later, q = (hh, 3) if g == 0 else (hh + 1, g - 1), (g + 3) % 2
                if not (last and g > 0):
                    sp.wait_ge(kb_done, at(1, 2))
                    load_rows(beta, beta_d, *later, q, beta_loaded)
                    sp.wait_ge(gamma_done, at(1, 2))
                    load_rows(alpha, alpha_d, *later, q, alpha_loaded)
                if not (isinstance(hh, int) and hh == 0 and g == 0):
                    sp.wait_ge(oG_done, at(1, 0))
                    where, gw = (hh, g - 1) if g > 0 else (hh - 1, 3)
                    sp.dma_start(oT_d[bass.ds(where, 1), :, gw * GT:(gw + 1) * GT].rearrange("o p t -> (o p) t"), oG[:])\
                      .then_inc(o_stored, 16)
                if g == 3 and after_next:
                    h2 = (hh + 2) & (H - 1)
                    h2 = fixed(sp, h2, H - 1)
                    for i in range(NPROJ):
                        sp.wait_ge(wlo_done, hh * NPROJ + (NPROJ + i + 1))
                        load_w(i, h2)
                    sp.wait_ge(tap_copied, hh + 2)
                    load_tap(h2)
                if x_next is not None:
                    sp.wait_ge(proj_done, NPROJ * ((H - 1) * GROUPS + x_next + 1))
                    load_x(1, x_next)

            sp.dma_start(lnw[:], ln_w).then_inc(ln_loaded, 16)
            sp.dma_start(lnb[:], ln_b).then_inc(ln_loaded, 16)
            for i in range(NPROJ):
                load_w(i, 0)
            load_tap(0)
            for g in range(GROUPS):
                load_x(0, g)
            for g in range(2):
                load_rows(beta, beta_d, 0, g, g, beta_loaded)
                load_rows(alpha, alpha_d, 0, g, g, alpha_loaded)
            sp.wait_ge(kb_done, 1)
            load_rows(beta, beta_d, 0, 2, 0, beta_loaded)
            for i in range(NPROJ):
                sp.wait_ge(wlo_done, i + 1)
                load_w(i, 1)
            sp.wait_ge(tap_copied, 1)
            load_tap(1)
            sp.wait_ge(gamma_done, 1)
            load_rows(alpha, alpha_d, 0, 2, 0, alpha_loaded)
            for g in range(GROUPS):
                turn(0, g)
            with sp.Fori(1, H - 2) as hh:
                for g in range(GROUPS):
                    turn(hh, g)
            for g in range(GROUPS):
                turn(H - 2, g, x_next={2: 0, 3: 1}.get(g))
            for g in range(GROUPS):
                turn(H - 1, g, x_next={0: 2, 1: 3}.get(g))
            with sp.Fori(H, NH - 2) as hh:
                for g in range(GROUPS):
                    turn(hh, g)
            for g in range(GROUPS):
                turn(NH - 2, g, after_next=False)
            for g in range(GROUPS):
                turn(NH - 1, g, after_next=False, last=True)
            sp.wait_ge(oG_done, NH * GROUPS)
            sp.dma_start(oT_d[NH - 1, :, 3 * GT:4 * GT], oG[:]).then_inc(o_stored, 16)
            sp.wait_ge(o_stored, 16 * NH * GROUPS)

        @block.gpsimd
        def _(pool):
            n = 0
            for tile in [*mask, zeros]:
                pool.memset(tile[:], 0.0).then_inc(built, 1)
                n += 1
            pool.memset(decay[:, :, 0:1], 0.0).then_inc(built, 1)
            pool.memset(gamma[:, :, :, 0:1], 1.0).then_inc(built, 1)
            for i in range(3):
                pool.memset(y[i][0][:, 0:KS - 1], 0.0).then_inc(built, 1)
            pool.memset(same[:], 1.0).then_inc(built, 1)
            n += 6
            pool.wait_ge(built, n)
            blocks = same[:].rearrange("p (q r) -> p q r", r=SB)
            for base, step, mult in ((0, -SB, 1), (SB - 1, SB, -1)):
                pool.affine_select(out=blocks, in_=blocks, compare_op=ALU.is_ge, fill=0.0, base=base,
                                   pattern=[[step, P // SB], [0, SB]], channel_multiplier=mult).then_inc(built, 1)
                n += 1
                pool.wait_ge(built, n)
            pool.wait_ge(sel_built, G)
            pool.tensor_copy(Tc[:, :, 0:1], sel[:, :, 0:1]).then_inc(built, 1)
            n += 1
            for tile, b in zip(mask, LEVELS):
                part = tile[:].rearrange("p c (q r) -> p c q r", r=2 * b)[:, :, :, b:2 * b]
                pool.memset(part, 1.0).then_inc(built, 1)
                n += 1
                for base, step, mult in ((0, -2 * b, 1), (b - 1, 2 * b, -1)):
                    pool.wait_ge(built, n)
                    for c in range(2):
                        pool.affine_select(out=part[:, c], in_=part[:, c], compare_op=ALU.is_ge, fill=0.0, base=base,
                                           pattern=[[step, P // (2 * b)], [0, b]], channel_multiplier=mult)\
                            .then_inc(built, 1)
                        n += 1
            assert n == BUILT

            def cut_low(i, value):
                pool.wait_ge(whi_done, value)
                pool.tensor_tensor(w_lo[:, i], w_raw[:, i], w_hi[:, i].bitcast(F32), ALU.subtract).then_inc(wlo_done, 1)

            for i in range(NPROJ):
                cut_low(i, i + 1)

            def turn(pool, hh, g, chain, inv, proj, ln):
                at = counter(hh, g)
                for s in range(STEPS):
                    if s in SOLVE_AT and (proj if s > STEPS // 2 else inv):
                        d = 1 if s > STEPS // 2 else 0
                        for i in range(*SOLVE_AT[s]):
                            k = 2 * i
                            if i == 0:
                                pool.wait_ge(lb_done, at(1, 2 + d))
                            wait(pool, solve_done, at(SOLVE_PER, 1 + d, k))
                            pool.tensor_tensor(prods[:, :, i + 1:], Lb[:, :, i + 1:, i],
                                               Tc[:, :, i:i + 1].to_broadcast([P, G, SB - 1 - i]), ALU.mult)\
                                .then_inc(solve_done, 1)
                            if i == 0:
                                wait(pool, t8_done, at(1, 1 + d))
                            pool.wait_ge(solve_done, at(SOLVE_PER, 1 + d, k + 1))
                            pool.tensor_tensor(Tc[:, :, i + 1:], (sel if i == 0 else Tc)[:, :, i + 1:],
                                               prods[:, :, i + 1:], ALU.subtract).then_inc(solve_done, 1)
                    if inv and s == 1:
                        pool.wait_ge(solve_done, at(SOLVE_PER, 2))
                        wait(pool, chain_done, at(12, 0))
                        pool.tensor_tensor(TT[:, (g + 1) % 2].rearrange("p c (q t) -> p c q t", t=SB),
                                           Tc[:].rearrange("p c (o t) -> p c o t", o=1).to_broadcast([P, G, P // SB, SB]),
                                           same[:].rearrange("p (c q t) -> p c q t", c=1, t=SB)
                                           .to_broadcast([P, G, P // SB, SB]), ALU.mult).then_inc(t8_done, 1)
                    if proj and s in MASK_AT:
                        lvl = MASK_AT[s]
                        pool.wait_ge(lt_done, at(1, 3))
                        for c in range(2):
                            wait(pool, step_done[c], at(STEP_PER, 1, 2 * lvl + 2))
                            pool.tensor_tensor(masked[:, lvl, half(c)], LT[:, g % 2, half(c)], mask[lvl][:], ALU.mult)\
                                .then_inc(mask_done, 1)
                    if ln and s == 5:
                        pool.wait_ge(veps_done, at(1, 0))
                        pool.tensor_tensor(rstd[:], veps[:], pow_half[:], ALU.pow).then_inc(rstd_done, 1)
                    if inv and s in (6, 7):
                        i, par = s - 6, (g + 1) % 2
                        if i == 0:
                            pool.wait_ge(gamma_done, at(1, 2))
                            wait(pool, chain_done, at(12, 0))
                        dst = (k_gamma, q_gamma)[i][:, par].rearrange("p (c t) -> p c t", c=G)
                        pool.tensor_tensor(dst, kq[:, par, i].rearrange("p (c t) -> p c t", c=G),
                                           gamma[:, par, :, i:i + C], ALU.mult).then_inc(kq_gamma_done, 1)
                    if proj and s == 10:
                        pool.wait_ge(silu_done, at(3, 2, 1))
                        pool.wait_ge(beta_loaded[g % 2], row_loads(hh, g))
                        wait(pool, k_turned, at(1, 2))
                        pool.tensor_tensor(k_beta[:], kq[:, g % 2, 0], beta[:, g % 2], ALU.mult).then_inc(kb_done, 1)
                    if ln and s == 11:
                        pool.wait_ge(oT_done, at(1, 0))
                        wait(pool, o_stored, at(16, -1))
                        pool.wait_ge(gate_done, at(1, 0))
                        pool.tensor_tensor(oG[:], oT[:], gT[:, (g - 1) % 4], ALU.mult).then_inc(oG_done, 1)
                    if proj and (g == 1 and s in (7, 12, 17) or g == 2 and s == 1) and has_next(hh):
                        i = {7: 0, 12: 1, 17: 2, 1: 3}[s]
                        cut_low(i, hh * NPROJ + (NPROJ + i + 1))

            turns(pool, turn)

        @block.vector
        def _(dve):
            dve.memset(S[:], 0.0).then_inc(s_done, 1)
            for c in range(G):
                dve.tensor_reduce(sel[:, c], ident[:, 0].rearrange("p (q i) -> p i q", i=SB), mybir.AxisListType.X,
                                  ALU.add).then_inc(sel_built, 1)
            dve.wait_ge(built, BUILT)
            dve.wait_ge(tap_loaded, 16)
            dve.tensor_copy(tap[:], tap_next[:]).then_inc(tap_copied, 1)

            def turn(dve, hh, g, chain, inv, proj, ln):
                at = counter(hh, g)
                par, cur = (g + 1) % 2, g % 2
                for s in range(STEPS):
                    if inv and s == A_AT:
                        for c in range(2):
                            dve.wait_ge(step_done[c], at(STEP_PER, 1, 1))
                            if c == 0:
                                dve.wait_ge(decay_done, at(1, 2))
                            wait(dve, chain_done, at(12, 0))
                            dve.tensor_tensor(AT[:, par, half(c)], IB[c][:, 0:2 * C].rearrange("p (c t) -> p c t", c=2),
                                              decay[:, half(c), 1:1 + C], ALU.mult).then_inc(at_done, 1)
                    if g == 2 and s == 0 and proj and has_next(hh):
                        dve.wait_ge(tap_loaded, (hh + 2) * 16)
                        dve.wait_ge(silu_done, at(3, 2))
                        dve.tensor_copy(tap[:], tap_next[:]).then_inc(tap_copied, 1)
                    if ln and s == 2:
                        dve.wait_ge(chain_done, at(12, 0))
                        wait(dve, on_done, at(4, -1))
                        for c in range(G):
                            dve.bn_stats(stats[:, c], OB[(g - 1) % 2][:, chunk(c)]).then_inc(stats_done, 1)
                    if ln and s == 3:
                        dve.wait_ge(stats_done, at(4, 0))
                    if inv and s == 3:
                        dve.wait_ge(k_turned, at(1, 2))
                        dve.tensor_tensor(k_rows[:, par], TR[:].rearrange("p (c d) -> p c d", c=G),
                                          decay[:, :, C:C + 1].to_broadcast([P, G, D]), ALU.mult).then_inc(k_done, 1)
                    if chain and s in CHAIN:
                        k = CHAIN[s]
                        c, r = k // 3, k % 3
                        if r == 0:
                            dve.wait_ge(chain_done, at(12, 0, k + 1))
                            if c == 0:
                                dve.wait_ge(v_done, at(1, 1))
                            dve.scalar_tensor_tensor(out=R[:], in0=CH[:, 0:D], scalar=-S_K, in1=v_rows[:, cur, c],
                                                     op0=ALU.mult, op1=ALU.add).then_inc(r_done, 1)
                        if r == 2:
                            dve.wait_ge(chain_done, at(12, 0, k + 1))
                            dve.wait_ge(s_done, at(4, 0, c + 1))
                            if g == 3 and c == 3:
                                dve.memset(S[:], 0.0).then_inc(s_done, 1)
                            else:
                                dve.scalar_tensor_tensor(out=S[:], in0=S[:], scalar=gamma[:, cur, c, C:C + 1],
                                                         in1=CH[:, 2 * D:3 * D], op0=ALU.mult, op1=ALU.add)\
                                   .then_inc(s_done, 1)
                    if inv and s == T8_AT:
                        dve.wait_ge(t8_done, at(1, 2))
                        wait(dve, late_done, at(LATE_PER, 0, 3))
                        for c in range(2):
                            dve.transpose(Tn[:, half(c)], TT[:, par, half(c)]).then_inc(tn_done[c], 1)
                    if ln and s == 4:
                        for c in range(G):
                            dve.bn_aggr(mv[:, c], stats[:, c]).then_inc(mv_done, 1)
                        dve.wait_ge(mv_done, at(4, 0))
                        dve.tensor_scalar(veps[:], mv[:, :, 1], EPS, None, ALU.add).then_inc(veps_done, 1)
                    if s == 5 and inv:
                        dve.wait_ge(alpha_loaded[par], row_loads(hh, g - 1))
                        wait(dve, s_done, at(4, 0, 1))
                        wait(dve, kq_gamma_done, at(2, 0))
                        for c in range(G):
                            last = dve.tensor_tensor_scan(gamma[:, par, c, 1:1 + C], alpha[:, par, chunk(c)], zeros[:],
                                                          1.0, ALU.mult, ALU.add)
                        last.then_inc(gamma_done, 1)
                    if ln and s == 7:
                        dve.wait_ge(rstd_done, at(1, 0))
                        wait(dve, o_turned, at(1, -1))
                        for c in range(G):
                            dve.tensor_scalar(on[:, c], OB[(g - 1) % 2][:, chunk(c)], mv[:, c, 0:1], rstd[:, c:c + 1],
                                              ALU.subtract, ALU.mult).then_inc(on_done, 1)
                    if inv and s in TT_AT:
                        lvl = TT_AT[s]
                        for c in range(2):
                            dve.wait_ge(step_done[c], at(STEP_PER, 1, 2 * lvl + 3))
                            dve.tensor_tensor(TT[:, par, half(c)], TT[:, par, half(c)],
                                              IB[c][:, 0:2 * C].rearrange("p (c t) -> p c t", c=2), ALU.subtract)\
                               .then_inc(tt_done[c], 1)
                        for c in range(2):
                            dve.wait_ge(tt_done[c], at(len(LEVELS), 1, lvl + 1))
                            dve.transpose(Tn[:, half(c)], TT[:, par, half(c)]).then_inc(tn_done[c], 1)
                    if inv and s == T32_AT:
                        dve.wait_ge(tt64_done, at(2, 1, 1))
                        dve.transpose(Tn[32:64, :, 0:32], TT[0:32, par, :, 32:64]).then_inc(tn64_done, 1)
                    if proj and s in CONV_AT:
                        i, j = CONV_AT[s]
                        if j == 0:
                            dve.wait_ge(tap_done, at(3, 2, i + 1))
                            dve.wait_ge(y_done, at(3, 2, i + 1))
                        else:
                            dve.wait_ge(conv_done, at(9, 2, 3 * i + j))
                        dve.scalar_tensor_tensor(out=conv[:], in0=y[i][Y_AT[(g + 2) % 4]][:, j:j + GT],
                                                 scalar=tap[:, i, j:j + 1], in1=conv[:], op0=ALU.mult, op1=ALU.add)\
                           .then_inc(conv_done, 1)
                    if proj and s == DECAY_AT:
                        dve.wait_ge(alpha_loaded[cur], row_loads(hh, g))
                        wait(dve, k_done, at(1, 2))
                        wait(dve, at_done, at(2, 2))
                        for c in range(G):
                            last = dve.tensor_tensor_scan(decay[:, c, 1:1 + C], alpha[:, cur, chunk(c)], ident[:, 0],
                                                          0.0, ALU.mult, ALU.add)
                        last.then_inc(decay_done, 1)
                    if proj and s == L_AT:
                        dve.wait_ge(l_done, at(1, 3))
                        dve.wait_ge(decay_done, at(1, 3))
                        wait(dve, late_done, at(LATE_PER, 1))
                        dve.scalar_tensor_tensor(out=LT[:, cur], in0=TR[:].rearrange("p (c t) -> p c t", c=G),
                                                 scalar=S_K * S_K, in1=decay[:, :, 0:C], op0=ALU.mult, op1=ALU.mult)\
                           .then_inc(lt_done, 1)
                    if proj and s == L_AT + 1:
                        dve.wait_ge(lt_done, at(1, 3))
                        wait(dve, lc_done, at(1, 2))
                        dve.tensor_tensor(diag[:], LT[:, cur],
                                          same[:].rearrange("p (c t) -> p c t", c=1).to_broadcast([P, G, C]), ALU.mult)\
                           .then_inc(diag_done, 1)
                    if proj and s == L_AT + 2:
                        dve.wait_ge(diag_done, at(1, 3))
                        wait(dve, lx_done, at(1, 2))
                        dve.tensor_reduce(Lc[:], diag[:].rearrange("p c (q t) -> p c t q", t=SB), mybir.AxisListType.X,
                                          ALU.add).then_inc(lc_done, 1)
                    if proj and s == L_AT + 3:
                        dve.wait_ge(lc_done, at(1, 3))
                        wait(dve, spread_done, at(1, 2))
                        dve.tensor_tensor(Lx[:], Lc[:].rearrange("p c (t o) -> p c t o", o=1).to_broadcast([P, G, SB, SB]),
                                          sel[:].rearrange("p c (o i) -> p c o i", o=1).to_broadcast([P, G, SB, SB]),
                                          ALU.mult).then_inc(lx_done, 1)

            turns(dve, turn)

        @block.scalar
        def _(act):
            act.wait_ge(built, BUILT)
            act.wait_ge(ln_loaded, 32)

            def cut_high(i, loads):
                act.wait_ge(w_loaded[i], loads)
                act.activation(w_hi[:, i], w_raw[:, i], ACT.Copy).then_inc(whi_done, 1)

            for i in range(NPROJ):
                cut_high(i, 16)

            def turn(act, hh, g, chain, inv, proj, ln):
                at = counter(hh, g)
                par, cur = (g + 1) % 2, g % 2
                for s in range(STEPS):
                    if s == 0 and inv:
                        act.wait_ge(conv_done, at(9, 2))
                        wait(act, v_turned, at(1, 1))
                        act.activation(vT[:], conv[:], ACT.Silu, bias=tap[:, 2, KS:KS + 1]).then_inc(silu_done, 1)
                        act.wait_ge(proj_done, at(NPROJ, 2))
                        wait(act, oG_done, at(1, -2))
                        act.activation(gT[:, (g + 1) % 4], PJ[1][:], ACT.Tanh, scale=0.5).then_inc(tanh_done, 1)
                    if s == 2 and inv:
                        act.wait_ge(tanh_done, at(1, 2))
                        act.activation(gT[:, (g + 1) % 4], gT[:, (g + 1) % 4], ACT.Copy, scale=0.5, bias=0.5)\
                           .then_inc(gate_done, 1)
                    if inv and s in MT_AT:
                        lvl = MT_AT[s]
                        for c in range(2):
                            act.wait_ge(step_done[c], at(STEP_PER, 1, 2 * lvl + 2))
                            act.activation(MT[:, half(c)], IB[c][:, 0:2 * C].rearrange("p (c t) -> p c t", c=2),
                                           ACT.Copy).then_inc(copied[c], 1)
                    if inv and s in (Y32_AT, T32_AT):
                        k = 0 if s == Y32_AT else 1
                        act.wait_ge(late_done, at(LATE_PER, 1, k + 1))
                        for u in range(0, P, 64):
                            lo, hi = slice(u, u + 32), slice(u + 32, u + 64)
                            w = IB[k][:, 0:GT // 2].rearrange("p (c t) -> p c t", c=G)
                            if k == 0:
                                act.activation(MT[hi, :, lo], w[hi, :, 0:32], ACT.Copy).then_inc(mt32_done, 1)
                            else:
                                act.activation(TT[lo, par, :, hi], w[lo, :, 0:32], ACT.Copy, scale=-1.0)\
                                   .then_inc(tt64_done, 1)
                    if inv and s in (Y64_AT, T64_AT):
                        k = 0 if s == Y64_AT else 1
                        act.wait_ge(late_done, at(LATE_PER, 1, k + 3))
                        w = IB[k][:, 0:GT // 2].rearrange("p (c t) -> p c t", c=G)
                        if k == 0:
                            act.activation(MT[64:128, :, 0:64], w[64:128], ACT.Copy).then_inc(mt64_done, 1)
                        else:
                            act.activation(TT[0:64, par, :, 64:128], w[0:64], ACT.Copy, scale=-1.0)\
                               .then_inc(tt128_done, 1)
                    if chain and s in CHAIN and CHAIN[s] % 3 == 1:
                        k = CHAIN[s]
                        act.wait_ge(chain_done, at(12, 0, k + 1))
                        act.activation(Wc[:], CH[:, D:2 * D], ACT.Copy, scale=S_K).then_inc(w_done, 1)
                    if proj and s == BASE_AT:
                        act.wait_ge(spread_done, at(1, 3))
                        wait(act, t8_done, at(1, 2))
                        act.activation(Lb[:].rearrange("p c t i -> p (c t i)"), TR[:, 0:G * SB * SB], ACT.Copy)\
                           .then_inc(lb_done, 1)
                    if proj and s in (5, 10, 15):
                        i = (5, 10, 15).index(s)
                        ahead = (g + 2) % 4
                        act.wait_ge(proj_done, at(NPROJ, 2, i + 1))
                        if i == 0:
                            act.wait_ge(tap_copied, (hh + 1) + (1 if g >= 2 else 0))
                        wait(act, silu_done, at(3, 2, i))
                        act.activation(conv[:], PJ[i % 2][:], ACT.Copy, scale=tap[:, i, KS - 1:KS]).then_inc(tap_done, 1)
                        wait(act, conv_done, at(9, 1, 3 * i + 3))
                        if ahead < 3:
                            act.activation(y[i][Y_AT[ahead + 1]][:, 0:KS - 1], PJ[i % 2][:, GT - KS + 1:GT], ACT.Copy)
                        act.activation(y[i][Y_AT[ahead]][:, KS - 1:], PJ[i % 2][:], ACT.Copy).then_inc(y_done, 1)
                    if inv and s == 6:
                        act.wait_ge(v_turned, at(1, 2))
                        wait(act, r_done, at(4, -1, 4))
                        act.activation(v_rows[:, par], TR[:].rearrange("p (c d) -> p c d", c=G), ACT.Copy)\
                           .then_inc(v_done, 1)
                    if proj and s in (9, 14):
                        i = (9, 14).index(s)
                        act.wait_ge(conv_done, at(9, 2, 3 * i + 3))
                        wait(act, kq_gamma_done, at(2, 1))
                        act.activation(kq[:, cur, i], conv[:], ACT.Silu, bias=tap[:, i, KS:KS + 1]).then_inc(silu_done, 1)
                    if ln and s == 10:
                        act.wait_ge(o_turned, at(1, 0))
                        wait(act, oG_done, at(1, -1))
                        act.activation(oT[:], TR[:], ACT.Identity, bias=lnb[:, 0:1], scale=lnw[:, 0:1])\
                           .then_inc(oT_done, 1)
                    if proj and (g == 1 and s in (7, 12, 17) or g == 2 and s == 1) and has_next(hh):
                        i = {7: 0, 12: 1, 17: 2, 1: 3}[s]
                        act.wait_ge(proj_done, hh * (GROUPS * NPROJ) + (3 * NPROJ + i + 1))
                        cut_high(i, (hh + 2) * 16)

            turns(act, turn)

        @block.tensor
        def _(pe):
            def turn(pe, hh, g, chain, inv, proj, ln):
                at = counter(hh, g)
                par, cur = (g + 1) % 2, g % 2
                sent = [0]

                def project_some(n):
                    cols = slice((g + 2) % 4 * GT, (g + 2) % 4 * GT + GT)
                    for _ in range(n):
                        i, j = divmod(sent[0], 3 * KC)
                        k, part = divmod(j, 3)
                        sent[0] += 1
                        dst = PJ[i % 2][:]
                        if j == 0:
                            if i == 0:
                                wait(pe, y_done, at(3, 2))
                                pe.wait_ge(x_loaded[(g + 2) % 4], (((hh + (1 if g >= 2 else 0)) >> 4) + 1) * 32)
                            if i == 1:
                                wait(pe, tanh_done, at(1, 2))
                            if i >= 2:
                                pe.wait_ge(y_done, at(3, 2, i - 1))
                            pe.wait_ge(wlo_done, (hh + (1 if g >= 2 else 0)) * NPROJ + (i + 1))
                        a, b = ((w_hi, x_hi), (w_hi, x_lo), (w_lo, x_hi))[part]
                        last = pe.matmul(dst, a[:, i, k], b[:, k, cols], start=(j == 0), stop=(j == 3 * KC - 1))
                        if j == 3 * KC - 1:
                            last.then_inc(proj_done, 1)

                def step(c, s):
                    w = IB[c]
                    if s == A_AT:
                        pe.wait_ge(kb_done, at(1, 2))
                        pe.wait_ge(silu_done, at(3, 1, 2))
                        wait(pe, tt128_done, at(1, 1))
                        for j in range(2):
                            n = 2 * c + j
                            last = pe.matmul(w[:, chunk(j)], k_beta[:, chunk(n)], kq[:, par, 1, chunk(n)],
                                             start=True, stop=True)
                    elif s in MT_AT:
                        lvl = MT_AT[s]
                        pe.wait_ge(mask_done, at(2 * len(LEVELS), 1, 2 * lvl + c + 1))
                        pe.wait_ge(tn_done[c], at(len(LEVELS) + 1, 1, lvl + 1))
                        if lvl == 0:
                            pe.wait_ge(at_done, at(2, 1, c + 1))
                        for j in range(2):
                            last = pe.matmul(w[:, chunk(j)], masked[:, lvl, 2 * c + j], Tn[:, 2 * c + j],
                                             start=True, stop=True)
                    elif s in TT_AT:
                        lvl = TT_AT[s]
                        pe.wait_ge(copied[c], at(len(LEVELS), 1, lvl + 1))
                        for j in range(2):
                            last = pe.matmul(w[:, chunk(j)], MT[:, 2 * c + j], TT[:, par, 2 * c + j],
                                             start=True, stop=True)
                    else:
                        return
                    last.then_inc(step_done[c], 1)

                def late_waits(s):
                    if s == Y32_AT:
                        for c in range(2):
                            pe.wait_ge(tn_done[c], at(len(LEVELS) + 1, 2))
                    if s == T32_AT:
                        pe.wait_ge(mt32_done, at(2, 2))
                    if s == Y64_AT:
                        pe.wait_ge(tt64_done, at(2, 2))
                        pe.wait_ge(tn64_done, at(1, 2))
                    if s == T64_AT:
                        pe.wait_ge(mt64_done, at(1, 2))

                def late(s):
                    b = 32 if s in (Y32_AT, T32_AT) else 64
                    first = s in (Y32_AT, Y64_AT)
                    for c in range(G):
                        for u in range(0, P, 2 * b):
                            lo, hi = slice(u, u + b), slice(u + b, u + 2 * b)
                            cols = slice(c * 64, c * 64 + b)
                            if first:
                                last = pe.matmul(IB[0][hi, cols], LT[lo, par, c, hi], Tn[lo, c, lo], start=True, stop=True)
                            else:
                                last = pe.matmul(IB[1][lo, cols], MT[hi, c, lo], TT[hi, par, c, hi], start=True, stop=True)
                    last.then_inc(late_done, 1)

                def chain_step(k):
                    c, r = divmod(k, 3)
                    o = OB[cur][:, chunk(c)]
                    if r == 0:
                        pe.wait_ge(s_done, at(4, 0, c + 1))
                        if c == 0:
                            pe.wait_ge(kq_gamma_done, at(2, 1))
                            wait(pe, on_done, at(4, -1))
                        pe.matmul(o, q_gamma[:, cur, chunk(c)], S[:], start=True, stop=False)
                        pe.matmul(CH[:, 0:D], k_gamma[:, cur, chunk(c)], S[:], start=True, stop=True)\
                          .then_inc(chain_done, 1)
                    if r == 1:
                        pe.wait_ge(r_done, at(4, 0, c + 1))
                        if c == 0:
                            pe.wait_ge(tt128_done, at(1, 1))
                        pe.matmul(CH[:, D:2 * D], TT[:, cur, c], R[:], start=True, stop=True).then_inc(chain_done, 1)
                    if r == 2:
                        pe.wait_ge(w_done, at(4, 0, c + 1))
                        if c == 0:
                            pe.wait_ge(k_done, at(1, 1))
                            pe.wait_ge(at_done, at(2, 1))
                        pe.matmul(o, AT[:, cur, c], Wc[:], start=False, stop=True)
                        pe.matmul(CH[:, 2 * D:3 * D], k_rows[:, cur, c], Wc[:], start=True, stop=True)\
                          .then_inc(chain_done, 1)

                for s in range(STEPS):
                    if inv:
                        step(0, s)
                    by_blocks = inv and s in (Y32_AT, T32_AT, Y64_AT, T64_AT)
                    if by_blocks:
                        late_waits(s)
                    if proj:
                        project_some(1)
                    if by_blocks:
                        late(s)
                    if proj:
                        project_some(PIECES[2 * s] - 1)
                    if chain and s in CHAIN:
                        chain_step(CHAIN[s])
                    if inv:
                        step(1, s)
                    if proj:
                        project_some(PIECES[2 * s + 1])
                    if inv and s == 0:
                        pe.wait_ge(lb_done, at(1, 2))
                        for c in range(G):
                            last = pe.transpose(TR[:, chunk(c)], k_beta[:, chunk(c)], ident[:, 0])
                        last.then_inc(k_turned, 1)
                    if inv and s == 5:
                        pe.wait_ge(silu_done, at(3, 2))
                        pe.wait_ge(k_done, at(1, 2))
                        for c in range(G):
                            last = pe.transpose(TR[:, chunk(c)], vT[:, chunk(c)], ident[:, 0])
                        last.then_inc(v_turned, 1)
                    if ln and s == 9:
                        pe.wait_ge(on_done, at(4, 0))
                        if inv:
                            pe.wait_ge(v_done, at(1, 2))
                        for c in range(G):
                            last = pe.transpose(TR[:, chunk(c)], on[:, c], ident[:, 0])
                        last.then_inc(o_turned, 1)
                    if proj and s == L_AT:
                        pe.wait_ge(kb_done, at(1, 3))
                        if ln:
                            pe.wait_ge(oT_done, at(1, 0))
                        elif inv:
                            pe.wait_ge(v_done, at(1, 2))
                        for c in range(G):
                            last = pe.matmul(TR[:, chunk(c)], k_beta[:, chunk(c)], kq[:, cur, 0, chunk(c)],
                                             start=True, stop=True)
                        last.then_inc(l_done, 1)
                    if proj and s == BASE_AT:
                        pe.wait_ge(lx_done, at(1, 3))
                        pe.matmul(TR[:, 0:G * SB * SB], same[:], Lx[:].rearrange("p c t i -> p (c t i)"),
                                  start=True, stop=True).then_inc(spread_done, 1)

            turns(pe, turn)


def project(nc, bank, moe, x_rows, oT_d, Wo, out_rows):
    HQ = 4
    with ExitStack() as ctx:
        def sb(name, shape, dt=F32):
            return ctx.enter_context(nc.sbuf_tensor(name, shape, dt))

        def sem(name):
            return ctx.enter_context(nc.semaphore(name))

        wo_raw = sb("wo_raw", [P, H, HID])
        wo_hi = sb("wo_hi", [P, H, HID], F32R)
        wo_lo = sb("wo_lo", [P, H, HID], F32R)
        o_raw = sb("o_raw", [P, 2, H, P])
        o_hi = sb("o_hi", [P, 2, H, P], F32R)
        o_lo = sb("o_lo", [P, 2, H, P], F32R)
        x_t = sb("x_t", [P, 2, HID])
        y = sb("y", [P, 2, HID])
        wo_loaded = [sem(f"wo_loaded{k}") for k in range(H // HQ)]
        wo_hi_done = sem("wo_hi_done")
        wo_lo_done = sem("wo_lo_done")
        o_loaded = [sem(f"o_loaded{q}") for q in range(2)]
        x_loaded = [sem(f"xr_loaded{q}") for q in range(2)]
        o_hi_done = sem("o_hi_done")
        o_lo_done = sem("o_lo_done")
        tile_done = sem("tile_done")
        x_moe_done = sem("x_moe_done")
        y_done = sem("y_done")
        y_stored = [sem(f"y_stored{q}") for q in range(2)]
        oT = oT_d.rearrange("(b h) p t -> b p h t", b=B)
        PAIRS = NT // P // 2
        MOE_PAIRS = GT // P // 2
        block = ctx.enter_context(nc.Block())

        @block.sync
        def _(sp):
            def load_o(b, i, q):
                sp.dma_start(o_raw[:, q], oT[bass.ds(b, 1), :, :, bass.ds(i * (2 * P) + q * P, P)]
                             .rearrange("o p h t -> (o p) h t")).then_inc(o_loaded[q], 16)

            load_o(0, 0, 0)
            wo_rows = Wo.rearrange("(h p) n -> p h n", p=P)
            for k in range(H // HQ):
                sp.dma_start(wo_raw[:, k * HQ:(k + 1) * HQ], wo_rows[:, k * HQ:(k + 1) * HQ]).then_inc(wo_loaded[k], 16)

            def turn(b, i, begun=False):
                j = b * (PAIRS // B) + i
                for q in range(2):
                    if not (begun and q == 0):
                        wait(sp, o_lo_done, 2 * j + q - 1)
                        load_o(b, i, q)
                    wait(sp, y_done, 2 * j + q - 1)
                    sp.dma_start(x_t[:, q], x_rows[bass.ds(j * (2 * P) + q * P, P), :]).then_inc(x_loaded[q], 16)

            turn(0, 0, begun=True)
            with sp.Fori(1, PAIRS // B) as i:
                turn(0, i)
            with sp.Fori(0, PAIRS // B) as i:
                turn(1, i)

        @block.gpsimd
        def _(pool):
            def turn(j):
                for q in range(2):
                    wait(pool, y_done, 2 * j + q + 1)
                    pool.dma_start(out_rows[bass.ds(j * (2 * P) + q * P, P), :], y[:, q]).then_inc(y_stored[q], 16)

            loop(pool, PAIRS, turn)
            for q in range(2):
                wait(pool, y_stored[q], 16 * PAIRS)

        @block.scalar
        def _(act):
            wait(act, o_loaded[0], 16)
            act.activation(o_hi[:, 0], o_raw[:, 0], ACT.Copy).then_inc(o_hi_done, 1)
            for i in range(0, H, HQ):
                act.wait_ge(wo_loaded[i // HQ], 16)
                act.activation(wo_hi[:, i:i + HQ], wo_raw[:, i:i + HQ], ACT.Copy).then_inc(wo_hi_done, 1)

            def turn(j, skip=0):
                for q in range(skip, 2):
                    wait(act, o_loaded[q], 16 * j + 16)
                    wait(act, tile_done, 2 * j + q - 1)
                    act.activation(o_hi[:, q], o_raw[:, q], ACT.Copy).then_inc(o_hi_done, 1)

            turn(0, skip=1)
            with act.Fori(1, PAIRS) as j:
                turn(j)

        @block.vector
        def _(dve):
            def cut(j, q):
                wait(dve, o_hi_done, 2 * j + q + 1)
                wait(dve, tile_done, 2 * j + q - 1)
                dve.tensor_tensor(o_lo[:, q], o_raw[:, q], o_hi[:, q].bitcast(F32), ALU.subtract)\
                   .then_inc(o_lo_done, 1)

            def finish(j, q):
                wait(dve, x_loaded[q], 16 * j + 16)
                if isinstance(j, int) and j < MOE_PAIRS:
                    dve.tensor_tensor(x_t[:, q], x_t[:, q], moe[:, 2 * j + q], ALU.add).then_inc(x_moe_done, 1)
                    wait(dve, x_moe_done, 2 * j + q + 1)
                wait(dve, tile_done, 2 * j + q + 1)
                wait(dve, y_stored[q], 16 * j)
                dve.tensor_tensor(y[:, q], bank[q][:], x_t[:, q], ALU.add).then_inc(y_done, 1)

            def turn(j, last=False):
                cut(j, 1)
                finish(j, 0)
                if not last:
                    cut(j + 1, 0)
                finish(j, 1)

            cut(0, 0)
            for i in range(0, H, HQ):
                wait(dve, wo_hi_done, i // HQ + 1)
                dve.tensor_tensor(wo_lo[:, i:i + HQ], wo_raw[:, i:i + HQ], wo_hi[:, i:i + HQ].bitcast(F32),
                                  ALU.subtract).then_inc(wo_lo_done, 1)
            for j in range(MOE_PAIRS):
                turn(j)
            with dve.Fori(MOE_PAIRS, PAIRS - 1) as j:
                turn(j)
            turn(PAIRS - 1, last=True)

        @block.tensor
        def _(pe):
            def turn(j):
                for q in range(2):
                    wait(pe, o_hi_done, 2 * j + q + 1)
                    wait(pe, o_lo_done, 2 * j + q + 1)
                    wait(pe, y_done, 2 * j + q - 1)
                    for i in range(H):
                        if isinstance(j, int) and j == 0 and q == 0 and i % HQ == 0:
                            pe.wait_ge(wo_lo_done, i // HQ + 1)
                        pe.matmul(bank[q][:], o_hi[:, q, i], wo_hi[:, i], start=(i == 0), stop=False)
                        pe.matmul(bank[q][:], o_hi[:, q, i], wo_lo[:, i], start=False, stop=False)
                        last = pe.matmul(bank[q][:], o_lo[:, q, i], wo_hi[:, i], start=False, stop=(i == H - 1))
                    last.then_inc(tile_done, 1)

            loop(pe, PAIRS, turn)


def kernel(**inputs):
    import numpy as np
    import concourse.bacc as bacc
    from concourse import mybir as _mybir
    from concourse.bass_utils import run_bass_kernel_spmd

    a = {n.removeprefix("L0_"): np.asarray(v) for n, v in inputs.items()}
    heads_last = lambda v: v.reshape(H, D, -1)
    laid = {
        "x": a["attn_x"], "Wq": a["attn_Wq"], "Wk": a["attn_Wk"], "Wv": a["attn_Wv"],
        "Wab": np.concatenate([a["attn_Wa"], a["attn_Wb"]], axis=1),
        "bab": np.concatenate([a["attn_ba"], a["attn_bb"]])[:, None],
        "Wg": a["attn_Wg"], "Wo": a["attn_Wo"],
        "taps": np.concatenate([np.concatenate([heads_last(a[f"attn_{n}cw"]), heads_last(a[f"attn_{n}cb"])], axis=2)
                                for n in "kqv"], axis=2),
        "ln_w": a["attn_ln_w"][:, None], "ln_b": a["attn_ln_b"][:, None],
        "topk_idx": a["ffn_topk_idx"].reshape(-1, TOPK), "topk_weight": a["ffn_topk_weight"].reshape(-1, TOPK),
        "gate_up": np.concatenate([a["ffn_gate_weight"].transpose(0, 2, 1), a["ffn_up_weight"].transpose(0, 2, 1)], axis=2),
        "down": a["ffn_down_weight"].transpose(0, 2, 1),
    }
    nc = bacc.Bacc("TRN2", target_bir_lowering=False, num_devices=1)
    arrays, args = {}, {}
    for name, v in laid.items():
        v = np.ascontiguousarray(v)
        arrays[f"in_{name}"] = v
        args[name] = nc.dram_tensor(f"in_{name}", v.shape, _mybir.dt.from_np(v.dtype), kind="ExternalInput").ap()
    args["out"] = nc.dram_tensor("out_0", laid["x"].shape, F32, kind="ExternalOutput").ap()
    program(nc, **args)
    r = run_bass_kernel_spmd(nc, [arrays], core_ids=[0])
    return r.results[0]["out_0"]
```

```python
from contextlib import ExitStack

import concourse.bass as bass
import concourse.mybir as mybir

F32 = mybir.dt.float32
F32R = mybir.dt.float32r
I32 = mybir.dt.int32
ALU = mybir.AluOpType
ACT = mybir.ActivationFunctionType

P = 128
B, T, HID = 2, 2048, 512
H, D = 16, 128
KS = 4
NT = B * T
KC = HID // P
C = 128
G = 4
GT = G * C
GROUPS = T // GT
NG = NT // GT
NH = B * H
E, I, TOPK = 16, 352, 4
IC = [(0, 128), (128, 128), (256, 96)]
S_K = float(D) ** -0.5
EPS = 1e-5

SB = 8
LEVELS = [8, 16]
STEPS = 19
CHAIN = {1: 0, 2: 1, 4: 2, 5: 3, 7: 4, 8: 5, 10: 6, 11: 7, 13: 8, 14: 9, 16: 10, 17: 11}
PIECES = [len(range(-(-48 * i // (2 * STEPS)), -(-48 * (i + 1) // (2 * STEPS)))) for i in range(2 * STEPS)]
A_AT, T8_AT = 0, 4
SOLVE_AT = {17: (0, 2), 18: (2, 4), 0: (4, 6), 1: (6, 7)}
MT_AT = {6: 0, 9: 1}
TT_AT = {7: 0, 10: 1}
Y32_AT, T32_AT, Y64_AT, T64_AT = 13, 14, 16, 17
L_AT, BASE_AT, DECAY_AT = 12, 16, 8
MASK_AT = {14: 0, 15: 1}
STEP_PER = 1 + 2 * len(LEVELS)
LATE_PER = 4
SOLVE_PER = 2 * (SB - 1)
Y_AT = [0, 1, 2, 1]
BUILT = 12 + 5 * len(LEVELS)
CONV_AT = {6: (0, 0), 7: (0, 1), 8: (0, 2), 11: (1, 0), 12: (1, 1), 13: (1, 2), 16: (2, 0), 17: (2, 1), 18: (2, 2)}


def wait(eng, sem, value):
    if isinstance(value, int) and value <= 0:
        return
    eng.wait_ge(sem, value)


def fixed(eng, value, most):
    return value if isinstance(value, int) else eng.snap(eng.to_reg(value), max_val=most)


def loop(eng, n, turn):
    turn(0)
    with eng.Fori(1, n) as i:
        turn(i)


def program(nc, x, Wq, Wk, Wv, Wab, bab, Wg, Wo, taps, ln_w, ln_b, topk_idx, topk_weight, gate_up, down, out):
    with ExitStack() as ctx:
        def sb(name, shape, dt=F32):
            return ctx.enter_context(nc.sbuf_tensor(name, shape, dt))

        xT_hi_d = nc.dram_tensor("xT_hi_d", (NG, P, KC, GT), F32, kind="Internal").ap()
        xT_lo_d = nc.dram_tensor("xT_lo_d", (NG, P, KC, GT), F32, kind="Internal").ap()
        alpha_d = nc.dram_tensor("alpha_d", (NG, H, GT), F32, kind="Internal").ap()
        beta_d = nc.dram_tensor("beta_d", (NG, H, GT), F32, kind="Internal").ap()
        oT_d = nc.dram_tensor("oT_d", (NH, P, T), F32, kind="Internal").ap()
        x_rows = x.rearrange("b t n -> (b t) n")
        out_rows = out.rearrange("b t n -> (b t) n")

        ident = sb("ident", [P, 2, P])
        pow_half = sb("pow_half", [P, G])
        moe = sb("moe", [P, GT // P, HID])
        bank = [ctx.enter_context(nc.psum_tensor(f"bank{i}", [P, 512], F32)) for i in range(8)]

        inputs = (x_rows, Wab, bab, topk_idx, topk_weight, gate_up, down)
        prepare(nc, bank, ident, pow_half, moe, inputs, (xT_hi_d, xT_lo_d), (alpha_d, beta_d))
        heads(nc, bank, ident, pow_half, xT_hi_d, xT_lo_d, alpha_d, beta_d, oT_d, (Wk, Wq, Wv, Wg), taps, ln_w, ln_b)
        project(nc, bank, moe, x_rows, oT_d, Wo, out_rows)


def prepare(nc, bank, ident, pow_half, moe, inputs, xT_d, gates_d):
    x_rows, Wab, bab, topk_idx, topk_weight, gate_up, down = inputs
    xT_hi_d, xT_lo_d = xT_d
    DOWN, PREP = (bank[4], bank[5], bank[2], bank[3]), bank[6:8]
    NM = len(IC)
    TT = GT // P
    with ExitStack() as ctx:
        def sb(name, shape, dt=F32):
            return ctx.enter_context(nc.sbuf_tensor(name, shape, dt))

        def sem(name):
            return ctx.enter_context(nc.semaphore(name))

        x_hi = sb("x_hi", [P, KC, GT], F32R)
        x_lo = sb("x_lo", [P, KC, GT], F32R)
        gu_raw = sb("gu_raw", [P, KC, 2 * I])
        dn_raw = sb("dn_raw", [P, NM, HID])
        gu_hi = sb("gu_hi", [P, 2, KC, 2 * I], F32R)
        gu_lo = sb("gu_lo", [P, 2, KC, 2 * I], F32R)
        dn_hi = sb("dn_hi", [P, 2, NM, HID], F32R)
        dn_lo = sb("dn_lo", [P, 2, NM, HID], F32R)
        gated = sb("gated", [P, 2, GT])
        h = sb("h", [P, NM, GT])
        h_hi = sb("h_hi", [P, NM, GT], F32R)
        h_lo = sb("h_lo", [P, NM, GT], F32R)
        idx = sb("idx", [P, TT, TOPK], I32)
        idx_f = sb("idx_f", [P, TT, TOPK])
        top_w = sb("top_w", [P, TT, TOPK])
        number = sb("number", [P, E])
        share = sb("share", [P, TT, TOPK, E])
        route = sb("route", [P, TT, E])
        x_in = sb("x_in", [P, TT, HID])
        stats = sb("stats", [P, TT, 6])
        mv = sb("mv", [P, TT, 2])
        veps = sb("veps", [P, TT])
        rstd = sb("rstd", [P, TT])
        xn = sb("xn", [P, TT, HID])
        xT = sb("xT", [P, KC, GT])
        xT_hi = sb("xT_hi", [P, KC, GT], F32R)
        xT_lo = sb("xT_lo", [P, KC, GT], F32R)
        wab = sb("wab", [P, KC, 2 * H])
        bab_s = sb("bab_s", [2 * H, 1])
        ab = sb("ab", [2 * H, GT])
        const_built = sem("const_built")
        small_loaded = sem("small_loaded")
        x_loaded = sem("x_loaded")
        stats_done = sem("stats_done")
        mv_done = sem("mv_done")
        veps_done = sem("veps_done")
        rstd_done = sem("rstd_done")
        xn_done = sem("xn_done")
        turned = sem("turned")
        hi_done = sem("hi_done")
        lo_done = sem("lo_done")
        z_done = sem("z_done")
        ab_done = sem("ab_done")
        xT_stored = sem("xT_stored")
        ab_stored = sem("ab_stored")
        top_loaded = sem("top_loaded")
        gu_loaded = sem("gu_loaded")
        dn_loaded = sem("dn_loaded")
        number_built = sem("number_built")
        dn_cleared = sem("dn_cleared")
        idx_done = sem("idx_done")
        share_done = sem("share_done")
        route_done = sem("route_done")
        gu_hi_done = sem("gu_hi_done")
        gu_lo_done = sem("gu_lo_done")
        dn_hi_done = sem("dn_hi_done")
        dn_lo_done = sem("dn_lo_done")
        gu_done = sem("gu_done")
        gated_done = sem("gated_done")
        h_done = sem("h_done")
        h_hi_done = sem("h_hi_done")
        h_lo_done = sem("h_lo_done")
        down_done = sem("down_done")
        moe_done = sem("moe_done")

        def parts(g):
            return (x_hi, x_lo) if isinstance(g, int) and g == 0 else (xT_hi, xT_lo)

        block = ctx.enter_context(nc.Block())

        @block.sync
        def _(sp):
            def load_x(g):
                sp.dma_start(x_in[:], x_rows[bass.ds(g * GT, GT), :].rearrange("(i p) n -> p i n", p=P))\
                  .then_inc(x_loaded, 16)

            def load_expert(i):
                e = fixed(sp, i & (E - 1), E - 1)
                wait(sp, gu_lo_done, i)
                sp.dma_start(gu_raw[:], gate_up[bass.ds(e, 1)].rearrange("o (k p) n -> p (o k) n", p=P))\
                  .then_inc(gu_loaded, 16)
                wait(sp, dn_lo_done, i)
                sp.dma_start(dn_raw[:, 0:2], down[bass.ds(e, 1), 0:2 * P].rearrange("o (k p) n -> p (o k) n", p=P))\
                  .then_inc(dn_loaded, 16)
                sp.dma_start(dn_raw[0:I - 2 * P, 2], down[bass.ds(e, 1), 2 * P:I].rearrange("o p n -> (o p) n"))\
                  .then_inc(dn_loaded, 16)

            def store(g):
                hi, lo = parts(g)
                wait(sp, hi_done, g * TT + TT)
                sp.dma_start(xT_hi_d[bass.ds(g, 1)].rearrange("o p k t -> (o p) k t"), hi[:].bitcast(F32))\
                  .then_inc(xT_stored, 16)
                wait(sp, ab_done, g + 1)
                wait(sp, lo_done, g * TT + TT)
                sp.dma_start(xT_lo_d[bass.ds(g, 1)].rearrange("o p k t -> (o p) k t"), lo[:].bitcast(F32))\
                  .then_inc(xT_stored, 16)
                for part, dst in enumerate(gates_d):
                    sp.dma_start(dst[bass.ds(g, 1)].rearrange("o h t -> (o h) t"), ab[part * H:(part + 1) * H, :])\
                      .then_inc(ab_stored, 16)

            load_x(0)
            sp.dma_start(wab[:], Wab.rearrange("(k p) n -> p k n", p=P)).then_inc(small_loaded, 16)
            sp.dma_start(bab_s[:], bab).then_inc(small_loaded, 16)
            wait(sp, dn_cleared, 1)
            load_expert(0)
            sp.dma_start(idx[:], topk_idx.rearrange("(t p) k -> p t k", p=P)).then_inc(top_loaded, 16)
            sp.dma_start(top_w[:], topk_weight.rearrange("(t p) k -> p t k", p=P)).then_inc(top_loaded, 16)
            store(0)
            load_expert(1)
            load_expert(2)
            with sp.Fori(1, E // 2) as j:
                wait(sp, xn_done, j * TT)
                load_expert(2 * j + 1)
                load_x(j)
                load_expert(2 * j + 2)
                store(j)
            wait(sp, xT_stored, NG * 32)
            wait(sp, ab_stored, NG * 32)

        @block.gpsimd
        def _(pool):
            pool.memset(dn_raw[:, 2], 0.0).then_inc(dn_cleared, 1)
            pool.memset(ident[:], 0.0).then_inc(const_built, 1)
            pool.memset(pow_half[:], -0.5).then_inc(const_built, 1)
            wait(pool, const_built, 2)
            for c in range(2):
                pool.affine_select(out=ident[:, c], in_=ident[:, c], compare_op=ALU.not_equal, fill=1.0, base=0,
                                   pattern=[[-1, P]], channel_multiplier=1).then_inc(const_built, 1)
            pool.iota(number[:], pattern=[[1, E]], base=0, channel_multiplier=0,
                      allow_small_or_imprecise_dtypes=True).then_inc(number_built, 1)

            def cut_low(e, q):
                wait(pool, dn_hi_done, e + 1)
                pool.tensor_tensor(dn_lo[:, q], dn_raw[:], dn_hi[:, q].bitcast(F32), ALU.subtract)\
                    .then_inc(dn_lo_done, 1)

            def deviation(g):
                wait(pool, veps_done, 2 * g + 2)
                pool.tensor_tensor(rstd[:], veps[:], pow_half[:], ALU.pow).then_inc(rstd_done, 1)

            def low(g, tiles):
                hi, lo = parts(g)
                for i in tiles:
                    cols = slice(i * P, (i + 1) * P)
                    wait(pool, hi_done, g * TT + i + 1)
                    if i == 0:
                        wait(pool, xT_stored, g * 32)
                    pool.tensor_tensor(lo[:, :, cols], xT[:, :, cols], hi[:, :, cols].bitcast(F32),
                                       ALU.subtract).then_inc(lo_done, 1)

            deviation(0)
            low(0, range(TT))
            cut_low(0, 0)

            def turn(j, group=True):
                for q in range(2):
                    e = 2 * j + q
                    for m in range(NM):
                        n = IC[m][1]
                        wait(pool, h_hi_done, NM * e + m + 1)
                        pool.tensor_tensor(h_lo[0:n, m], h[0:n, m], h_hi[0:n, m].bitcast(F32), ALU.subtract)\
                            .then_inc(h_lo_done, 1)
                    cut_low(e + 1, 1 - q)
                    if group and q == 0:
                        deviation(j)
                    if group and q == 1:
                        low(j, range(TT))

            turn(0, group=False)
            with pool.Fori(1, E // 2) as j:
                turn(j)

        @block.vector
        def _(dve):
            def statistics(g):
                last = TT - 1
                for i in range(TT):
                    if i == 0:
                        wait(dve, x_loaded, g * 16 + 16)
                    else:
                        wait(dve, stats_done, g * TT + i)
                    dve.bn_stats(stats[:, i], x_in[:, i]).then_inc(stats_done, 1)
                    if i:
                        dve.bn_aggr(mv[:, i - 1], stats[:, i - 1]).then_inc(mv_done, 1)
                wait(dve, stats_done, g * TT + TT)
                wait(dve, mv_done, g * TT + last)
                dve.tensor_scalar(veps[:, 0:last], mv[:, 0:last, 1], EPS, None, ALU.add).then_inc(veps_done, 1)
                dve.bn_aggr(mv[:, last], stats[:, last]).then_inc(mv_done, 1)
                wait(dve, mv_done, g * TT + TT)
                dve.tensor_scalar(veps[:, last:], mv[:, last:, 1], EPS, None, ALU.add).then_inc(veps_done, 1)

            def normalise(g):
                wait(dve, rstd_done, g + 1)
                wait(dve, turned, g * TT)
                for i in range(TT):
                    dve.tensor_scalar(xn[:, i], x_in[:, i], mv[:, i, 0:1], rstd[:, i:i + 1],
                                      ALU.subtract, ALU.mult).then_inc(xn_done, 1)

            statistics(0)
            normalise(0)
            dve.memset(moe[:], 0.0).then_inc(moe_done, 1)
            wait(dve, top_loaded, 32)
            wait(dve, number_built, 1)
            dve.tensor_copy(idx_f[:], idx[:]).then_inc(idx_done, 1)
            wait(dve, idx_done, 1)
            for t in range(TT):
                for k in range(TOPK):
                    dve.tensor_scalar(share[:, t, k], number[:], idx_f[:, t, k:k + 1], top_w[:, t, k:k + 1],
                                      ALU.is_equal, ALU.mult).then_inc(share_done, 1)
            wait(dve, share_done, TT * TOPK)
            dve.tensor_reduce(route[:], share[:].rearrange("p t k e -> p t e k"), mybir.AxisListType.X, ALU.add)\
                .then_inc(route_done, 1)
            wait(dve, route_done, 1)

            def cut_low(e, q):
                wait(dve, gu_hi_done, e + 1)
                dve.tensor_tensor(gu_lo[:, q], gu_raw[:], gu_hi[:, q].bitcast(F32), ALU.subtract)\
                   .then_inc(gu_lo_done, 1)

            cut_low(0, 0)

            def turn(j, group=True):
                for q in range(2):
                    e = 2 * j + q
                    for m in range(NM):
                        n = IC[m][1]
                        wait(dve, gated_done, NM * e + m + 1)
                        wait(dve, h_lo_done, NM * e)
                        dve.tensor_tensor(h[0:n, m], gated[0:n, m % 2], bank[2 * (m % 2) + 1][0:n, :], ALU.mult)\
                           .then_inc(h_done, 1)
                    cut_low(e + 1, 1 - q)
                    if group and q == 0:
                        statistics(j)
                    for t in range(TT):
                        wait(dve, down_done, TT * e + t + 1)
                        wait(dve, moe_done, TT * e + 1)
                        dve.scalar_tensor_tensor(out=moe[:, t], in0=DOWN[t][:], scalar=route[:, t, bass.ds(e, 1)],
                                                 in1=moe[:, t], op0=ALU.mult, op1=ALU.add).then_inc(moe_done, 1)
                    if group and q == 0:
                        normalise(j)

            turn(0, group=False)
            with dve.Fori(1, E // 2) as j:
                turn(j)

        @block.scalar
        def _(act):
            def cut_high(e, q):
                wait(act, gu_loaded, 16 * e + 16)
                act.activation(gu_hi[:, q], gu_raw[:], ACT.Copy).then_inc(gu_hi_done, 1)
                wait(act, dn_loaded, 32 * e + 32)
                act.activation(dn_hi[:, q], dn_raw[:], ACT.Copy).then_inc(dn_hi_done, 1)

            def take(g, tiles):
                for i in tiles:
                    if i == 0:
                        wait(act, xT_stored, g * 32)
                        wait(act, lo_done, g * TT)
                        wait(act, z_done, g)
                    cols = slice(i * P, (i + 1) * P)
                    tile = PREP[i % 2][:, :].rearrange("p (k n) -> p k n", k=KC)
                    wait(act, turned, g * TT + i + 1)
                    act.activation(xT[:, :, cols], tile, ACT.Copy)
                    act.activation(parts(g)[0][:, :, cols], tile, ACT.Copy).then_inc(hi_done, 1)

            def gates(g):
                wait(act, z_done, g + 1)
                wait(act, ab_stored, g * 32)
                act.activation(ab[:], PREP[0][0:2 * H, :], ACT.Sigmoid, bias=bab_s[:, 0:1]).then_inc(ab_done, 1)

            take(0, range(TT))
            cut_high(0, 0)
            wait(act, small_loaded, 32)
            gates(0)

            def turn(j, group=True):
                for q in range(2):
                    e = 2 * j + q
                    for m in range(NM):
                        n = IC[m][1]
                        wait(act, gu_done, NM * e + m + 1)
                        wait(act, h_done, NM * e + max(m - 1, 0))
                        act.activation(gated[0:n, m % 2], bank[2 * (m % 2)][0:n, :], ACT.Silu).then_inc(gated_done, 1)
                        wait(act, h_done, NM * e + m + 1)
                        wait(act, down_done, TT * e)
                        act.activation(h_hi[0:n, m], h[0:n, m], ACT.Copy).then_inc(h_hi_done, 1)
                        if group and q == 1 and m < 2:
                            take(j, (2 * m, 2 * m + 1))
                    cut_high(e + 1, 1 - q)
                    if group and q == 1:
                        gates(j)

            turn(0, group=False)
            with act.Fori(1, E // 2) as j:
                turn(j)

        @block.tensor
        def _(pe):
            def turn_tiles(g, tiles):
                for i in tiles:
                    wait(pe, xn_done, g * TT + i + 1)
                    wait(pe, hi_done, g * TT + i - 1)
                    if i == 0:
                        wait(pe, ab_done, g)
                    for k in range(KC):
                        last = pe.transpose(PREP[i % 2][:, k * P:(k + 1) * P], xn[:, i, k * P:(k + 1) * P], ident[:, 0])
                    last.then_inc(turned, 1)

            def gates(g):
                wait(pe, hi_done, g * TT + TT)
                for k in range(KC):
                    last = pe.matmul(PREP[0][0:2 * H, :], wab[:, k], xT[:, k], start=(k == 0), stop=(k == KC - 1))
                last.then_inc(z_done, 1)

            wait(pe, const_built, 4)
            turn_tiles(0, range(TT))
            wait(pe, small_loaded, 32)
            gates(0)
            wait(pe, lo_done, TT)

            def turn(j, group=True):
                for q in range(2):
                    e = 2 * j + q
                    wait(pe, gu_hi_done, e + 1)
                    wait(pe, gu_lo_done, e + 1)
                    for m in range(NM):
                        i0, n = IC[m]
                        wait(pe, h_done, NM * e + max(m - 1, 0))
                        if m == 1:
                            wait(pe, moe_done, TT * e + 1)
                        for u in range(2):
                            dst = bank[2 * (m % 2) + u][0:n, :]
                            cols = slice(u * I + i0, u * I + i0 + n)
                            for k in range(KC):
                                pe.matmul(dst, gu_hi[:, q, k, cols], x_hi[:, k], start=(k == 0), stop=False)
                                pe.matmul(dst, gu_hi[:, q, k, cols], x_lo[:, k], start=False, stop=False)
                                last = pe.matmul(dst, gu_lo[:, q, k, cols], x_hi[:, k], start=False,
                                                 stop=(k == KC - 1))
                        last.then_inc(gu_done, 1)
                        if group and q == 1 and m < 2:
                            turn_tiles(j, (2 * m, 2 * m + 1))
                    wait(pe, dn_hi_done, e + 1)
                    wait(pe, dn_lo_done, e + 1)
                    wait(pe, moe_done, TT * e + 1)
                    for m in range(NM):
                        n = IC[m][1]
                        if m == 0:
                            wait(pe, h_done, NM * e + 2)
                        wait(pe, h_hi_done, NM * e + m + 1)
                        wait(pe, h_lo_done, NM * e + m + 1)
                        for t in range(TT):
                            dst, rows = DOWN[t][:], slice(t * P, (t + 1) * P)
                            pe.matmul(dst, h_hi[0:n, m, rows], dn_hi[0:n, q, m], start=(m == 0), stop=False)
                            pe.matmul(dst, h_hi[0:n, m, rows], dn_lo[0:n, q, m], start=False, stop=False)
                            last = pe.matmul(dst, h_lo[0:n, m, rows], dn_hi[0:n, q, m], start=False,
                                             stop=(m == NM - 1))
                            if m == NM - 1:
                                last.then_inc(down_done, 1)
                    if group and q == 1:
                        gates(j)

            turn(0, group=False)
            with pe.Fori(1, E // 2) as j:
                turn(j)


def heads(nc, bank, ident, pow_half, xT_hi_d, xT_lo_d, alpha_d, beta_d, oT_d, weights, taps, ln_w, ln_b):
    NPROJ = len(weights)
    with ExitStack() as ctx:
        def sb(name, shape, dt=F32):
            return ctx.enter_context(nc.sbuf_tensor(name, shape, dt))

        def sem(name):
            return ctx.enter_context(nc.semaphore(name))

        mask = [sb(f"mask{b}", [P, 2, P]) for b in LEVELS]
        same = sb("same", [P, P])
        sel = sb("sel", [P, G, SB])
        zeros = sb("zeros", [P, C])
        lnw = sb("lnw", [P, 1])
        lnb = sb("lnb", [P, 1])
        x_hi = sb("hx_hi", [P, KC, T], F32R)
        x_lo = sb("hx_lo", [P, KC, T], F32R)
        w_raw = sb("w_raw", [P, NPROJ, KC, D])
        w_hi = sb("w_hi", [P, NPROJ, KC, D], F32R)
        w_lo = sb("w_lo", [P, NPROJ, KC, D], F32R)
        tap_next = sb("tap_next", [P, 3, KS + 1])
        tap = sb("tap", [P, 3, KS + 1])
        y = [[sb(f"y{i}_{j}", [P, KS - 1 + GT]) for j in range(3)] for i in range(3)]
        conv = sb("conv", [P, GT])
        kq = sb("kq", [P, 2, 2, GT])
        vT = sb("vT", [P, GT])
        gT = sb("gT", [P, GROUPS, GT])
        alpha = sb("alpha", [P, 2, GT])
        beta = sb("beta", [P, 2, GT])
        decay = sb("decay", [P, G, 1 + C])
        gamma = sb("gamma", [P, 2, G, 1 + C])
        k_beta = sb("k_beta", [P, GT])
        k_gamma = sb("k_gamma", [P, 2, GT])
        q_gamma = sb("q_gamma", [P, 2, GT])
        LT = sb("LT", [P, 2, G, C])
        diag = sb("diag", [P, G, C])
        Lc = sb("Lc", [P, G, SB])
        Lx = sb("Lx", [P, G, SB, SB])
        Lb = sb("Lb", [P, G, SB, SB])
        prods = sb("prods", [P, G, SB])
        Tc = sb("Tc", [P, G, SB])
        AT = sb("AT", [P, 2, G, C])
        masked = sb("masked", [P, len(LEVELS), G, C])
        TT = sb("TT", [P, 2, G, C])
        Tn = sb("Tn", [P, G, C])
        MT = sb("MT", [P, G, C])
        k_rows = sb("k_rows", [P, 2, G, D])
        v_rows = sb("v_rows", [P, 2, G, D])
        S = sb("S", [P, D])
        R = sb("R", [P, D])
        Wc = sb("Wc", [P, D])
        stats = sb("hstats", [P, G, 6])
        mv = sb("hmv", [P, G, 2])
        veps = sb("hveps", [P, G])
        rstd = sb("hrstd", [P, G])
        on = sb("on", [P, G, D])
        oT = sb("oT", [P, GT])
        oG = sb("oG", [P, GT])

        PJ, IB, TR, CH, OB = bank[0:2], bank[2:4], bank[4], bank[5], bank[6:8]

        built = sem("hbuilt")
        ln_loaded = sem("ln_loaded")
        x_loaded = [sem(f"hx_loaded{g}") for g in range(GROUPS)]
        w_loaded = [sem(f"w_loaded{i}") for i in range(NPROJ)]
        tap_loaded = sem("tap_loaded")
        alpha_loaded = [sem(f"alpha_loaded{i}") for i in range(2)]
        beta_loaded = [sem(f"beta_loaded{i}") for i in range(2)]
        o_stored = sem("o_stored")
        proj_done = sem("proj_done")
        step_done = [sem("step_done_a"), sem("step_done_b")]
        late_done = sem("late_done")
        l_done = sem("l_done")
        spread_done = sem("spread_done")
        chain_done = sem("chain_done")
        k_turned = sem("k_turned")
        v_turned = sem("v_turned")
        o_turned = sem("o_turned")
        y_done = sem("hy_done")
        silu_done = sem("silu_done")
        tanh_done = sem("tanh_done")
        copied = [sem("copied_a"), sem("copied_b")]
        lb_done = sem("lb_done")
        mt32_done = sem("mt32_done")
        tt64_done = sem("tt64_done")
        mt64_done = sem("mt64_done")
        tt128_done = sem("tt128_done")
        tap_done = sem("tap_done")
        gate_done = sem("gate_done")
        w_done = sem("w_done")
        v_done = sem("v_done")
        oT_done = sem("oT_done")
        whi_done = sem("whi_done")
        wlo_done = sem("wlo_done")
        tap_copied = sem("tap_copied")
        decay_done = sem("decay_done")
        gamma_done = sem("gamma_done")
        sel_built = sem("sel_built")
        lt_done = sem("lt_done")
        diag_done = sem("diag_done")
        lc_done = sem("lc_done")
        lx_done = sem("lx_done")
        at_done = sem("at_done")
        tt_done = [sem("tt_done_a"), sem("tt_done_b")]
        tn_done = [sem("tn_done_a"), sem("tn_done_b")]
        tn64_done = sem("tn64_done")
        k_done = sem("k_done")
        r_done = sem("r_done")
        s_done = sem("s_done")
        conv_done = sem("conv_done")
        stats_done = sem("hstats_done")
        mv_done = sem("hmv_done")
        veps_done = sem("hveps_done")
        on_done = sem("on_done")
        mask_done = sem("mask_done")
        solve_done = sem("solve_done")
        t8_done = sem("t8_done")
        kb_done = sem("kb_done")
        kq_gamma_done = sem("kq_gamma_done")
        rstd_done = sem("hrstd_done")
        oG_done = sem("oG_done")
        block = ctx.enter_context(nc.Block())

        def turns(eng, turn):
            turn(eng, -1, 2, False, False, True, False)
            turn(eng, -1, 3, False, True, True, False)
            for g in range(GROUPS):
                turn(eng, 0, g, True, True, True, g > 0)
            with eng.Fori(1, NH - 1) as hh:
                for g in range(GROUPS):
                    turn(eng, hh, g, True, True, True, True)
            for g in range(GROUPS):
                turn(eng, NH - 1, g, True, g < 3, g < 2, True)
            turn(eng, NH, 0, False, False, False, True)

        def counter(hh, g):
            def at(per, d, c=0):
                return hh * (GROUPS * per) + ((g + d) * per + c)
            return at

        def half(c):
            return slice(2 * c, 2 * c + 2)

        def chunk(c):
            return slice(c * C, (c + 1) * C)

        def has_next(hh):
            return not isinstance(hh, int) or 0 <= hh < NH - 1

        def row_loads(hh, g):
            return (hh * (GROUPS // 2)) * 16 + ((g + 2) // 2 + 1) * 16

        @block.sync
        def _(sp):
            def load_x(b, g):
                group = b * GROUPS + g
                sp.dma_start(x_hi[:, :, g * GT:(g + 1) * GT].bitcast(F32), xT_hi_d[group]).then_inc(x_loaded[g], 16)
                sp.dma_start(x_lo[:, :, g * GT:(g + 1) * GT].bitcast(F32), xT_lo_d[group]).then_inc(x_loaded[g], 16)

            def load_w(i, h):
                sp.dma_start(w_raw[:, i], weights[i][:, bass.ds(h * D, D)].rearrange("(k p) n -> p k n", p=P))\
                  .then_inc(w_loaded[i], 16)

            def load_tap(h):
                sp.dma_start(tap_next[:], taps[bass.ds(h, 1)].rearrange("o p (i j) -> (o p) i j", i=3))\
                  .then_inc(tap_loaded, 16)

            batch = [0]

            def load_rows(dst, src, hh, g, q, sem):
                b = hh // H if isinstance(hh, int) else batch[0]
                rows = src.rearrange("g h t -> (g h) t")[bass.ds(hh + (b * (GROUPS - 1) + g) * H, 1)]
                sp.dma_start(dst[:, q], rows.to_broadcast([P, GT])).then_inc(sem[q], 16)

            def turn(hh, g, x_next=None, after_next=True, last=False):
                at = counter(hh, g)
                later, q = (hh, 3) if g == 0 else (hh + 1, g - 1), (g + 3) % 2
                if not (last and g > 0):
                    sp.wait_ge(kb_done, at(1, 2))
                    load_rows(beta, beta_d, *later, q, beta_loaded)
                    sp.wait_ge(gamma_done, at(1, 2))
                    load_rows(alpha, alpha_d, *later, q, alpha_loaded)
                if not (isinstance(hh, int) and hh == 0 and g == 0):
                    sp.wait_ge(oG_done, at(1, 0))
                    where, gw = (hh, g - 1) if g > 0 else (hh - 1, 3)
                    sp.dma_start(oT_d[bass.ds(where, 1), :, gw * GT:(gw + 1) * GT].rearrange("o p t -> (o p) t"), oG[:])\
                      .then_inc(o_stored, 16)
                if g == 3 and after_next:
                    h2 = (hh + 2) & (H - 1)
                    h2 = fixed(sp, h2, H - 1)
                    for i in range(NPROJ):
                        sp.wait_ge(wlo_done, hh * NPROJ + (NPROJ + i + 1))
                        load_w(i, h2)
                    sp.wait_ge(tap_copied, hh + 2)
                    load_tap(h2)
                if x_next is not None:
                    sp.wait_ge(proj_done, NPROJ * ((H - 1) * GROUPS + x_next + 1))
                    load_x(1, x_next)

            sp.dma_start(lnw[:], ln_w).then_inc(ln_loaded, 16)
            sp.dma_start(lnb[:], ln_b).then_inc(ln_loaded, 16)
            load_w(0, 0)
            load_x(0, 0)
            load_tap(0)
            for i in range(1, NPROJ):
                load_w(i, 0)
            for g in range(2):
                load_rows(beta, beta_d, 0, g, g, beta_loaded)
                load_rows(alpha, alpha_d, 0, g, g, alpha_loaded)
            for g in range(1, GROUPS):
                load_x(0, g)
            sp.wait_ge(kb_done, 1)
            load_rows(beta, beta_d, 0, 2, 0, beta_loaded)
            for i in range(NPROJ):
                sp.wait_ge(wlo_done, i + 1)
                load_w(i, 1)
            sp.wait_ge(tap_copied, 1)
            load_tap(1)
            sp.wait_ge(gamma_done, 1)
            load_rows(alpha, alpha_d, 0, 2, 0, alpha_loaded)
            for g in range(GROUPS):
                turn(0, g)
            with sp.Fori(1, H - 2) as hh:
                for g in range(GROUPS):
                    turn(hh, g)
            for g in range(GROUPS):
                turn(H - 2, g, x_next={2: 0, 3: 1}.get(g))
            for g in range(GROUPS):
                turn(H - 1, g, x_next={0: 2, 1: 3}.get(g))
            batch[0] = 1
            with sp.Fori(H, NH - 2) as hh:
                for g in range(GROUPS):
                    turn(hh, g)
            for g in range(GROUPS):
                turn(NH - 2, g, after_next=False)
            for g in range(GROUPS):
                turn(NH - 1, g, after_next=False, last=True)
            sp.wait_ge(oG_done, NH * GROUPS)
            sp.dma_start(oT_d[NH - 1, :, 3 * GT:4 * GT], oG[:]).then_inc(o_stored, 16)
            sp.wait_ge(o_stored, 16 * NH * GROUPS)

        @block.gpsimd
        def _(pool):
            n = 0
            for tile in [*mask, zeros]:
                pool.memset(tile[:], 0.0).then_inc(built, 1)
                n += 1
            pool.memset(decay[:, :, 0:1], 0.0).then_inc(built, 1)
            pool.memset(gamma[:, :, :, 0:1], 1.0).then_inc(built, 1)
            for i in range(3):
                pool.memset(y[i][0][:, 0:KS - 1], 0.0).then_inc(built, 1)
            pool.memset(same[:], 1.0).then_inc(built, 1)
            n += 6
            pool.wait_ge(built, n)
            blocks = same[:].rearrange("p (q r) -> p q r", r=SB)
            for base, step, mult in ((0, -SB, 1), (SB - 1, SB, -1)):
                pool.affine_select(out=blocks, in_=blocks, compare_op=ALU.is_ge, fill=0.0, base=base,
                                   pattern=[[step, P // SB], [0, SB]], channel_multiplier=mult).then_inc(built, 1)
                n += 1
                pool.wait_ge(built, n)
            pool.wait_ge(sel_built, G)
            pool.tensor_copy(Tc[:, :, 0:1], sel[:, :, 0:1]).then_inc(built, 1)
            n += 1
            for tile, b in zip(mask, LEVELS):
                part = tile[:].rearrange("p c (q r) -> p c q r", r=2 * b)[:, :, :, b:2 * b]
                pool.memset(part, 1.0).then_inc(built, 1)
                n += 1
                for base, step, mult in ((0, -2 * b, 1), (b - 1, 2 * b, -1)):
                    pool.wait_ge(built, n)
                    for c in range(2):
                        pool.affine_select(out=part[:, c], in_=part[:, c], compare_op=ALU.is_ge, fill=0.0, base=base,
                                           pattern=[[step, P // (2 * b)], [0, b]], channel_multiplier=mult)\
                            .then_inc(built, 1)
                        n += 1
            assert n == BUILT

            def cut_low(i, value):
                pool.wait_ge(whi_done, value)
                pool.tensor_tensor(w_lo[:, i], w_raw[:, i], w_hi[:, i].bitcast(F32), ALU.subtract).then_inc(wlo_done, 1)

            for i in range(NPROJ):
                cut_low(i, i + 1)

            def turn(pool, hh, g, chain, inv, proj, ln):
                at = counter(hh, g)
                for s in range(STEPS):
                    if s in SOLVE_AT and (proj if s > STEPS // 2 else inv):
                        d = 1 if s > STEPS // 2 else 0
                        for i in range(*SOLVE_AT[s]):
                            k = 2 * i
                            if i == 0:
                                pool.wait_ge(lb_done, at(1, 2 + d))
                            wait(pool, solve_done, at(SOLVE_PER, 1 + d, k))
                            pool.tensor_tensor(prods[:, :, i + 1:], Lb[:, :, i + 1:, i],
                                               Tc[:, :, i:i + 1].to_broadcast([P, G, SB - 1 - i]), ALU.mult)\
                                .then_inc(solve_done, 1)
                            if i == 0:
                                wait(pool, t8_done, at(1, 1 + d))
                            pool.wait_ge(solve_done, at(SOLVE_PER, 1 + d, k + 1))
                            pool.tensor_tensor(Tc[:, :, i + 1:], (sel if i == 0 else Tc)[:, :, i + 1:],
                                               prods[:, :, i + 1:], ALU.subtract).then_inc(solve_done, 1)
                    if inv and s == 1:
                        pool.wait_ge(solve_done, at(SOLVE_PER, 2))
                        wait(pool, chain_done, at(12, 0))
                        pool.tensor_tensor(TT[:, (g + 1) % 2].rearrange("p c (q t) -> p c q t", t=SB),
                                           Tc[:].rearrange("p c (o t) -> p c o t", o=1).to_broadcast([P, G, P // SB, SB]),
                                           same[:].rearrange("p (c q t) -> p c q t", c=1, t=SB)
                                           .to_broadcast([P, G, P // SB, SB]), ALU.mult).then_inc(t8_done, 1)
                    if proj and s in MASK_AT:
                        lvl = MASK_AT[s]
                        pool.wait_ge(lt_done, at(1, 3))
                        for c in range(2):
                            wait(pool, step_done[c], at(STEP_PER, 1, 2 * lvl + 2))
                            pool.tensor_tensor(masked[:, lvl, half(c)], LT[:, g % 2, half(c)], mask[lvl][:], ALU.mult)\
                                .then_inc(mask_done, 1)
                    if ln and s == 5:
                        pool.wait_ge(veps_done, at(1, 0))
                        pool.tensor_tensor(rstd[:], veps[:], pow_half[:], ALU.pow).then_inc(rstd_done, 1)
                    if inv and s in (6, 7):
                        i, par = s - 6, (g + 1) % 2
                        if i == 0:
                            pool.wait_ge(gamma_done, at(1, 2))
                            wait(pool, chain_done, at(12, 0))
                        dst = (k_gamma, q_gamma)[i][:, par].rearrange("p (c t) -> p c t", c=G)
                        pool.tensor_tensor(dst, kq[:, par, i].rearrange("p (c t) -> p c t", c=G),
                                           gamma[:, par, :, i:i + C], ALU.mult).then_inc(kq_gamma_done, 1)
                    if proj and s == 10:
                        pool.wait_ge(silu_done, at(3, 2, 1))
                        pool.wait_ge(beta_loaded[g % 2], row_loads(hh, g))
                        wait(pool, k_turned, at(1, 2))
                        pool.tensor_tensor(k_beta[:], kq[:, g % 2, 0], beta[:, g % 2], ALU.mult).then_inc(kb_done, 1)
                    if ln and s == 11:
                        pool.wait_ge(oT_done, at(1, 0))
                        wait(pool, o_stored, at(16, -1))
                        pool.wait_ge(gate_done, at(1, 0))
                        pool.tensor_tensor(oG[:], oT[:], gT[:, (g - 1) % 4], ALU.mult).then_inc(oG_done, 1)
                    if proj and (g == 1 and s in (7, 12, 17) or g == 2 and s == 1) and has_next(hh):
                        i = {7: 0, 12: 1, 17: 2, 1: 3}[s]
                        cut_low(i, hh * NPROJ + (NPROJ + i + 1))

            turns(pool, turn)

        @block.vector
        def _(dve):
            dve.memset(S[:], 0.0).then_inc(s_done, 1)
            for c in range(G):
                dve.tensor_reduce(sel[:, c], ident[:, 0].rearrange("p (q i) -> p i q", i=SB), mybir.AxisListType.X,
                                  ALU.add).then_inc(sel_built, 1)
            dve.wait_ge(built, BUILT)
            dve.wait_ge(tap_loaded, 16)
            dve.tensor_copy(tap[:], tap_next[:]).then_inc(tap_copied, 1)

            def turn(dve, hh, g, chain, inv, proj, ln):
                at = counter(hh, g)
                par, cur = (g + 1) % 2, g % 2
                for s in range(STEPS):
                    if inv and s == A_AT:
                        for c in range(2):
                            dve.wait_ge(step_done[c], at(STEP_PER, 1, 1))
                            if c == 0:
                                dve.wait_ge(decay_done, at(1, 2))
                            wait(dve, chain_done, at(12, 0))
                            dve.tensor_tensor(AT[:, par, half(c)], IB[c][:, 0:2 * C].rearrange("p (c t) -> p c t", c=2),
                                              decay[:, half(c), 1:1 + C], ALU.mult).then_inc(at_done, 1)
                    if g == 2 and s == 0 and proj and has_next(hh):
                        dve.wait_ge(tap_loaded, (hh + 2) * 16)
                        dve.wait_ge(silu_done, at(3, 2))
                        dve.tensor_copy(tap[:], tap_next[:]).then_inc(tap_copied, 1)
                    if ln and s == 2:
                        dve.wait_ge(chain_done, at(12, 0))
                        wait(dve, on_done, at(4, -1))
                        for c in range(G):
                            dve.bn_stats(stats[:, c], OB[(g - 1) % 2][:, chunk(c)]).then_inc(stats_done, 1)
                    if ln and s == 3:
                        dve.wait_ge(stats_done, at(4, 0))
                    if inv and s == 3:
                        dve.wait_ge(k_turned, at(1, 2))
                        dve.tensor_tensor(k_rows[:, par], TR[:].rearrange("p (c d) -> p c d", c=G),
                                          decay[:, :, C:C + 1].to_broadcast([P, G, D]), ALU.mult).then_inc(k_done, 1)
                    if chain and s in CHAIN:
                        k = CHAIN[s]
                        c, r = k // 3, k % 3
                        if r == 0:
                            dve.wait_ge(chain_done, at(12, 0, k + 1))
                            if c == 0:
                                dve.wait_ge(v_done, at(1, 1))
                            dve.scalar_tensor_tensor(out=R[:], in0=CH[:, 0:D], scalar=-S_K, in1=v_rows[:, cur, c],
                                                     op0=ALU.mult, op1=ALU.add).then_inc(r_done, 1)
                        if r == 2:
                            dve.wait_ge(chain_done, at(12, 0, k + 1))
                            dve.wait_ge(s_done, at(4, 0, c + 1))
                            if g == 3 and c == 3:
                                dve.memset(S[:], 0.0).then_inc(s_done, 1)
                            else:
                                dve.scalar_tensor_tensor(out=S[:], in0=S[:], scalar=gamma[:, cur, c, C:C + 1],
                                                         in1=CH[:, 2 * D:3 * D], op0=ALU.mult, op1=ALU.add)\
                                   .then_inc(s_done, 1)
                    if inv and s == T8_AT:
                        dve.wait_ge(t8_done, at(1, 2))
                        wait(dve, late_done, at(LATE_PER, 0, 3))
                        for c in range(2):
                            dve.transpose(Tn[:, half(c)], TT[:, par, half(c)]).then_inc(tn_done[c], 1)
                    if ln and s == 4:
                        for c in range(G):
                            dve.bn_aggr(mv[:, c], stats[:, c]).then_inc(mv_done, 1)
                        dve.wait_ge(mv_done, at(4, 0))
                        dve.tensor_scalar(veps[:], mv[:, :, 1], EPS, None, ALU.add).then_inc(veps_done, 1)
                    if s == 5 and inv:
                        dve.wait_ge(alpha_loaded[par], row_loads(hh, g - 1))
                        wait(dve, s_done, at(4, 0, 1))
                        wait(dve, kq_gamma_done, at(2, 0))
                        for c in range(G):
                            last = dve.tensor_tensor_scan(gamma[:, par, c, 1:1 + C], alpha[:, par, chunk(c)], zeros[:],
                                                          1.0, ALU.mult, ALU.add)
                        last.then_inc(gamma_done, 1)
                    if ln and s == 7:
                        dve.wait_ge(rstd_done, at(1, 0))
                        wait(dve, o_turned, at(1, -1))
                        for c in range(G):
                            dve.tensor_scalar(on[:, c], OB[(g - 1) % 2][:, chunk(c)], mv[:, c, 0:1], rstd[:, c:c + 1],
                                              ALU.subtract, ALU.mult).then_inc(on_done, 1)
                    if inv and s in TT_AT:
                        lvl = TT_AT[s]
                        for c in range(2):
                            dve.wait_ge(step_done[c], at(STEP_PER, 1, 2 * lvl + 3))
                            dve.tensor_tensor(TT[:, par, half(c)], TT[:, par, half(c)],
                                              IB[c][:, 0:2 * C].rearrange("p (c t) -> p c t", c=2), ALU.subtract)\
                               .then_inc(tt_done[c], 1)
                        for c in range(2):
                            dve.wait_ge(tt_done[c], at(len(LEVELS), 1, lvl + 1))
                            dve.transpose(Tn[:, half(c)], TT[:, par, half(c)]).then_inc(tn_done[c], 1)
                    if inv and s == T32_AT:
                        dve.wait_ge(tt64_done, at(2, 1, 1))
                        dve.transpose(Tn[32:64, :, 0:32], TT[0:32, par, :, 32:64]).then_inc(tn64_done, 1)
                    if proj and s in CONV_AT:
                        i, j = CONV_AT[s]
                        if j == 0:
                            dve.wait_ge(tap_done, at(3, 2, i + 1))
                            dve.wait_ge(y_done, at(3, 2, i + 1))
                        else:
                            dve.wait_ge(conv_done, at(9, 2, 3 * i + j))
                        dve.scalar_tensor_tensor(out=conv[:], in0=y[i][Y_AT[(g + 2) % 4]][:, j:j + GT],
                                                 scalar=tap[:, i, j:j + 1], in1=conv[:], op0=ALU.mult, op1=ALU.add)\
                           .then_inc(conv_done, 1)
                    if proj and s == DECAY_AT:
                        dve.wait_ge(alpha_loaded[cur], row_loads(hh, g))
                        wait(dve, k_done, at(1, 2))
                        wait(dve, at_done, at(2, 2))
                        for c in range(G):
                            last = dve.tensor_tensor_scan(decay[:, c, 1:1 + C], alpha[:, cur, chunk(c)], ident[:, 0],
                                                          0.0, ALU.mult, ALU.add)
                        last.then_inc(decay_done, 1)
                    if proj and s == L_AT:
                        dve.wait_ge(l_done, at(1, 3))
                        dve.wait_ge(decay_done, at(1, 3))
                        wait(dve, late_done, at(LATE_PER, 1))
                        dve.scalar_tensor_tensor(out=LT[:, cur], in0=TR[:].rearrange("p (c t) -> p c t", c=G),
                                                 scalar=S_K * S_K, in1=decay[:, :, 0:C], op0=ALU.mult, op1=ALU.mult)\
                           .then_inc(lt_done, 1)
                    if proj and s == L_AT + 1:
                        dve.wait_ge(lt_done, at(1, 3))
                        wait(dve, lc_done, at(1, 2))
                        dve.tensor_tensor(diag[:], LT[:, cur],
                                          same[:].rearrange("p (c t) -> p c t", c=1).to_broadcast([P, G, C]), ALU.mult)\
                           .then_inc(diag_done, 1)
                    if proj and s == L_AT + 2:
                        dve.wait_ge(diag_done, at(1, 3))
                        wait(dve, lx_done, at(1, 2))
                        dve.tensor_reduce(Lc[:], diag[:].rearrange("p c (q t) -> p c t q", t=SB), mybir.AxisListType.X,
                                          ALU.add).then_inc(lc_done, 1)
                    if proj and s == L_AT + 3:
                        dve.wait_ge(lc_done, at(1, 3))
                        wait(dve, spread_done, at(1, 2))
                        dve.tensor_tensor(Lx[:], Lc[:].rearrange("p c (t o) -> p c t o", o=1).to_broadcast([P, G, SB, SB]),
                                          sel[:].rearrange("p c (o i) -> p c o i", o=1).to_broadcast([P, G, SB, SB]),
                                          ALU.mult).then_inc(lx_done, 1)

            turns(dve, turn)

        @block.scalar
        def _(act):
            act.wait_ge(built, BUILT)
            act.wait_ge(ln_loaded, 32)

            def cut_high(i, loads):
                act.wait_ge(w_loaded[i], loads)
                act.activation(w_hi[:, i], w_raw[:, i], ACT.Copy).then_inc(whi_done, 1)

            for i in range(NPROJ):
                cut_high(i, 16)

            def turn(act, hh, g, chain, inv, proj, ln):
                at = counter(hh, g)
                par, cur = (g + 1) % 2, g % 2
                for s in range(STEPS):
                    if s == 0 and inv:
                        act.wait_ge(conv_done, at(9, 2))
                        wait(act, v_turned, at(1, 1))
                        act.activation(vT[:], conv[:], ACT.Silu, bias=tap[:, 2, KS:KS + 1]).then_inc(silu_done, 1)
                        act.wait_ge(proj_done, at(NPROJ, 2))
                        wait(act, oG_done, at(1, -2))
                        act.activation(gT[:, (g + 1) % 4], PJ[1][:], ACT.Tanh, scale=0.5).then_inc(tanh_done, 1)
                    if s == 2 and inv:
                        act.wait_ge(tanh_done, at(1, 2))
                        act.activation(gT[:, (g + 1) % 4], gT[:, (g + 1) % 4], ACT.Copy, scale=0.5, bias=0.5)\
                           .then_inc(gate_done, 1)
                    if inv and s in MT_AT:
                        lvl = MT_AT[s]
                        for c in range(2):
                            act.wait_ge(step_done[c], at(STEP_PER, 1, 2 * lvl + 2))
                            act.activation(MT[:, half(c)], IB[c][:, 0:2 * C].rearrange("p (c t) -> p c t", c=2),
                                           ACT.Copy).then_inc(copied[c], 1)
                    if inv and s in (Y32_AT, T32_AT):
                        k = 0 if s == Y32_AT else 1
                        act.wait_ge(late_done, at(LATE_PER, 1, k + 1))
                        for u in range(0, P, 64):
                            lo, hi = slice(u, u + 32), slice(u + 32, u + 64)
                            w = IB[k][:, 0:GT // 2].rearrange("p (c t) -> p c t", c=G)
                            if k == 0:
                                act.activation(MT[hi, :, lo], w[hi, :, 0:32], ACT.Copy).then_inc(mt32_done, 1)
                            else:
                                act.activation(TT[lo, par, :, hi], w[lo, :, 0:32], ACT.Copy, scale=-1.0)\
                                   .then_inc(tt64_done, 1)
                    if inv and s in (Y64_AT, T64_AT):
                        k = 0 if s == Y64_AT else 1
                        act.wait_ge(late_done, at(LATE_PER, 1, k + 3))
                        w = IB[k][:, 0:GT // 2].rearrange("p (c t) -> p c t", c=G)
                        if k == 0:
                            act.activation(MT[64:128, :, 0:64], w[64:128], ACT.Copy).then_inc(mt64_done, 1)
                        else:
                            act.activation(TT[0:64, par, :, 64:128], w[0:64], ACT.Copy, scale=-1.0)\
                               .then_inc(tt128_done, 1)
                    if chain and s in CHAIN and CHAIN[s] % 3 == 1:
                        k = CHAIN[s]
                        act.wait_ge(chain_done, at(12, 0, k + 1))
                        act.activation(Wc[:], CH[:, D:2 * D], ACT.Copy, scale=S_K).then_inc(w_done, 1)
                    if proj and s == BASE_AT:
                        act.wait_ge(spread_done, at(1, 3))
                        wait(act, t8_done, at(1, 2))
                        act.activation(Lb[:].rearrange("p c t i -> p (c t i)"), TR[:, 0:G * SB * SB], ACT.Copy)\
                           .then_inc(lb_done, 1)
                    if proj and s in (5, 10, 15):
                        i = (5, 10, 15).index(s)
                        ahead = (g + 2) % 4
                        act.wait_ge(proj_done, at(NPROJ, 2, i + 1))
                        if i == 0:
                            act.wait_ge(tap_copied, (hh + 1) + (1 if g >= 2 else 0))
                        wait(act, silu_done, at(3, 2, i))
                        act.activation(conv[:], PJ[i % 2][:], ACT.Copy, scale=tap[:, i, KS - 1:KS]).then_inc(tap_done, 1)
                        wait(act, conv_done, at(9, 1, 3 * i + 3))
                        if ahead < 3:
                            act.activation(y[i][Y_AT[ahead + 1]][:, 0:KS - 1], PJ[i % 2][:, GT - KS + 1:GT], ACT.Copy)
                        act.activation(y[i][Y_AT[ahead]][:, KS - 1:], PJ[i % 2][:], ACT.Copy).then_inc(y_done, 1)
                    if inv and s == 6:
                        act.wait_ge(v_turned, at(1, 2))
                        wait(act, r_done, at(4, -1, 4))
                        act.activation(v_rows[:, par], TR[:].rearrange("p (c d) -> p c d", c=G), ACT.Copy)\
                           .then_inc(v_done, 1)
                    if proj and s in (9, 14):
                        i = (9, 14).index(s)
                        act.wait_ge(conv_done, at(9, 2, 3 * i + 3))
                        wait(act, kq_gamma_done, at(2, 1))
                        act.activation(kq[:, cur, i], conv[:], ACT.Silu, bias=tap[:, i, KS:KS + 1]).then_inc(silu_done, 1)
                    if ln and s == 10:
                        act.wait_ge(o_turned, at(1, 0))
                        wait(act, oG_done, at(1, -1))
                        act.activation(oT[:], TR[:], ACT.Identity, bias=lnb[:, 0:1], scale=lnw[:, 0:1])\
                           .then_inc(oT_done, 1)
                    if proj and (g == 1 and s in (7, 12, 17) or g == 2 and s == 1) and has_next(hh):
                        i = {7: 0, 12: 1, 17: 2, 1: 3}[s]
                        act.wait_ge(proj_done, hh * (GROUPS * NPROJ) + (3 * NPROJ + i + 1))
                        cut_high(i, (hh + 2) * 16)

            turns(act, turn)

        @block.tensor
        def _(pe):
            def turn(pe, hh, g, chain, inv, proj, ln):
                at = counter(hh, g)
                par, cur = (g + 1) % 2, g % 2
                sent = [0]

                def project_some(n):
                    cols = slice((g + 2) % 4 * GT, (g + 2) % 4 * GT + GT)
                    for _ in range(n):
                        i, j = divmod(sent[0], 3 * KC)
                        k, part = divmod(j, 3)
                        sent[0] += 1
                        dst = PJ[i % 2][:]
                        if j == 0:
                            if i == 0:
                                wait(pe, y_done, at(3, 2))
                                pe.wait_ge(x_loaded[(g + 2) % 4], (((hh + (1 if g >= 2 else 0)) >> 4) + 1) * 32)
                            if i == 1:
                                wait(pe, tanh_done, at(1, 2))
                            if i >= 2:
                                pe.wait_ge(y_done, at(3, 2, i - 1))
                            pe.wait_ge(wlo_done, (hh + (1 if g >= 2 else 0)) * NPROJ + (i + 1))
                        a, b = ((w_hi, x_hi), (w_hi, x_lo), (w_lo, x_hi))[part]
                        last = pe.matmul(dst, a[:, i, k], b[:, k, cols], start=(j == 0), stop=(j == 3 * KC - 1))
                        if j == 3 * KC - 1:
                            last.then_inc(proj_done, 1)

                def step(c, s):
                    w = IB[c]
                    if s == A_AT:
                        pe.wait_ge(kb_done, at(1, 2))
                        pe.wait_ge(silu_done, at(3, 1, 2))
                        wait(pe, tt128_done, at(1, 1))
                        for j in range(2):
                            n = 2 * c + j
                            last = pe.matmul(w[:, chunk(j)], k_beta[:, chunk(n)], kq[:, par, 1, chunk(n)],
                                             start=True, stop=True)
                    elif s in MT_AT:
                        lvl = MT_AT[s]
                        pe.wait_ge(mask_done, at(2 * len(LEVELS), 1, 2 * lvl + c + 1))
                        pe.wait_ge(tn_done[c], at(len(LEVELS) + 1, 1, lvl + 1))
                        if lvl == 0:
                            pe.wait_ge(at_done, at(2, 1, c + 1))
                        for j in range(2):
                            last = pe.matmul(w[:, chunk(j)], masked[:, lvl, 2 * c + j], Tn[:, 2 * c + j],
                                             start=True, stop=True)
                    elif s in TT_AT:
                        lvl = TT_AT[s]
                        pe.wait_ge(copied[c], at(len(LEVELS), 1, lvl + 1))
                        for j in range(2):
                            last = pe.matmul(w[:, chunk(j)], MT[:, 2 * c + j], TT[:, par, 2 * c + j],
                                             start=True, stop=True)
                    else:
                        return
                    last.then_inc(step_done[c], 1)

                def late_waits(s):
                    if s == Y32_AT:
                        for c in range(2):
                            pe.wait_ge(tn_done[c], at(len(LEVELS) + 1, 2))
                    if s == T32_AT:
                        pe.wait_ge(mt32_done, at(2, 2))
                    if s == Y64_AT:
                        pe.wait_ge(tt64_done, at(2, 2))
                        pe.wait_ge(tn64_done, at(1, 2))
                    if s == T64_AT:
                        pe.wait_ge(mt64_done, at(1, 2))

                def late(s):
                    b = 32 if s in (Y32_AT, T32_AT) else 64
                    first = s in (Y32_AT, Y64_AT)
                    for c in range(G):
                        for u in range(0, P, 2 * b):
                            lo, hi = slice(u, u + b), slice(u + b, u + 2 * b)
                            cols = slice(c * 64, c * 64 + b)
                            if first:
                                last = pe.matmul(IB[0][hi, cols], LT[lo, par, c, hi], Tn[lo, c, lo], start=True, stop=True)
                            else:
                                last = pe.matmul(IB[1][lo, cols], MT[hi, c, lo], TT[hi, par, c, hi], start=True, stop=True)
                    last.then_inc(late_done, 1)

                def chain_step(k):
                    c, r = divmod(k, 3)
                    o = OB[cur][:, chunk(c)]
                    if r == 0:
                        pe.wait_ge(s_done, at(4, 0, c + 1))
                        if c == 0:
                            pe.wait_ge(kq_gamma_done, at(2, 1))
                            wait(pe, on_done, at(4, -1))
                        pe.matmul(o, q_gamma[:, cur, chunk(c)], S[:], start=True, stop=False)
                        pe.matmul(CH[:, 0:D], k_gamma[:, cur, chunk(c)], S[:], start=True, stop=True)\
                          .then_inc(chain_done, 1)
                    if r == 1:
                        pe.wait_ge(r_done, at(4, 0, c + 1))
                        if c == 0:
                            pe.wait_ge(tt128_done, at(1, 1))
                        pe.matmul(CH[:, D:2 * D], TT[:, cur, c], R[:], start=True, stop=True).then_inc(chain_done, 1)
                    if r == 2:
                        pe.wait_ge(w_done, at(4, 0, c + 1))
                        if c == 0:
                            pe.wait_ge(k_done, at(1, 1))
                            pe.wait_ge(at_done, at(2, 1))
                        pe.matmul(o, AT[:, cur, c], Wc[:], start=False, stop=True)
                        pe.matmul(CH[:, 2 * D:3 * D], k_rows[:, cur, c], Wc[:], start=True, stop=True)\
                          .then_inc(chain_done, 1)

                for s in range(STEPS):
                    if inv:
                        step(0, s)
                    by_blocks = inv and s in (Y32_AT, T32_AT, Y64_AT, T64_AT)
                    if by_blocks:
                        late_waits(s)
                    if proj:
                        project_some(1)
                    if by_blocks:
                        late(s)
                    if proj:
                        project_some(PIECES[2 * s] - 1)
                    if chain and s in CHAIN:
                        chain_step(CHAIN[s])
                    if inv:
                        step(1, s)
                    if proj:
                        project_some(PIECES[2 * s + 1])
                    if inv and s == 0:
                        pe.wait_ge(lb_done, at(1, 2))
                        for c in range(G):
                            last = pe.transpose(TR[:, chunk(c)], k_beta[:, chunk(c)], ident[:, 0])
                        last.then_inc(k_turned, 1)
                    if inv and s == 5:
                        pe.wait_ge(silu_done, at(3, 2))
                        pe.wait_ge(k_done, at(1, 2))
                        for c in range(G):
                            last = pe.transpose(TR[:, chunk(c)], vT[:, chunk(c)], ident[:, 0])
                        last.then_inc(v_turned, 1)
                    if ln and s == 9:
                        pe.wait_ge(on_done, at(4, 0))
                        if inv:
                            pe.wait_ge(v_done, at(1, 2))
                        for c in range(G):
                            last = pe.transpose(TR[:, chunk(c)], on[:, c], ident[:, 0])
                        last.then_inc(o_turned, 1)
                    if proj and s == L_AT:
                        pe.wait_ge(kb_done, at(1, 3))
                        if ln:
                            pe.wait_ge(oT_done, at(1, 0))
                        elif inv:
                            pe.wait_ge(v_done, at(1, 2))
                        for c in range(G):
                            last = pe.matmul(TR[:, chunk(c)], k_beta[:, chunk(c)], kq[:, cur, 0, chunk(c)],
                                             start=True, stop=True)
                        last.then_inc(l_done, 1)
                    if proj and s == BASE_AT:
                        pe.wait_ge(lx_done, at(1, 3))
                        pe.matmul(TR[:, 0:G * SB * SB], same[:], Lx[:].rearrange("p c t i -> p (c t i)"),
                                  start=True, stop=True).then_inc(spread_done, 1)

            turns(pe, turn)


def project(nc, bank, moe, x_rows, oT_d, Wo, out_rows):
    HQ = 4
    with ExitStack() as ctx:
        def sb(name, shape, dt=F32):
            return ctx.enter_context(nc.sbuf_tensor(name, shape, dt))

        def sem(name):
            return ctx.enter_context(nc.semaphore(name))

        wo_raw = sb("wo_raw", [P, H, HID])
        wo_hi = sb("wo_hi", [P, H, HID], F32R)
        wo_lo = sb("wo_lo", [P, H, HID], F32R)
        o_raw = sb("o_raw", [P, 2, H, P])
        o_hi = sb("o_hi", [P, 2, H, P], F32R)
        o_lo = sb("o_lo", [P, 2, H, P], F32R)
        x_t = sb("x_t", [P, 2, HID])
        y = sb("y", [P, 2, HID])
        wo_loaded = [sem(f"wo_loaded{k}") for k in range(H // HQ)]
        wo_hi_done = sem("wo_hi_done")
        wo_lo_done = sem("wo_lo_done")
        o_loaded = [sem(f"o_loaded{q}") for q in range(2)]
        x_loaded = [sem(f"xr_loaded{q}") for q in range(2)]
        o_hi_done = sem("o_hi_done")
        o_lo_done = sem("o_lo_done")
        tile_done = sem("tile_done")
        x_moe_done = sem("x_moe_done")
        y_done = sem("y_done")
        y_stored = [sem(f"y_stored{q}") for q in range(2)]
        oT = oT_d.rearrange("(b h) p t -> b p h t", b=B)
        PAIRS = NT // P // 2
        MOE_PAIRS = GT // P // 2
        block = ctx.enter_context(nc.Block())

        @block.sync
        def _(sp):
            def load_o(b, i, q):
                sp.dma_start(o_raw[:, q], oT[bass.ds(b, 1), :, :, bass.ds(i * (2 * P) + q * P, P)]
                             .rearrange("o p h t -> (o p) h t")).then_inc(o_loaded[q], 16)

            load_o(0, 0, 0)
            wo_rows = Wo.rearrange("(h p) n -> p h n", p=P)
            for k in range(H // HQ):
                sp.dma_start(wo_raw[:, k * HQ:(k + 1) * HQ], wo_rows[:, k * HQ:(k + 1) * HQ]).then_inc(wo_loaded[k], 16)

            def turn(b, i, begun=False):
                j = b * (PAIRS // B) + i
                for q in range(2):
                    if not (begun and q == 0):
                        wait(sp, o_lo_done, 2 * j + q - 1)
                        load_o(b, i, q)
                    wait(sp, y_done, 2 * j + q - 1)
                    sp.dma_start(x_t[:, q], x_rows[bass.ds(j * (2 * P) + q * P, P), :]).then_inc(x_loaded[q], 16)

            turn(0, 0, begun=True)
            with sp.Fori(1, PAIRS // B) as i:
                turn(0, i)
            with sp.Fori(0, PAIRS // B) as i:
                turn(1, i)

        @block.gpsimd
        def _(pool):
            def turn(j):
                for q in range(2):
                    wait(pool, y_done, 2 * j + q + 1)
                    pool.dma_start(out_rows[bass.ds(j * (2 * P) + q * P, P), :], y[:, q]).then_inc(y_stored[q], 16)

            loop(pool, PAIRS, turn)
            for q in range(2):
                wait(pool, y_stored[q], 16 * PAIRS)

        @block.scalar
        def _(act):
            wait(act, o_loaded[0], 16)
            act.activation(o_hi[:, 0], o_raw[:, 0], ACT.Copy).then_inc(o_hi_done, 1)
            for i in range(0, H, HQ):
                act.wait_ge(wo_loaded[i // HQ], 16)
                act.activation(wo_hi[:, i:i + HQ], wo_raw[:, i:i + HQ], ACT.Copy).then_inc(wo_hi_done, 1)

            def turn(j, skip=0):
                for q in range(skip, 2):
                    wait(act, o_loaded[q], 16 * j + 16)
                    wait(act, tile_done, 2 * j + q - 1)
                    act.activation(o_hi[:, q], o_raw[:, q], ACT.Copy).then_inc(o_hi_done, 1)

            turn(0, skip=1)
            with act.Fori(1, PAIRS) as j:
                turn(j)

        @block.vector
        def _(dve):
            def cut(j, q):
                wait(dve, o_hi_done, 2 * j + q + 1)
                wait(dve, tile_done, 2 * j + q - 1)
                dve.tensor_tensor(o_lo[:, q], o_raw[:, q], o_hi[:, q].bitcast(F32), ALU.subtract)\
                   .then_inc(o_lo_done, 1)

            def finish(j, q):
                wait(dve, x_loaded[q], 16 * j + 16)
                if isinstance(j, int) and j < MOE_PAIRS:
                    dve.tensor_tensor(x_t[:, q], x_t[:, q], moe[:, 2 * j + q], ALU.add).then_inc(x_moe_done, 1)
                    wait(dve, x_moe_done, 2 * j + q + 1)
                wait(dve, tile_done, 2 * j + q + 1)
                wait(dve, y_stored[q], 16 * j)
                dve.tensor_tensor(y[:, q], bank[q][:], x_t[:, q], ALU.add).then_inc(y_done, 1)

            def turn(j, last=False):
                cut(j, 1)
                finish(j, 0)
                if not last:
                    cut(j + 1, 0)
                finish(j, 1)

            cut(0, 0)
            for i in range(0, H, HQ):
                wait(dve, wo_hi_done, i // HQ + 1)
                dve.tensor_tensor(wo_lo[:, i:i + HQ], wo_raw[:, i:i + HQ], wo_hi[:, i:i + HQ].bitcast(F32),
                                  ALU.subtract).then_inc(wo_lo_done, 1)
            for j in range(MOE_PAIRS):
                turn(j)
            with dve.Fori(MOE_PAIRS, PAIRS - 1) as j:
                turn(j)
            turn(PAIRS - 1, last=True)

        @block.tensor
        def _(pe):
            def turn(j):
                for q in range(2):
                    wait(pe, o_hi_done, 2 * j + q + 1)
                    wait(pe, o_lo_done, 2 * j + q + 1)
                    wait(pe, y_done, 2 * j + q - 1)
                    for i in range(H):
                        if isinstance(j, int) and j == 0 and q == 0 and i % HQ == 0:
                            pe.wait_ge(wo_lo_done, i // HQ + 1)
                        pe.matmul(bank[q][:], o_hi[:, q, i], wo_hi[:, i], start=(i == 0), stop=False)
                        pe.matmul(bank[q][:], o_hi[:, q, i], wo_lo[:, i], start=False, stop=False)
                        last = pe.matmul(bank[q][:], o_lo[:, q, i], wo_hi[:, i], start=False, stop=(i == H - 1))
                    last.then_inc(tile_done, 1)

            loop(pe, PAIRS, turn)


def kernel(**inputs):
    import numpy as np
    import concourse.bacc as bacc
    from concourse import mybir as _mybir
    from concourse.bass_utils import run_bass_kernel_spmd

    a = {n.removeprefix("L0_"): np.asarray(v) for n, v in inputs.items()}
    heads_last = lambda v: v.reshape(H, D, -1)
    laid = {
        "x": a["attn_x"], "Wq": a["attn_Wq"], "Wk": a["attn_Wk"], "Wv": a["attn_Wv"],
        "Wab": np.concatenate([a["attn_Wa"], a["attn_Wb"]], axis=1),
        "bab": np.concatenate([a["attn_ba"], a["attn_bb"]])[:, None],
        "Wg": a["attn_Wg"], "Wo": a["attn_Wo"],
        "taps": np.concatenate([np.concatenate([heads_last(a[f"attn_{n}cw"]), heads_last(a[f"attn_{n}cb"])], axis=2)
                                for n in "kqv"], axis=2),
        "ln_w": a["attn_ln_w"][:, None], "ln_b": a["attn_ln_b"][:, None],
        "topk_idx": a["ffn_topk_idx"].reshape(-1, TOPK), "topk_weight": a["ffn_topk_weight"].reshape(-1, TOPK),
        "gate_up": np.concatenate([a["ffn_gate_weight"].transpose(0, 2, 1), a["ffn_up_weight"].transpose(0, 2, 1)], axis=2),
        "down": a["ffn_down_weight"].transpose(0, 2, 1),
    }
    nc = bacc.Bacc("TRN2", target_bir_lowering=False, num_devices=1)
    arrays, args = {}, {}
    for name, v in laid.items():
        v = np.ascontiguousarray(v)
        arrays[f"in_{name}"] = v
        args[name] = nc.dram_tensor(f"in_{name}", v.shape, _mybir.dt.from_np(v.dtype), kind="ExternalInput").ap()
    args["out"] = nc.dram_tensor("out_0", laid["x"].shape, F32, kind="ExternalOutput").ap()
    program(nc, **args)
    r = run_bass_kernel_spmd(nc, [arrays], core_ids=[0])
    return r.results[0]["out_0"]
```
